# Optimizing a Trainium2 kernel written in Bass

```python
import numpy as np
import jax
import jax.numpy as jnp

def _softmax(x, axis=-1):
    return jax.nn.softmax(x, axis=axis)

def _gelu(x):
    return jax.nn.gelu(x, approximate=True)

def _silu(x):
    return jax.nn.silu(x)

def _sigmoid(x):
    return jax.nn.sigmoid(x)

def _layernorm(x, axis=-1, eps=1e-05):
    m = jnp.mean(x, axis=axis, keepdims=True)
    v = jnp.var(x, axis=axis, keepdims=True)
    return (x - m) / jnp.sqrt(v + eps)

def _scatter_add(tgt, idx, src, axis=0):
    return tgt.at[idx].add(src)

def _segment_sum(src, seg, n):
    return jax.ops.segment_sum(src, seg, n)
kernel_name = 'mk_vit_tower_d2_tok_img256_r4_9a2f83'

def setup_inputs(seed: int=0):
    np.random.seed(seed)
    _w = jnp.asarray

    def _rec_inputs():
        import jax
        import jax.numpy as jnp
        _rk = jax.random.key(seed)
        x = -7.10856e-05 + 0.999911 * jax.random.normal(jax.random.fold_in(_rk, 1), (4, 64, 128, 64), jnp.float32)
        return x
    x = _rec_inputs()

    def _L0_tok_setup():
        import jax, jax.numpy as jnp
        import numpy as np
        PATCH_LEN = 16
        STRIDE = 8
        PAD = 8
        key = jax.random.key(seed)
        k1, k2 = jax.random.split(key)
        x = jax.random.normal(k1, (32, 64, 128, 64), dtype=jnp.float32)
        in_feat = 64 * (PATCH_LEN // 2 + 1) * 2
        W = jax.random.normal(k2, (64, in_feat), dtype=jnp.float32) * 0.02
        return {'x': x, 'W': W}
    _L0_tok_all = _L0_tok_setup()
    _L0_tok_in = {k: v for k, v in _L0_tok_all.items() if k in ('W',)}
    del _L0_tok_all

    def _L0_attn_setup():
        import jax, jax.numpy as jnp
        import numpy as np
        import math
        B, T, D_MODEL = (1, 512, 64)
        N_Q, N_KV = (16, 1)
        D_HEAD = D_MODEL // N_KV
        QPG = N_Q // N_KV
        ROPE_BASE = 10000.0
        WINDOW = 128
        EPS = 1.1920929e-07
        NEG = -1e+30

        def _rope(x, base=ROPE_BASE):
            t, d = (x.shape[-2], x.shape[-1])
            freqs = base ** (-2.0 * jnp.arange(d // 2, dtype=jnp.float32) / d)
            theta = jnp.arange(t, dtype=jnp.float32)[:, None] * freqs[None, :]
            cos, sin = (jnp.cos(theta), jnp.sin(theta))
            x1, x2 = (x[..., 0::2], x[..., 1::2])
            r1 = x1 * cos - x2 * sin
            r2 = x1 * sin + x2 * cos
            return jnp.stack([r1, r2], axis=-1).reshape(x.shape)

        def _rmsnorm(x, w):
            return x * jax.lax.rsqrt(jnp.mean(x * x, axis=-1, keepdims=True) + EPS) * w
        key = jax.random.key(seed)
        k0, k1, k2, k3 = jax.random.split(key, 4)
        x = jax.random.normal(k0, (B, T, D_MODEL), dtype=jnp.float32)
        wq = jax.random.normal(k1, (QPG * N_KV * D_HEAD, D_MODEL), dtype=jnp.float32) * 0.02
        wkv = jax.random.normal(k2, (2 * D_HEAD * N_KV, D_MODEL), dtype=jnp.float32) * 0.02
        wo = jax.random.normal(k3, (D_MODEL, D_HEAD * N_Q * N_KV), dtype=jnp.float32) * 0.02
        q_norm_w = jnp.ones((D_HEAD,), dtype=jnp.float32)
        k_norm_w = jnp.ones((D_HEAD,), dtype=jnp.float32)
        return {'x': x, 'wq': wq, 'wkv': wkv, 'wo': wo, 'q_norm_w': q_norm_w, 'k_norm_w': k_norm_w}
    _L0_attn_all = _L0_attn_setup()
    _L0_attn_in = {k: v for k, v in _L0_attn_all.items() if k in ('wq', 'wkv', 'wo', 'q_norm_w', 'k_norm_w')}
    del _L0_attn_all

    def _L0_ffn_setup():
        import jax, jax.numpy as jnp
        import numpy as np
        NUM_EXPERTS = 8
        TOP_K = 2
        B, S, D = (8, 2048, 64)

        def _moe(tokens, router_w, w1, b1, w2, b2):
            N = tokens.shape[0]
            E = router_w.shape[0]
            logits = tokens.astype(jnp.float32) @ router_w.astype(jnp.float32).T
            probs = jax.nn.softmax(logits, axis=-1)
            rw, re = jax.lax.top_k(probs, TOP_K)
            if TOP_K > 1:
                rw = rw / jnp.maximum(rw.sum(-1, keepdims=True), 1e-12)
            rw = rw.astype(tokens.dtype)
            combine = jnp.zeros((N, E), tokens.dtype).at[jnp.arange(N)[:, None], re].set(rw)
            out = tokens
            for e in range(E):
                h = jax.nn.gelu(tokens @ w1[e] + b1[e], approximate=False)
                y = h @ w2[e] + b2[e]
                out = out + combine[:, e:e + 1] * y
            return out
        key = jax.random.key(seed)
        ks = jax.random.split(key, 4)
        scale = 1.0 / np.sqrt(D).astype(np.float32)
        return {'input_embeddings': jax.random.normal(ks[0], (B, S, D), jnp.float32), 'router_w': jax.random.normal(ks[1], (NUM_EXPERTS, D), jnp.float32) * scale, 'w1': jax.random.normal(ks[2], (NUM_EXPERTS, D, D), jnp.float32) * scale, 'b1': jnp.zeros((NUM_EXPERTS, D), jnp.float32), 'w2': jax.random.normal(ks[3], (NUM_EXPERTS, D, D), jnp.float32) * scale, 'b2': jnp.zeros((NUM_EXPERTS, D), jnp.float32)}
    _L0_ffn_all = _L0_ffn_setup()
    _L0_ffn_in = {k: v for k, v in _L0_ffn_all.items() if k in ('router_w', 'w1', 'b1', 'w2', 'b2')}
    del _L0_ffn_all

    def _L1_attn_setup():
        import jax, jax.numpy as jnp
        import numpy as np
        BN_EPS = 1e-05
        key = jax.random.key(seed)
        ks = jax.random.split(key, 12)
        B, N, d_e, d_a = (16, 512, 64, 64)
        s_e = 1.0 / np.sqrt(d_e)
        return {'x': jax.random.normal(ks[0], (B, N, d_e), dtype=jnp.float32), 'Wq': jax.random.uniform(ks[1], (d_e, d_a), jnp.float32, -s_e, s_e), 'bq': jax.random.uniform(ks[2], (d_a,), jnp.float32, -s_e, s_e), 'Wk': jax.random.uniform(ks[3], (d_e, d_a), jnp.float32, -s_e, s_e), 'bk': jax.random.uniform(ks[4], (d_a,), jnp.float32, -s_e, s_e), 'Wv': jax.random.uniform(ks[5], (d_e, d_e), jnp.float32, -s_e, s_e), 'bv': jax.random.uniform(ks[6], (d_e,), jnp.float32, -s_e, s_e), 'Wl': jax.random.uniform(ks[7], (d_e, d_e), jnp.float32, -s_e, s_e), 'bl': jax.random.uniform(ks[8], (d_e,), jnp.float32, -s_e, s_e), 'gamma': jnp.ones((d_e,), jnp.float32), 'beta': jnp.zeros((d_e,), jnp.float32)}
    _L1_attn_all = _L1_attn_setup()
    _L1_attn_in = {k: v for k, v in _L1_attn_all.items() if k in ('Wq', 'bq', 'Wk', 'bk', 'Wv', 'bv', 'Wl', 'bl', 'gamma', 'beta')}
    del _L1_attn_all

    def _L1_ffn_setup():
        import math
        import jax, jax.numpy as jnp
        import numpy as np
        CAPACITY_FACTOR = 1.25
        key = jax.random.key(seed)
        ks = jax.random.split(key, 5)
        B, L, D, F, E = (8, 2048, 64, 256, 8)
        h = jax.random.normal(ks[0], (B, L, D), dtype=jnp.float32)
        gate_w = jax.random.normal(ks[1], (D, E), dtype=jnp.float32) * 0.02
        gate_b = jnp.zeros((E,), dtype=jnp.float32)
        w1 = jax.random.normal(ks[2], (E, D, F), dtype=jnp.float32) * (1.0 / math.sqrt(D))
        b1 = jnp.zeros((E, F), dtype=jnp.float32)
        w2 = jax.random.normal(ks[3], (E, F, D), dtype=jnp.float32) * (1.0 / math.sqrt(F))
        b2 = jnp.zeros((E, D), dtype=jnp.float32)
        return {'h': h, 'gate_w': gate_w, 'gate_b': gate_b, 'w1': w1, 'b1': b1, 'w2': w2, 'b2': b2}
    _L1_ffn_all = _L1_ffn_setup()
    _L1_ffn_in = {k: v for k, v in _L1_ffn_all.items() if k in ('gate_w', 'gate_b', 'w1', 'b1', 'w2', 'b2')}
    del _L1_ffn_all
    return {'x': x, 'L0_tok_W': _L0_tok_in['W'], 'L0_attn_wq': _L0_attn_in['wq'], 'L0_attn_wkv': _L0_attn_in['wkv'], 'L0_attn_wo': _L0_attn_in['wo'], 'L0_attn_q_norm_w': _L0_attn_in['q_norm_w'], 'L0_attn_k_norm_w': _L0_attn_in['k_norm_w'], 'L0_ffn_router_w': _L0_ffn_in['router_w'], 'L0_ffn_w1': _L0_ffn_in['w1'], 'L0_ffn_b1': _L0_ffn_in['b1'], 'L0_ffn_w2': _L0_ffn_in['w2'], 'L0_ffn_b2': _L0_ffn_in['b2'], 'L1_attn_Wq': _L1_attn_in['Wq'], 'L1_attn_bq': _L1_attn_in['bq'], 'L1_attn_Wk': _L1_attn_in['Wk'], 'L1_attn_bk': _L1_attn_in['bk'], 'L1_attn_Wv': _L1_attn_in['Wv'], 'L1_attn_bv': _L1_attn_in['bv'], 'L1_attn_Wl': _L1_attn_in['Wl'], 'L1_attn_bl': _L1_attn_in['bl'], 'L1_attn_gamma': _L1_attn_in['gamma'], 'L1_attn_beta': _L1_attn_in['beta'], 'L1_ffn_gate_w': _L1_ffn_in['gate_w'], 'L1_ffn_gate_b': _L1_ffn_in['gate_b'], 'L1_ffn_w1': _L1_ffn_in['w1'], 'L1_ffn_b1': _L1_ffn_in['b1'], 'L1_ffn_w2': _L1_ffn_in['w2'], 'L1_ffn_b2': _L1_ffn_in['b2']}

def reference(x, L0_tok_W, L0_attn_wq, L0_attn_wkv, L0_attn_wo, L0_attn_q_norm_w, L0_attn_k_norm_w, L0_ffn_router_w, L0_ffn_w1, L0_ffn_b1, L0_ffn_w2, L0_ffn_b2, L1_attn_Wq, L1_attn_bq, L1_attn_Wk, L1_attn_bk, L1_attn_Wv, L1_attn_bv, L1_attn_Wl, L1_attn_bl, L1_attn_gamma, L1_attn_beta, L1_ffn_gate_w, L1_ffn_gate_b, L1_ffn_w1, L1_ffn_b1, L1_ffn_w2, L1_ffn_b2):
    import jax
    import jax.numpy as jnp

    def _L0_tok_ref(x, W):
        import jax, jax.numpy as jnp
        import numpy as np
        PATCH_LEN = 16
        STRIDE = 8
        PAD = 8
        B, C, T, V = x.shape
        xp = jnp.pad(x, ((0, 0), (0, 0), (0, PAD), (0, 0)), mode='edge')
        Tp = T + PAD
        N = (Tp - PATCH_LEN) // STRIDE + 1
        idx = jnp.arange(N)[:, None] * STRIDE + jnp.arange(PATCH_LEN)[None, :]
        patches = xp[:, :, idx, :]
        patches = jnp.transpose(patches, (0, 4, 2, 3, 1))
        xf = jnp.fft.rfft(patches, axis=-2, norm='ortho')
        F = xf.shape[-2]
        x_real = xf.real.reshape(B, V, N, F * C)
        x_imag = xf.imag.reshape(B, V, N, F * C)
        x_emb = jnp.concatenate([x_real, x_imag], axis=-1)
        x_emb = x_emb @ W.T
        return x_emb.reshape(B, V * N, -1)

    def _L0_attn_ref(x, wq, wkv, wo, q_norm_w, k_norm_w):
        import jax, jax.numpy as jnp
        import numpy as np
        import math
        B, T, D_MODEL = (1, 512, 64)
        N_Q, N_KV = (16, 1)
        D_HEAD = D_MODEL // N_KV
        QPG = N_Q // N_KV
        ROPE_BASE = 10000.0
        WINDOW = 128
        EPS = 1.1920929e-07
        NEG = -1e+30

        def _rope(x, base=ROPE_BASE):
            t, d = (x.shape[-2], x.shape[-1])
            freqs = base ** (-2.0 * jnp.arange(d // 2, dtype=jnp.float32) / d)
            theta = jnp.arange(t, dtype=jnp.float32)[:, None] * freqs[None, :]
            cos, sin = (jnp.cos(theta), jnp.sin(theta))
            x1, x2 = (x[..., 0::2], x[..., 1::2])
            r1 = x1 * cos - x2 * sin
            r2 = x1 * sin + x2 * cos
            return jnp.stack([r1, r2], axis=-1).reshape(x.shape)

        def _rmsnorm(x, w):
            return x * jax.lax.rsqrt(jnp.mean(x * x, axis=-1, keepdims=True) + EPS) * w
        Bx, Tx, C = x.shape
        q = x @ wq.T
        kv = x @ wkv.T
        k, v = (kv[..., :N_KV * D_HEAD], kv[..., N_KV * D_HEAD:])
        q = q.reshape(Bx, Tx, QPG, N_KV, D_HEAD).transpose(0, 2, 3, 1, 4)
        k = k.reshape(Bx, Tx, 1, N_KV, D_HEAD).transpose(0, 2, 3, 1, 4)
        v = v.reshape(Bx, Tx, 1, N_KV, D_HEAD).transpose(0, 2, 3, 1, 4)
        q = _rmsnorm(_rope(q), q_norm_w)
        k = _rmsnorm(_rope(k), k_norm_w)
        rows = jnp.arange(Tx)[:, None]
        cols = jnp.arange(Tx)[None, :]
        mask = (cols <= rows) & (rows - cols <= WINDOW)
        scale = 1.0 / math.sqrt(D_HEAD)
        scores = jnp.einsum('bqgtd,bqgsd->bqgts', q, k) * scale
        scores = jnp.where(mask[None, None, None], scores, NEG)
        attn = jax.nn.softmax(scores, axis=-1)
        out = jnp.einsum('bqgts,bqgsd->bqgtd', attn, v)
        out = out.transpose(0, 3, 1, 2, 4).reshape(Bx, Tx, QPG * N_KV * D_HEAD)
        return out @ wo.T

    def _L0_ffn_ref(input_embeddings, router_w, w1, b1, w2, b2):
        import jax, jax.numpy as jnp
        import numpy as np
        NUM_EXPERTS = 8
        TOP_K = 2
        B, S, D = (8, 2048, 64)

        def _moe(tokens, router_w, w1, b1, w2, b2):
            N = tokens.shape[0]
            E = router_w.shape[0]
            logits = tokens.astype(jnp.float32) @ router_w.astype(jnp.float32).T
            probs = jax.nn.softmax(logits, axis=-1)
            rw, re = jax.lax.top_k(probs, TOP_K)
            if TOP_K > 1:
                rw = rw / jnp.maximum(rw.sum(-1, keepdims=True), 1e-12)
            rw = rw.astype(tokens.dtype)
            combine = jnp.zeros((N, E), tokens.dtype).at[jnp.arange(N)[:, None], re].set(rw)
            out = tokens
            for e in range(E):
                h = jax.nn.gelu(tokens @ w1[e] + b1[e], approximate=False)
                y = h @ w2[e] + b2[e]
                out = out + combine[:, e:e + 1] * y
            return out
        b, s, d = input_embeddings.shape
        tokens = input_embeddings.reshape(b * s, d)
        return _moe(tokens, router_w, w1, b1, w2, b2).reshape(b, s, d)

    def _L1_attn_ref(x, Wq, bq, Wk, bk, Wv, bv, Wl, bl, gamma, beta):
        import jax, jax.numpy as jnp
        import numpy as np
        BN_EPS = 1e-05
        q = x @ Wq + bq
        k = x @ Wk + bk
        v = x @ Wv + bv
        d_a = q.shape[-1]
        score = jnp.einsum('bnd,bmd->bnm', q, k) / jnp.asarray(d_a, q.dtype)
        score = jax.nn.softmax(score, axis=2)
        attn = jnp.einsum('bnm,bmd->bnd', score, v)
        h = attn @ Wl + bl
        mean = jnp.mean(h, axis=(0, 1))
        var = jnp.mean((h - mean) ** 2, axis=(0, 1))
        y = jax.nn.relu((h - mean) * jax.lax.rsqrt(var + BN_EPS) * gamma + beta)
        return y + x

    def _L1_ffn_ref(h, gate_w, gate_b, w1, b1, w2, b2):
        import math
        import jax, jax.numpy as jnp
        import numpy as np
        CAPACITY_FACTOR = 1.25
        B, L, D = h.shape
        E = gate_w.shape[1]
        T = B * L
        C = max(1, math.ceil(CAPACITY_FACTOR * T / E))
        x = h.reshape(T, D)
        logits = x @ gate_w + gate_b
        probs = jax.nn.softmax(logits, axis=-1)
        idx = jnp.argmax(probs, axis=-1)
        prb = jnp.take_along_axis(probs, idx[:, None], axis=1)[:, 0]
        one_hot = jax.nn.one_hot(idx, E, dtype=jnp.float32)
        pos = (jnp.cumsum(one_hot, axis=0) * one_hot).sum(-1).astype(jnp.int32) - 1
        kept = pos < C
        pos_safe = jnp.where(kept, pos, C)
        buf = jnp.zeros((E, C, D), dtype=h.dtype).at[idx, pos_safe].set(x, mode='drop')
        hmid = jax.nn.relu(jnp.einsum('ecd,edf->ecf', buf, w1) + b1[:, None, :])
        ybuf = jnp.einsum('ecf,efd->ecd', hmid, w2) + b2[:, None, :]
        pos_g = jnp.minimum(pos, C - 1)
        y_tok = ybuf[idx, pos_g] * (prb * kept)[:, None]
        y = y_tok.reshape(B, L, D)
        y = jnp.nan_to_num(y, nan=0.0, posinf=10000.0, neginf=-10000.0)
        return y
    h = _L0_tok_ref(x, L0_tok_W)
    h = h + _L0_attn_ref(_layernorm(h, axis=-1), L0_attn_wq, L0_attn_wkv, L0_attn_wo, L0_attn_q_norm_w, L0_attn_k_norm_w)
    h = h + _L0_ffn_ref(_layernorm(h, axis=-1), L0_ffn_router_w, L0_ffn_w1, L0_ffn_b1, L0_ffn_w2, L0_ffn_b2)
    h = h + _L1_attn_ref(_layernorm(h, axis=-1), L1_attn_Wq, L1_attn_bq, L1_attn_Wk, L1_attn_bk, L1_attn_Wv, L1_attn_bv, L1_attn_Wl, L1_attn_bl, L1_attn_gamma, L1_attn_beta)
    h = h + _L1_ffn_ref(_layernorm(h, axis=-1), L1_ffn_gate_w, L1_ffn_gate_b, L1_ffn_w1, L1_ffn_b1, L1_ffn_w2, L1_ffn_b2)
    return h

_drawn_inputs = setup_inputs


def setup_inputs(seed=0):
    import zlib

    import numpy as np

    out = dict(_drawn_inputs(seed))
    spreads = {'L0_attn_q_norm_w': (1.0, 0.6),
     'L0_attn_k_norm_w': (1.0, 0.6),
     'L0_ffn_b1': (0.0, 0.1),
     'L0_ffn_b2': (0.0, 0.1),
     'L1_attn_gamma': (1.0, 0.2),
     'L1_attn_beta': (0.0, 0.1),
     'L1_ffn_gate_b': (0.0, 0.1),
     'L1_ffn_b1': (0.0, 0.8),
     'L1_ffn_b2': (0.0, 0.8)}
    factors = {'L1_attn_bq': 34.736, 'L1_attn_bk': 64.0, 'L1_attn_bv': 64.0, 'L1_attn_bl': 64.0}
    for name, (base, spread) in spreads.items():
        noise = np.random.default_rng([zlib.crc32(name.encode()), seed]).standard_normal(out[name].shape)
        drawn = base * np.exp(spread * noise) if base else spread * noise
        out[name] = jnp.asarray(drawn.astype(out[name].dtype))
    for name, factor in factors.items():
        out[name] = (out[name] * factor).astype(out[name].dtype)
    return out
```

```python
from contextlib import ExitStack

import numpy as np

import concourse.bass as bass
from concourse import mybir

F32 = mybir.dt.float32
BF16 = mybir.dt.bfloat16
I32 = mybir.dt.int32
ALU = mybir.AluOpType
ACT = mybir.ActivationFunctionType
X = mybir.AxisListType.X

P = 128
IMAGES, CH, T, V = 4, 64, 128, 64
D = 64
PATCH, STRIDE = 16, 8
NPATCH = T // STRIDE
SEQ = V * NPATCH
TILES = SEQ // P
ALLT = IMAGES * TILES
FREQ = PATCH // 2 + 1
HEADS = 16
PAIRS = HEADS // 2
WINDOW = 128
CHUNK = 32
CHUNKS = SEQ // CHUNK
SPAN = WINDOW + CHUNK
EARLY = WINDOW // CHUNK
NQ = 4
E = 8
F1 = 256
FCH = E * F1 // P
GROUP_TILES = 4
GROUPS = ALLT // GROUP_TILES
GT = GROUP_TILES * P
CAPACITY = -(-5 * IMAGES * SEQ // (4 * E))
LN_EPS = 1e-5
BN_EPS = 1e-5
RMS_EPS = 1.1920929e-07
HUGE = 3.4028235e38
HALF = 512


class Chain:

    def __init__(self, engine, sem):
        self.engine, self.sem, self.n = engine, sem, 0

    def step(self, ins):
        self.n += 1
        ins.then_inc(self.sem, 1)
        self.engine.wait_ge(self.sem, self.n)


def program(nc, inp, out):
    with ExitStack() as ctx:
        def sb(name, shape, dt=F32):
            return ctx.enter_context(nc.sbuf_tensor(name, shape, dt))

        def sem(name):
            return ctx.enter_context(nc.semaphore(name))

        bank = [ctx.enter_context(nc.psum_tensor(f"bank{i}", [P, HALF], F32)) for i in range(8)]

        shapes = {k: (list(v.shape), v.dtype) for k, v in inp.items()}
        loaded = ["ident", "dft", "rope_cos", "rope_sin", "row_of_t", "window_mask", "lower", "copies", "first_weight",
                  "tok_w", "by_head", "wq", "wk", "wv0", "wo0", "router", "moe_w1", "moe_b1", "moe_w2",
                  "wq1", "wk1", "wvT1", "wl1", "gate", "ffn_b1"]
        big1 = sb("big1", [P, PAIRS, SEQ])
        big2 = sb("big2", [P, PAIRS, SEQ])
        aside = ("tok_w", "row_of_t", "window_mask")
        sbuf = {k: sb("s_" + k, *shapes[k]) for k in loaded if k not in aside}
        sbuf["tok_w"] = big1[0:2 * FREQ, 0:D * CH // SEQ, :].rearrange("p a n -> p (a n)").rearrange(
            "p (o c) -> p o c", c=CH)
        sbuf["row_of_t"] = big2[0:CHUNK, 0, 0:P]
        sbuf["window_mask"] = big2[0:CHUNK, 1, 0:(EARLY + 1) * SPAN].rearrange("p (v k) -> p v k", k=SPAN)
        row_of_t = sb("row_of_t", [CHUNK, P], BF16)
        window_mask = sb("window_mask", [CHUNK, EARLY + 1, SPAN], BF16)
        ident, lower = sbuf["ident"], sbuf["lower"]
        qn, kn, wqk = sb("qn", [P, 1]), sb("kn", [P, 1]), sb("wqk", [P, 1])
        bq, bk = sb("bq", [P, 1]), sb("bk", [P, 1])
        bvcol, bvrep = sb("bvcol", [D, 1]), sb("bvrep", [D, P])
        blrow, gammarow, betarow = sb("blrow", [P, D]), sb("gammarow", [P, D]), sb("betarow", [P, D])
        vbias = sb("vbias", [P, D])
        gate_b = sb("gate_b", [P, E])
        b2sel0 = sb("b2sel0", [TILES * E, TILES, D])
        b2sel1 = sb("b2sel1", [GROUP_TILES * E, GROUP_TILES, D])
        ones, ones_mean, zeros = sb("ones", [P, P]), sb("ones_mean", [P, P]), sb("zeros", [P, P])
        ten_k = sb("ten_k", [P, 2, GROUP_TILES * D])
        wvl = sb("wvl", [D, D])
        newton = sb("newton", [P, 3, P])
        weff = sb("weff", [P, STRIDE, D])

        xb = sb("xb", [P, V, T])
        xflat = xb[:].rearrange("p v t -> p (v t)")
        sbuf["ffn_w1"] = xflat[:, 0:E * P].rearrange("p (e f) -> p e f", f=P)
        sbuf["ffn_w2"] = xflat[:, E * P:E * P + FCH * D].rearrange("p (f d) -> p f d", d=D)
        h = sb("h", [P, TILES, D])
        xn = sb("xn", [P, TILES, 2, D])
        tmp = sb("tmp", [P, TILES, D])
        st = sb("st", [P, 8, TILES])
        xT = sb("xT", [P, WINDOW + SEQ])
        qT = big1[:].rearrange("p a n -> p (a n)").rearrange("p (c a t) -> p c a t", a=PAIRS, t=CHUNK)
        sq = big2[:].rearrange("p a n -> p (a n)").rearrange("p (c a t) -> p c a t", a=PAIRS, t=CHUNK)
        oT = big2
        work = sb("work", [P, 4 * HALF])
        prod = work[:].rearrange("p (a c n) -> p a c n", a=2, c=2)
        probs = work[:, 0:3 * NQ * SPAN].rearrange("p (a q k) -> p a q k", a=3, q=NQ)
        rq = sb("rq", [P, CHUNKS, 2, 2])
        rqflat = rq[:].rearrange("p c a e -> p (c a e)")
        kT = sb("kT", [P, WINDOW + SEQ])
        rk = sb("rk", [P, TILES])
        vwin = sb("vwin", [P, CHUNKS + 1, D])
        vrem = sb("vrem", [P, CHUNKS, D])
        turned = sb("turned", [P, 2 * HALF])
        pT = turned[:].rearrange("p (a q r) -> p a q r", a=2, q=NQ)
        yw = turned[:].rearrange("p (a e d) -> p a e d", a=2, e=E)
        diag = turned[:]
        pTr = sb("pTr", [P, 2, P])
        own = sb("own", [P, 2, P])
        small = sb("small", [P, 4, 4, NQ])
        lg = sb("lg", [P, 8, TILES, E])
        comb = sb("comb", [P, TILES, E])
        combT = sb("combT", [TILES * E, P])
        moe = sb("moe", [P, TILES, D])
        hT = big2[:].rearrange("p a b -> p (a b)")

        res = sb("res", [P, ALLT, D])
        hl = sb("hl", [P, ALLT, D])
        base = sb("base", [P, E])
        mean_row, var_row = sb("mean_row", [P, D]), sb("var_row", [P, D])
        yout = kT[:, 0:3 * GROUP_TILES * D].rearrange("p (k i d) -> p k i d", k=3, d=D)
        maski = kT[:, 3 * GROUP_TILES * D:4 * GROUP_TILES * D].bitcast(I32)

        first_sem = sem("const_loaded")
        sems = {n: sem(n) for n in [
            "set_ready", "x_loaded", "tok_done", "h_ready", "dve_chain", "cos_done", "q_root", "k_root", "xn_ready", "xT_psum",
            "xT_act", "xT_dve", "proj_done", "square_done", "prod_done", "rot_done", "ssq_done", "v_psum", "v_act",
            "v_dve", "kprod", "scores_done", "bias_ready", "exp_done", "scaled", "transposed",
            "pT_ready", "pTr_ready", "pv_done", "oT_ready", "wo_done", "last"]}
        S = sems
        clear = range(first_sem.num, S["last"].num + 1)

        def stage(build):
            with nc.Block() as block:
                build(block)
            nc.all_engine_barrier(sems_to_clear=clear)

        def bc(ap, n):
            return ap.unsqueeze(2).to_broadcast([ap.shape[0], ap.shape[1], n])

        def rows(ap, n):
            return ap.unsqueeze(1).to_broadcast([ap.shape[0], n, ap.shape[1]])

        def layernorm(v, ch, src, dst, diff, work, stat, tiles):
            ch.step(v.tensor_reduce(stat[:, 0, :tiles], src, X, ALU.add))
            ch.step(v.tensor_scalar(stat[:, 1, :tiles], stat[:, 0, :tiles], 1.0 / D, None, ALU.mult))
            ch.step(v.tensor_tensor(diff, src, bc(stat[:, 1, :tiles], D), ALU.subtract))
            ch.step(v.tensor_tensor(work, diff, diff, ALU.mult))
            ch.step(v.tensor_reduce(stat[:, 2, :tiles], work, X, ALU.add))
            ch.step(v.tensor_scalar(stat[:, 3, :tiles], stat[:, 2, :tiles], 1.0 / D, LN_EPS, ALU.mult, ALU.add))
            one_over_root(v, ch, stat[:, 4, :tiles], stat[:, 3, :tiles])
            ch.step(v.tensor_tensor(dst, diff.unsqueeze(2).to_broadcast([P, tiles, 2, D]),
                                    stat[:, 4, :tiles].unsqueeze(2).unsqueeze(3).to_broadcast([P, tiles, 2, D]),
                                    ALU.mult))

        def one_over_root(v, ch, dst, x):
            n = x.shape[1]
            half, y, t = (newton[:, k, 0:n] for k in range(3))
            ch.step(v.tensor_scalar(half.bitcast(I32), x.bitcast(I32), 1, None, ALU.logical_shift_right))
            ch.step(v.tensor_scalar(y.bitcast(I32), half.bitcast(I32), -1.0, float(0x5F3759DF), ALU.mult, ALU.add))
            for k in range(3):
                ch.step(v.tensor_tensor(t, y, y, ALU.mult))
                ch.step(v.scalar_tensor_tensor(out=t, in0=t, scalar=-0.5, in1=x, op0=ALU.mult, op1=ALU.mult))
                ch.step(v.scalar_tensor_tensor(out=dst if k == 2 else y, in0=t, scalar=1.5, in1=y, op0=ALU.add,
                                               op1=ALU.mult))

        def transpose_tiles(pe, src, tiles, banks):
            for i in range(tiles):
                twice = src[:, i].rearrange("p a d -> p (a d)")
                ins = nc.tensor.transpose(bank[banks[i // 4]][:, (i % 4) * P:(i % 4 + 1) * P], twice, ident[:])
                if i % 4 == 3:
                    ins.then_inc(S["xT_psum"], 1)

        def setup(block):
            @block.sync
            def _(sp):
                n = 0
                for k in loaded:
                    sp.dma_start(sbuf[k] if k in aside else sbuf[k][:], inp[k]).then_inc(first_sem, 16)
                    n += 1
                for half in range(2):
                    r = slice(D * half, D * half + D)
                    for dst, src in ((qn, "q_norm"), (kn, "k_norm"), (bq, "bq1"), (bk, "bk1")):
                        sp.dma_start(dst[r, :], inp[src]).then_inc(first_sem, 16)
                        n += 1
                sp.dma_start(bvcol[:], inp["bv1"]).then_inc(first_sem, 16)
                n += 1
                for dst, src in ((blrow, "bl1"), (gammarow, "gamma"), (betarow, "beta"), (gate_b, "gate_b")):
                    sp.dma_start(dst[:], inp[src].to_broadcast([P, inp[src].shape[1]])).then_inc(first_sem, 16)
                    n += 1
                sp.wait_ge(S["set_ready"], 1)
                for i in range(TILES):
                    sp.dma_start(b2sel0[E * i:E * i + E, i, :], inp["moe_b2"]).then_inc(first_sem, 16)
                    n += 1
                for i in range(GROUP_TILES):
                    sp.dma_start(b2sel1[E * i:E * i + E, i, :], inp["ffn_b2"]).then_inc(first_sem, 16)
                    n += 1
                load_x(sp, 0, first_sem)
                n += 1
                sp.wait_ge(first_sem, 16 * n)
                sp.sem_inc(S["x_loaded"], 1)

            @block.vector
            def _(v):
                ch = Chain(v, S["dve_chain"])
                v.memset(b2sel0[:], 0.0)
                ch.step(v.memset(b2sel1[:], 0.0))
                v.sem_inc(S["set_ready"], 1)
                v.memset(ones[:], 1.0)
                v.memset(ones_mean[:], 1.0 / (ALLT * P))
                v.memset(zeros[:], 0.0)
                v.memset(base[:], 0.0)
                v.memset(xT[:, 0:WINDOW], 0.0)
                v.memset(kT[:, 0:WINDOW], 0.0)
                v.memset(ten_k[:, 0, :], 1e4)
                ch.step(v.memset(ten_k[:, 1, :], -1e4))
                v.wait_ge(S["x_loaded"], 1)
                v.tensor_copy(row_of_t[:], sbuf["row_of_t"])
                v.tensor_copy(window_mask[:], sbuf["window_mask"])
                ch.step(v.tensor_scalar(wqk[:], qn[:], kn[:, 0:1], float(np.sqrt(D)), ALU.mult, ALU.mult))
                ch.step(v.tensor_scalar(bvrep[:], zeros[0:D, :], bvcol[:, 0:1], None, ALU.add))
                v.sem_inc(S["h_ready"], 1)
                v.wait_ge(S["tok_done"], 1)
                v.tensor_copy(weff[:], bank[0][:].rearrange("p (o r) -> p r o", r=STRIDE))
                v.wait_ge(S["proj_done"], 1)
                v.tensor_tensor(vbias[:], bank[1][:, 0:D], blrow[:], ALU.add)
                ch.step(v.tensor_copy(wvl[:], bank[1][0:D, D:2 * D]))

            @block.tensor
            def _(pe):
                pe.wait_ge(S["x_loaded"], 1)
                w = sbuf["tok_w"]
                for o in range(D):
                    for j in range(2):
                        ins = nc.tensor.matmul(bank[0][D * j:D * j + D, o * STRIDE:(o + 1) * STRIDE], w[:, o, :],
                                               sbuf["dft"][:, j * STRIDE:(j + 1) * STRIDE], start=True, stop=True)
                ins.then_inc(S["tok_done"], 1)
                pe.wait_ge(S["h_ready"], 1)
                nc.tensor.matmul(bank[1][:, 0:D], bvrep[:], sbuf["wl1"][:], start=True, stop=True)
                nc.tensor.matmul(bank[1][0:D, D:2 * D], sbuf["wvT1"][:], sbuf["wl1"][:], start=True,
                                 stop=True).then_inc(S["proj_done"], 1)

        def load_x(sp, b, s):
            sp.dma_start(xb[:], inp["x"][bass.ds(b, 1)].rearrange("b p v t -> (b p) v t")).then_inc(s, 16)

        def tokens(block):
            @block.tensor
            def _(pe):
                steps = xflat.rearrange("p (s r) -> p r s", r=STRIDE)
                for i in range(TILES):
                    for r in range(STRIDE):
                        ins = nc.tensor.matmul(bank[0][:, D * i:D * i + D], steps[:, r, P * i:P * i + P], weff[:, r, :],
                                               start=(r == 0), stop=(r == STRIDE - 1))
                ins.then_inc(S["tok_done"], 1)
                pe.wait_ge(S["xn_ready"], 1)
                transpose_tiles(pe, xn, TILES, [1, 2])

            @block.scalar
            def _(a):
                a.wait_ge(S["tok_done"], 1)
                nc.scalar.activation(h[:].rearrange("p i d -> p (i d)"), bank[0][:], ACT.Copy).then_inc(S["h_ready"], 1)
                a.wait_ge(S["xT_psum"], 1)
                nc.scalar.activation(xT[:, WINDOW:WINDOW + HALF], bank[1][:], ACT.Copy)

            @block.vector
            def _(v):
                ch = Chain(v, S["dve_chain"])
                v.wait_ge(S["h_ready"], 1)
                layernorm(v, ch, h[:], xn[:], tmp[:], moe[:], st, TILES)
                v.sem_inc(S["xn_ready"], 1)
                v.wait_ge(S["xT_psum"], 2)
                v.tensor_copy(xT[:, WINDOW + HALF:], bank[2][:])

        UNITS = 2 * (PAIRS + 1)

        def project(block):
            @block.tensor
            def _(pe):
                for u in range(UNITS):
                    pair, w = divmod(u, 2)
                    if u >= 3:
                        pe.wait_ge(S["prod_done"], u - 2)
                        pe.wait_ge(S["square_done"], u - 2)
                    for c in range(2):
                        r = slice(D * c, D * c + D)
                        lhs = sbuf["wq"][r, pair, :] if pair < PAIRS else sbuf["wk"][r, :]
                        ins = nc.tensor.matmul(bank[2 * (u % 3) + c][:], lhs,
                                               xT[r, WINDOW + w * HALF:WINDOW + (w + 1) * HALF], start=True, stop=True)
                    ins.then_inc(S["proj_done"], 1)
                pe.wait_ge(S["square_done"], UNITS)
                for i in range(TILES):
                    nc.tensor.matmul(bank[6][:, i:i + 1], kT[:, WINDOW + P * i:WINDOW + P * i + P],
                                     sbuf["by_head"][:, 0:1], start=True, stop=True)
                for c in range(CHUNKS):
                    for hh in range(2):
                        ins = nc.tensor.matmul(bank[6][:, 8 + 4 * c + 2 * hh:10 + 4 * c + 2 * hh],
                                               sq[:, c, 4 * hh:4 * hh + 4, :].rearrange("p a t -> p (a t)"),
                                               sbuf["by_head"][:], start=True, stop=True)
                ins.then_inc(S["ssq_done"], 1)
                pe.wait_ge(S["prod_done"], UNITS)
                for n in range(4):
                    for m in range(8):
                        c = 8 * n + m
                        ins = nc.tensor.matmul(bank[2 + n][:, D * m:D * m + D], xT[0:D, CHUNK * c:CHUNK * c + P],
                                               sbuf["wv0"][:], start=True, stop=True)
                    ins.then_inc(S["v_psum"], 1)
                nc.tensor.matmul(bank[7][:, 0:D], xT[0:D, SEQ:SEQ + P], sbuf["wv0"][:], start=True,
                                 stop=True).then_inc(S["v_psum"], 1)
                pe.wait_ge(S["k_root"], 1)
                for w in range(2):
                    ins = nc.tensor.matmul(bank[w][:], ones[:], diag[:, w * HALF:(w + 1) * HALF], start=True, stop=True)
                ins.then_inc(S["k_root"], 1)
                pe.wait_ge(S["v_act"], 3)
                pe.wait_ge(S["v_dve"], 2)
                for m in range(4):
                    nc.tensor.matmul(bank[2 + m][:], sbuf["copies"][:, m, :], vwin[:, NQ:CHUNKS + 1:NQ, :], start=True,
                                     stop=True).then_inc(S["v_psum"], 1)

            @block.scalar
            def _(a):
                for u in range(UNITS):
                    pair, w = divmod(u, 2)
                    a.wait_ge(S["cos_done"], u + 1)
                    dst = (sq[:, w * CHUNKS // 2:(w + 1) * CHUNKS // 2, pair, :] if pair < PAIRS
                           else kT[:, WINDOW + w * HALF:WINDOW + (w + 1) * HALF])
                    src = bank[2 * (u % 3)][:]
                    if pair < PAIRS:
                        src = src.rearrange("p (c t) -> p c t", t=CHUNK)
                    nc.scalar.activation(dst, src, ACT.Square).then_inc(S["square_done"], 1)
                for n in (0, 2):
                    a.wait_ge(S["v_psum"], n + 1)
                    nc.scalar.activation(vwin[:, 8 * n:8 * n + 8, :].rearrange("p c d -> p (c d)"), bank[2 + n][:],
                                         ACT.Copy).then_inc(S["v_act"], 1)
                a.wait_ge(S["v_psum"], 5)
                nc.scalar.activation(vwin[:, CHUNKS, :], bank[7][:, 0:D], ACT.Copy).then_inc(S["v_act"], 1)
                for m in (0, 2):
                    a.wait_ge(S["v_psum"], 6 + m)
                    nc.scalar.activation(vrem[:, m::NQ, :], bank[2 + m][:].rearrange("p (c d) -> p c d", d=D), ACT.Copy)

            @block.vector
            def _(v):
                ch = Chain(v, S["dve_chain"])
                for u in range(UNITS):
                    pair, w = divmod(u, 2)
                    cols = slice(w * HALF, (w + 1) * HALF)
                    v.wait_ge(S["proj_done"], u + 1)
                    if u >= 2:
                        v.wait_ge(S["rot_done"], u - 1)
                    v.tensor_tensor(prod[:, u % 2, 0, :], bank[2 * (u % 3)][:], sbuf["rope_cos"][:, cols],
                                    ALU.mult).then_inc(S["cos_done"], 1)
                    v.tensor_tensor(prod[:, u % 2, 1, :], bank[2 * (u % 3) + 1][:], sbuf["rope_sin"][:, cols],
                                    ALU.mult).then_inc(S["prod_done"], 1)
                v.wait_ge(S["ssq_done"], 1)
                ch.step(v.tensor_scalar(rk[:], bank[6][:, 0:TILES], D * RMS_EPS, None, ALU.add))
                one_over_root(v, ch, rk[:], rk[:])
                v.tensor_tensor(diag[:].rearrange("p (i k) -> p i k", k=P), rows(ident[:], TILES), bc(rk[:], P),
                                ALU.mult).then_inc(S["k_root"], 1)
                ch.step(v.tensor_scalar(rqflat, bank[6][:, 8:8 + NQ * CHUNKS], D * RMS_EPS, None, ALU.add))
                one_over_root(v, ch, rqflat, rqflat)
                v.wait_ge(S["k_root"], 2)
                v.wait_ge(S["rot_done"], UNITS)
                for w in range(2):
                    v.scalar_tensor_tensor(out=kT[:, WINDOW + w * HALF:WINDOW + (w + 1) * HALF], in0=prod[:, w, 0, :],
                                           scalar=wqk[:, 0:1], in1=bank[w][:], op0=ALU.mult, op1=ALU.mult)
                for n in (1, 3):
                    v.wait_ge(S["v_psum"], n + 1)
                    v.tensor_copy(vwin[:, 8 * n:8 * n + 8, :].rearrange("p c d -> p (c d)"),
                                  bank[2 + n][:]).then_inc(S["v_dve"], 1)
                for m in (1, 3):
                    v.wait_ge(S["v_psum"], 6 + m)
                    v.tensor_copy(vrem[:, m::NQ, :], bank[2 + m][:].rearrange("p (c d) -> p c d", d=D))

            @block.gpsimd
            def _(g):
                for u in range(UNITS):
                    pair, w = divmod(u, 2)
                    g.wait_ge(S["prod_done"], u + 1)
                    dst, first, second = prod[:, u % 2, 0, :], prod[:, u % 2, 0, :], prod[:, u % 2, 1, :]
                    if pair < PAIRS:
                        dst = qT[:, w * CHUNKS // 2:(w + 1) * CHUNKS // 2, pair, :]
                        first, second = (z.rearrange("p (c t) -> p c t", t=CHUNK) for z in (first, second))
                    g.tensor_tensor(dst, first, second, ALU.add).then_inc(S["rot_done"], 1)

        def windowed(block, b):
            def s_bank(c, e):
                return bank[2 * (c % 2) + e]

            @block.sync
            def _(sp):
                load_x(sp, b, S["x_loaded"])
                sp.wait_ge(S["x_loaded"], 16)

            @block.tensor
            def _(pe):
                def scores(c):
                    if c >= 2:
                        pe.wait_ge(S["exp_done"], NQ * (c - 1))
                    variant = min(c, EARLY)
                    mask = rows(window_mask[:, variant, :], 2)
                    for e in range(2):
                        nc.tensor.matmul(s_bank(c, e)[:, 0:2 * SPAN], row_of_t[:], mask, start=True, stop=True,
                                         skip_group_check=True)
                    for hh in range(2):
                        for e in range(2):
                            r = slice(D * e, D * e + D)
                            ins = nc.tensor.matmul(s_bank(c, e)[:, SPAN * hh:SPAN * hh + SPAN],
                                                   qT[r, c, 4 * hh:4 * hh + 4, :].rearrange("p a t -> p (a t)"),
                                                   kT[r, CHUNK * c:CHUNK * c + SPAN], start=False, stop=True,
                                                   skip_group_check=True)
                    ins.then_inc(S["scores_done"], 1)

                def turn(c):
                    pe.wait_ge(S["scaled"], c + 1)
                    if c >= 2:
                        pe.wait_ge(S["pT_ready"], c - 1)
                        pe.wait_ge(S["pTr_ready"], c - 1)
                    for q in range(NQ):
                        nc.tensor.transpose(bank[4 + c % 2][:, P * q:P * q + P], probs[:, c % 3, q, 0:P], ident[:])
                    nc.tensor.transpose(bank[6 + c % 2][:, 0:P], own[:, c % 2, :],
                                        ident[:]).then_inc(S["transposed"], 1)

                def values(c):
                    pe.wait_ge(S["pT_ready"], c + 1)
                    pe.wait_ge(S["pTr_ready"], c + 1)
                    if c >= 2:
                        pe.wait_ge(S["oT_ready"], c - 1)
                    pe.wait_ge(S["exp_done"], NQ * min(c + 3, CHUNKS))
                    for own_keys in range(2):
                        for hh in range(2):
                            for e in range(2):
                                q = 2 * e + hh
                                o = s_bank(c, hh)[D * e:D * e + D, 2 * SPAN:2 * SPAN + P]
                                r = slice(CHUNK * q, CHUNK * q + CHUNK)
                                if own_keys:
                                    ins = nc.tensor.matmul(o, vrem[r, c, :], pTr[r, c % 2, :], start=False, stop=True,
                                                           tile_position=(CHUNK * q, D * e), skip_group_check=True)
                                else:
                                    nc.tensor.matmul(o, vwin[:, c, :], pT[:, c % 2, q, :], start=True, stop=True,
                                                     skip_group_check=True)
                    ins.then_inc(S["pv_done"], 1)

                for n in range(CHUNKS + 4):
                    if n >= 4:
                        values(n - 4)
                    if n < CHUNKS:
                        scores(n)
                    if 2 <= n < CHUNKS + 2:
                        turn(n - 2)
                pe.wait_ge(S["oT_ready"], CHUNKS)
                for i in range(TILES):
                    for p in range(PAIRS):
                        ins = nc.tensor.matmul(bank[0][:, D * i:D * i + D], oT[:, p, P * i:P * i + P],
                                               sbuf["wo0"][:, p, :], start=(p == 0), stop=(p == PAIRS - 1))
                ins.then_inc(S["wo_done"], 1)
                pe.wait_ge(S["xn_ready"], 1)
                transpose_tiles(pe, xn, TILES, [1, 2])

            @block.vector
            def _(v):
                ch = Chain(v, S["dve_chain"])
                for n in range(CHUNKS + 2):
                    c = n
                    if c < CHUNKS:
                        v.wait_ge(S["scores_done"], c + 1)
                        for e in range(2):
                            ins = v.tensor_reduce(small[:, c % 4, 0, 2 * e:2 * e + 2],
                                                  s_bank(c, e)[:, 0:2 * SPAN].rearrange("p (a k) -> p a k", a=2),
                                                  X, ALU.max)
                        ch.step(ins)
                        v.scalar_tensor_tensor(out=small[:, c % 4, 1, :].rearrange("p (e a) -> p e a", e=2),
                                               in0=small[:, c % 4, 0, :].rearrange("p (e a) -> p e a", e=2),
                                               scalar=-1.0, in1=rq[:, c].rearrange("p a e -> p e a"), op0=ALU.mult,
                                               op1=ALU.mult).then_inc(S["bias_ready"], 1)
                    c = n - 1
                    if 0 <= c < CHUNKS:
                        v.wait_ge(S["exp_done"], NQ * (c + 1))
                        ch.step(v.reciprocal(small[:, c % 4, 3, :], small[:, c % 4, 2, :]))
                        if c >= 2:
                            v.wait_ge(S["transposed"], c - 1)
                        for q in range(NQ):
                            v.tensor_scalar(probs[:, c % 3, q, 0:P], probs[:, c % 3, q, 0:P], small[:, c % 4, 3, q:q + 1],
                                            None, ALU.mult)
                        v.tensor_tensor(own[:, c % 2, :].rearrange("p (q k) -> p q k", q=NQ), probs[:, c % 3, :, P:SPAN],
                                        bc(small[:, c % 4, 3, :], CHUNK), ALU.mult).then_inc(S["scaled"], 1)
                    c = n - 2
                    if c >= 0:
                        v.wait_ge(S["transposed"], c + 1)
                        if c >= 2:
                            v.wait_ge(S["pv_done"], c - 1)
                        v.tensor_copy(pT[:, c % 2, :, :].rearrange("p q r -> p (q r)"),
                                      bank[4 + c % 2][:]).then_inc(S["pT_ready"], 1)
                v.wait_ge(S["wo_done"], 1)
                ch.step(v.tensor_tensor(h[:].rearrange("p i d -> p (i d)"), h[:].rearrange("p i d -> p (i d)"),
                                        bank[0][:], ALU.add))
                layernorm(v, ch, h[:], xn[:], tmp[:], moe[:], st, TILES)
                v.sem_inc(S["xn_ready"], 1)
                v.wait_ge(S["xT_psum"], 2)
                v.tensor_copy(xT[:, WINDOW + HALF:], bank[2][:])

            @block.scalar
            def _(a):
                for n in range(CHUNKS + 4):
                    c = n
                    if c < CHUNKS:
                        a.wait_ge(S["bias_ready"], c + 1)
                        if c >= 3:
                            a.wait_ge(S["transposed"], c - 2)
                        for q in range(NQ):
                            nc.scalar.activation(probs[:, c % 3, q, :],
                                                 s_bank(c, q // 2)[:, SPAN * (q % 2):SPAN * (q % 2) + SPAN], ACT.Exp,
                                                 bias=small[:, c % 4, 1, q:q + 1], scale=rq[:, c, q % 2, q // 2:q // 2 + 1],
                                                 accum_out=small[:, c % 4, 2, q:q + 1]).then_inc(S["exp_done"], 1)
                    c = n - 2
                    if 0 <= c < CHUNKS:
                        a.wait_ge(S["transposed"], c + 1)
                        if c >= 2:
                            a.wait_ge(S["pv_done"], c - 1)
                        nc.scalar.activation(pTr[:, c % 2, :], bank[6 + c % 2][:, 0:P],
                                             ACT.Copy).then_inc(S["pTr_ready"], 1)
                    c = n - 4
                    if c >= 0:
                        a.wait_ge(S["pv_done"], c + 1)
                        for hh in range(2):
                            ins = nc.scalar.activation(
                                oT[:, 4 * hh:4 * hh + 4, CHUNK * c:CHUNK * (c + 1)],
                                s_bank(c, hh)[:, 2 * SPAN:2 * SPAN + P].rearrange("p (a t) -> p a t", t=CHUNK),
                                ACT.Copy)
                        ins.then_inc(S["oT_ready"], 1)
                a.wait_ge(S["xT_psum"], 1)
                nc.scalar.activation(xT[:, WINDOW:WINDOW + HALF], bank[1][:], ACT.Copy)

        def first_argmax(v, ch, p, top, cand, best, hot, tiles):
            ch.step(v.tensor_reduce(top, p, X, ALU.max))
            ch.step(v.tensor_tensor(cand, p, bc(top, E), ALU.is_ge))
            ch.step(v.tensor_tensor(cand, cand, rows(sbuf["first_weight"][:], tiles), ALU.mult))
            ch.step(v.tensor_reduce(best, cand, X, ALU.max))
            ch.step(v.tensor_tensor(hot, cand, bc(best, E), ALU.is_equal))

        def experts(block, b):
            @block.tensor
            def _(pe):
                for i in range(TILES):
                    ins = nc.tensor.matmul(bank[7][:, E * i:E * i + E], xT[0:D, WINDOW + P * i:WINDOW + P * i + P],
                                           sbuf["router"][:], start=True, stop=True)
                ins.then_inc(S["tok_done"], 1)
                for u in range(8):
                    k, w = divmod(u, 2)
                    r = slice(D * w, D * w + D)
                    if u >= 4:
                        pe.wait_ge(S["exp_done"], u - 3 + 1)
                    nc.tensor.matmul(bank[u % 4][:], sbuf["moe_w1"][r, k, :],
                                     xT[r, WINDOW + w * HALF:WINDOW + (w + 1) * HALF], start=True,
                                     stop=True).then_inc(S["proj_done"], 1)
                pe.wait_ge(S["bias_ready"], 1)
                nc.tensor.transpose(bank[6][0:TILES * E, 0:P], comb[:].rearrange("p i e -> p (i e)"),
                                    ident[:]).then_inc(S["transposed"], 1)
                pe.wait_ge(S["exp_done"], 9)
                pe.wait_ge(S["pT_ready"], 1)
                for i in range(TILES):
                    if i >= 2:
                        pe.wait_ge(S["prod_done"], i - 1)
                    for k in range(E // 2):
                        for r in range(2):
                            nc.tensor.matmul(bank[2 * (i % 2) + r][:, D * k:D * k + D],
                                             hT[D * r:D * r + D, SEQ * k + P * i:SEQ * k + P * i + P],
                                             sbuf["moe_w2"][D * r:D * r + D, k, :], start=True, stop=True)
                    nc.tensor.matmul(bank[5][:, D * i:D * i + D], combT[:], b2sel0[:, i, :], start=True,
                                     stop=True).then_inc(S["pv_done"], 1)
                pe.wait_ge(S["xn_ready"], 1)
                transpose_tiles(pe, xn, TILES, [6, 4])

            @block.scalar
            def _(a):
                a.wait_ge(S["h_ready"], 1)
                nc.scalar.activation(lg[:, 1], lg[:, 0], ACT.Exp).then_inc(S["exp_done"], 1)
                for u in range(8):
                    k, w = divmod(u, 2)
                    a.wait_ge(S["proj_done"], u + 1)
                    nc.scalar.activation(hT[:, SEQ * k + w * HALF:SEQ * k + (w + 1) * HALF], bank[u % 4][:], ACT.Gelu,
                                         bias=sbuf["moe_b1"][:, k:k + 1]).then_inc(S["exp_done"], 1)
                a.wait_ge(S["xT_psum"], 1)
                nc.scalar.activation(xT[:, WINDOW:WINDOW + HALF], bank[6][:], ACT.Copy)

            @block.vector
            def _(v):
                ch = Chain(v, S["dve_chain"])
                v.wait_ge(S["tok_done"], 1)
                logits = bank[7][:, 0:TILES * E].rearrange("p (i e) -> p i e", e=E)
                ch.step(v.tensor_reduce(st[:, 0, :], logits, X, ALU.max))
                ch.step(v.tensor_tensor(lg[:, 0], logits, bc(st[:, 0, :], E), ALU.subtract))
                v.sem_inc(S["h_ready"], 1)
                v.wait_ge(S["exp_done"], 1)
                ch.step(v.tensor_reduce(st[:, 1, :], lg[:, 1], X, ALU.add))
                ch.step(v.reciprocal(st[:, 2, :], st[:, 1, :]))
                ch.step(v.tensor_tensor(lg[:, 2], lg[:, 1], bc(st[:, 2, :], E), ALU.mult))
                first_argmax(v, ch, lg[:, 2], st[:, 3, :], lg[:, 3], st[:, 4, :], lg[:, 4], TILES)
                ch.step(v.scalar_tensor_tensor(out=lg[:, 5], in0=lg[:, 4], scalar=-2.0, in1=lg[:, 2], op0=ALU.mult,
                                               op1=ALU.add))
                first_argmax(v, ch, lg[:, 5], st[:, 5, :], lg[:, 3], st[:, 4, :], lg[:, 6], TILES)
                ch.step(v.tensor_tensor(st[:, 6, :], st[:, 3, :], st[:, 5, :], ALU.add))
                ch.step(v.tensor_scalar(st[:, 7, :], st[:, 6, :], 1e-12, None, ALU.max))
                ch.step(v.reciprocal(st[:, 6, :], st[:, 7, :]))
                ch.step(v.tensor_tensor(lg[:, 7], lg[:, 4], lg[:, 6], ALU.add))
                ch.step(v.tensor_tensor(lg[:, 7], lg[:, 7], lg[:, 2], ALU.mult))
                ch.step(v.tensor_tensor(comb[:], lg[:, 7], bc(st[:, 6, :], E), ALU.mult))
                v.sem_inc(S["bias_ready"], 1)
                v.wait_ge(S["transposed"], 1)
                v.tensor_copy(combT[:], bank[6][0:TILES * E, 0:P]).then_inc(S["pT_ready"], 1)
                for i in range(TILES):
                    v.wait_ge(S["pv_done"], i + 1)
                    for r in range(2):
                        w = comb[:, i, r::2]
                        ins = v.tensor_tensor(yw[:, i % 2, r::2, :],
                                              bank[2 * (i % 2) + r][:, 0:E // 2 * D].rearrange("p (k d) -> p k d", d=D),
                                              bc(w, D), ALU.mult)
                        if r == 0:
                            continue
                        ins.then_inc(S["prod_done"], 1)
                    v.wait_ge(S["prod_done"], i + 1)
                    ins = v.tensor_reduce(moe[:, i, :], yw[:, i % 2].rearrange("p e d -> p d e"), X, ALU.add)
                ch.step(ins)
                mflat = moe[:].rearrange("p i d -> p (i d)")
                ch.step(v.tensor_tensor(mflat, mflat, bank[5][:], ALU.add))
                ch.step(v.tensor_tensor(moe[:], moe[:], xn[:, :, 0, :], ALU.add))
                ch.step(v.tensor_tensor(h[:], h[:], moe[:], ALU.add))
                layernorm(v, ch, h[:], xn[:], tmp[:], moe[:], st, TILES)
                v.sem_inc(S["xn_ready"], 1)
                v.tensor_tensor(res[:, bass.ds(b * TILES, TILES), :], h[:], xn[:, :, 0, :], ALU.add)
                v.wait_ge(S["xT_psum"], 2)
                v.tensor_copy(xT[:, WINDOW + HALF:], bank[4][:])

        qT1 = big1[:, 0, :]
        kT1 = big1[:, 1, :]
        v1 = big1[:, 2, 0:HALF].rearrange("p (i d) -> p i d", d=D)
        p1 = big2[:, 0:2, :]
        pT1 = big2[:, 2:4, :]

        def full(block, b):
            @block.tensor
            def _(pe):
                for n, name in enumerate(("wq1", "wk1")):
                    for w in range(2):
                        r = slice(D * w, D * w + D)
                        ins = nc.tensor.matmul(bank[2 * n + w][:], sbuf[name][r, :],
                                               xT[r, WINDOW + w * HALF:WINDOW + (w + 1) * HALF], start=True, stop=True)
                    ins.then_inc(S["proj_done"], 1)
                for i in range(TILES):
                    ins = nc.tensor.matmul(bank[4][:, D * i:D * i + D], xT[0:D, WINDOW + P * i:WINDOW + P * i + P],
                                           wvl[:], start=True, stop=True)
                ins.then_inc(S["proj_done"], 1)

                def scores(i):
                    if i == 0:
                        pe.wait_ge(S["h_ready"], 2)
                        pe.wait_ge(S["square_done"], 2)
                    if i >= 2:
                        pe.wait_ge(S["exp_done"], i - 1)
                    for w in range(2):
                        r = slice(D * w, D * w + D)
                        ins = nc.tensor.matmul(bank[2 * (i % 2) + w][:], qT1[r, P * i:P * i + P],
                                               kT1[r, w * HALF:(w + 1) * HALF], start=True, stop=True)
                    ins.then_inc(S["scores_done"], 1)

                def turn(i):
                    pe.wait_ge(S["exp_done"], i + 1)
                    if i == 0:
                        pe.wait_ge(S["v_act"], 1)
                    else:
                        pe.wait_ge(S["pT_ready"], i)
                        pe.wait_ge(S["pTr_ready"], i)
                    for k in range(8):
                        ins = nc.tensor.transpose(bank[4 + k // 4][:, P * (k % 4):P * (k % 4) + P],
                                                  p1[:, i % 2, P * k:P * k + P], ident[:])
                        if k % 4 == 3:
                            ins.then_inc(S["transposed"], 1)

                def values(i):
                    pe.wait_ge(S["pT_ready"], i + 1)
                    pe.wait_ge(S["pTr_ready"], i + 1)
                    if i >= 2:
                        pe.wait_ge(S["last"], i - 1)
                    for k in range(8):
                        ins = nc.tensor.matmul(bank[6 + i % 2][:, 0:D], pT1[:, i % 2, P * k:P * k + P], v1[:, k, :],
                                               start=(k == 0), stop=(k == 7))
                    ins.then_inc(S["pv_done"], 1)

                for n in range(TILES + 2):
                    if n < TILES:
                        scores(n)
                    if 1 <= n < TILES + 1:
                        turn(n - 1)
                    if n >= 2:
                        values(n - 2)

            @block.scalar
            def _(a):
                a.wait_ge(S["proj_done"], 1)
                for w in range(2):
                    nc.scalar.activation(qT1[:, w * HALF:(w + 1) * HALF], bank[w][:], ACT.Identity,
                                         bias=bq[:, 0:1]).then_inc(S["h_ready"], 1)
                a.wait_ge(S["proj_done"], 3)
                nc.scalar.activation(v1.rearrange("p i d -> p (i d)"), bank[4][:], ACT.Copy).then_inc(S["v_act"], 1)
                for n in range(TILES + 1):
                    if n < TILES:
                        a.wait_ge(S["bias_ready"], n + 1)
                        if n >= 2:
                            a.wait_ge(S["transposed"], 2 * n - 2)
                        for w in range(2):
                            ins = nc.scalar.activation(p1[:, n % 2, w * HALF:(w + 1) * HALF], bank[2 * (n % 2) + w][:],
                                                       ACT.Exp, bias=st[:, 1, n:n + 1], scale=1.0 / D,
                                                       accum_out=st[:, 2 + w, n:n + 1])
                        ins.then_inc(S["exp_done"], 1)
                    i = n - 1
                    if i >= 0:
                        a.wait_ge(S["transposed"], 2 * i + 1)
                        if i >= 2:
                            a.wait_ge(S["pv_done"], i - 1)
                        nc.scalar.activation(pT1[:, i % 2, 0:HALF], bank[4][:], ACT.Copy).then_inc(S["pTr_ready"], 1)

            @block.vector
            def _(v):
                ch = Chain(v, S["dve_chain"])
                v.wait_ge(S["proj_done"], 2)
                for w in range(2):
                    v.tensor_scalar(kT1[:, w * HALF:(w + 1) * HALF], bank[2 + w][:], bk[:, 0:1], None,
                                    ALU.add).then_inc(S["square_done"], 1)
                for n in range(TILES + 2):
                    if n < TILES:
                        v.wait_ge(S["scores_done"], n + 1)
                        for w in range(2):
                            ins = v.tensor_reduce(st[:, 4 + w, n:n + 1], bank[2 * (n % 2) + w][:], X, ALU.max)
                        ch.step(ins)
                        ch.step(v.tensor_tensor(st[:, 6, n:n + 1], st[:, 4, n:n + 1], st[:, 5, n:n + 1], ALU.max))
                        v.tensor_scalar(st[:, 1, n:n + 1], st[:, 6, n:n + 1], -1.0 / D, None,
                                        ALU.mult).then_inc(S["bias_ready"], 1)
                    i = n - 1
                    if 0 <= i < TILES:
                        v.wait_ge(S["transposed"], 2 * i + 2)
                        if i >= 2:
                            v.wait_ge(S["pv_done"], i - 1)
                        v.tensor_copy(pT1[:, i % 2, HALF:], bank[5][:]).then_inc(S["pT_ready"], 1)
                        ch.step(v.tensor_tensor(st[:, 7, i:i + 1], st[:, 2, i:i + 1], st[:, 3, i:i + 1], ALU.add))
                        ch.step(v.reciprocal(st[:, 0, i:i + 1], st[:, 7, i:i + 1]))
                    i = n - 2
                    if i >= 0:
                        v.wait_ge(S["pv_done"], i + 1)
                        v.scalar_tensor_tensor(out=hl_row(b, i), in0=bank[6 + i % 2][:, 0:D], scalar=st[:, 0, i:i + 1],
                                               in1=vbias[:], op0=ALU.mult, op1=ALU.add).then_inc(S["last"], 1)

        def hl_row(b, i):
            return hl[:, bass.ds(b * TILES + i, 1), :].rearrange("p a d -> p (a d)")

        def batchnorm(block):
            @block.sync
            def _(sp):
                for k in ("ffn_w1", "ffn_w2"):
                    sp.dma_start(sbuf[k], inp[k]).then_inc(S["x_loaded"], 16)
                sp.wait_ge(S["x_loaded"], 32)

            q4 = [slice(TILES * g, TILES * g + TILES) for g in range(IMAGES)]

            @block.tensor
            def _(pe):
                for step in range(2):
                    if step:
                        pe.wait_ge(S["square_done"], 1)
                    src = (hl, big1_tok)[step]
                    for g in range(IMAGES):
                        ins = nc.tensor.matmul(bank[step][:], ones_mean[:], src[:, q4[g], :], start=(g == 0),
                                               stop=(g == IMAGES - 1))
                    ins.then_inc(S["proj_done"], 1)

            @block.scalar
            def _(a):
                a.wait_ge(S["h_ready"], 1)
                nc.scalar.activation(big1_tok[:], hl[:], ACT.Square).then_inc(S["square_done"], 1)

            @block.vector
            def _(v):
                ch = Chain(v, S["dve_chain"])
                v.wait_ge(S["proj_done"], 1)
                ch.step(v.tensor_reduce(mean_row[:], bank[0][:].rearrange("p (i d) -> p d i", d=D), X, ALU.add))
                ch.step(v.tensor_tensor(hl[:], hl[:], rows(mean_row[:], ALLT), ALU.subtract))
                v.sem_inc(S["h_ready"], 1)
                v.wait_ge(S["proj_done"], 2)
                ch.step(v.tensor_reduce(var_row[:], bank[1][:].rearrange("p (i d) -> p d i", d=D), X, ALU.add))
                ch.step(v.tensor_scalar(var_row[:], var_row[:], BN_EPS, None, ALU.add))
                one_over_root(v, ch, mean_row[:], var_row[:])
                ch.step(v.tensor_copy(var_row[:], mean_row[:]))
                ch.step(v.tensor_tensor(var_row[:], var_row[:], gammarow[:], ALU.mult))
                ch.step(v.tensor_tensor(hl[:], hl[:], rows(var_row[:], ALLT), ALU.mult))
                ch.step(v.tensor_tensor(hl[:], hl[:], rows(betarow[:], ALLT), ALU.add))
                ch.step(v.scalar_tensor_tensor(out=res[:], in0=hl[:], scalar=0.0, in1=res[:], op0=ALU.max, op1=ALU.add))

        big1_tok = big1[:].rearrange("p a b -> p (a b)")[:, 0:ALLT * D].rearrange("p (i d) -> p i d", d=D)

        G = GROUP_TILES
        hid = big2[:].rearrange("p a b -> p (a b)").rearrange("p (f t) -> p f t", t=GT)
        hg, xg, tg, mg = h[:, 0:G, :], xn[:, 0:G], tmp[:, 0:G, :], moe[:, 0:G, :]
        lc = [lg[:, k, 0:G, :] for k in range(8)]
        sc = [st[:, k, 0:G] for k in range(8)]

        def capacity_experts(block, g):
            @block.tensor
            def _(pe):
                pe.wait_ge(S["xn_ready"], 1)
                transpose_tiles(pe, xg, G, [6])
                pe.wait_ge(S["xT_dve"], 1)
                for i in range(G):
                    ins = nc.tensor.matmul(bank[7][:, E * i:E * i + E], xT[0:D, P * i:P * i + P], sbuf["gate"][:],
                                           start=True, stop=True)
                ins.then_inc(S["tok_done"], 1)

                def hidden(f):
                    r = slice(D * (f % 2), D * (f % 2) + D)
                    if f >= 4:
                        pe.wait_ge(S["v_act"], f // 2 - 1)
                        pe.wait_ge(S["v_dve"], f // 2 - 1)
                    nc.tensor.matmul(bank[f % 4][:], sbuf["ffn_w1"][r, f // 2, :], xT[r, 0:GT], start=True,
                                     stop=True).then_inc(S["proj_done"], 1)

                for f in range(FCH):
                    hidden(f)
                pe.wait_ge(S["bias_ready"], 1)
                ohb = lc[4].rearrange("p i e -> p (i e)")
                nc.tensor.matmul(bank[7][:, 64:64 + G * E], lower[:], ohb, start=True, stop=True)
                nc.tensor.matmul(bank[7][:, 128:128 + G * E], ones[:], ohb, start=True, stop=True).then_inc(S["ssq_done"], 1)
                pe.wait_ge(S["bias_ready"], 2)
                nc.tensor.transpose(bank[6][0:G * E, 0:P], lc[7].rearrange("p i e -> p (i e)"),
                                    ident[:]).then_inc(S["transposed"], 1)
                pe.wait_ge(S["pT_ready"], 1)
                pe.wait_ge(S["v_act"], FCH // 2)
                pe.wait_ge(S["v_dve"], FCH // 2)
                for i in range(G):
                    if i >= 2:
                        pe.wait_ge(S["prod_done"], i - 1)
                    for e in range(E):
                        for k in range(2):
                            nc.tensor.matmul(bank[4 + i % 2][:, D * e:D * e + D], hid[:, 2 * e + k, P * i:P * i + P],
                                             sbuf["ffn_w2"][:, 2 * e + k, :], start=(k == 0), stop=(k == 1))
                    nc.tensor.matmul(bank[6][:, 256 + D * i:256 + D * i + D], combT[0:G * E, :], b2sel1[:, i, :], start=True,
                                     stop=True).then_inc(S["pv_done"], 1)

            @block.scalar
            def _(a):
                for f in range(0, FCH, 2):
                    a.wait_ge(S["proj_done"], f + 1)
                    nc.scalar.activation(hid[:, f, :], bank[f % 4][:], ACT.Relu,
                                         bias=sbuf["ffn_b1"][:, f:f + 1]).then_inc(S["v_act"], 1)
                    if f == 0:
                        a.wait_ge(S["h_ready"], 1)
                        nc.scalar.activation(lc[1], lc[0], ACT.Exp).then_inc(S["exp_done"], 1)

            @block.vector
            def _(v):
                ch = Chain(v, S["dve_chain"])
                ch.step(v.tensor_copy(hg, res[:, bass.ds(g * G, G), :]))
                layernorm(v, ch, hg, xg, tg, mg, st, G)
                v.sem_inc(S["xn_ready"], 1)
                v.wait_ge(S["xT_psum"], 1)
                v.tensor_copy(xT[:, 0:GT], bank[6][:]).then_inc(S["xT_dve"], 1)
                v.wait_ge(S["tok_done"], 1)
                ch.step(v.tensor_tensor(lc[2], bank[7][:, 0:G * E].rearrange("p (i e) -> p i e", e=E),
                                        rows(gate_b[:], G), ALU.add))
                ch.step(v.tensor_reduce(sc[0], lc[2], X, ALU.max))
                ch.step(v.tensor_tensor(lc[0], lc[2], bc(sc[0], E), ALU.subtract))
                v.sem_inc(S["h_ready"], 1)

                def hidden(f):
                    v.wait_ge(S["proj_done"], f + 1)
                    v.tensor_scalar(hid[:, f, :], bank[f % 4][:], sbuf["ffn_b1"][:, f:f + 1], 0.0, ALU.add,
                                    ALU.max).then_inc(S["v_dve"], 1)

                hidden(1)
                v.wait_ge(S["exp_done"], 1)
                ch.step(v.tensor_reduce(sc[1], lc[1], X, ALU.add))
                ch.step(v.reciprocal(sc[2], sc[1]))
                ch.step(v.tensor_tensor(lc[2], lc[1], bc(sc[2], E), ALU.mult))
                first_argmax(v, ch, lc[2], sc[3], lc[3], sc[4], lc[4], G)
                v.sem_inc(S["bias_ready"], 1)
                for f in range(3, FCH, 2):
                    hidden(f)
                v.wait_ge(S["ssq_done"], 1)
                for i in range(G):
                    v.tensor_tensor(lc[5][:, i, :], bank[7][:, 64 + E * i:64 + E * i + E], base[:], ALU.add)
                    ch.step(v.tensor_tensor(base[:], base[:], bank[7][:, 128 + E * i:128 + E * i + E], ALU.add))
                ch.step(v.tensor_scalar(lc[6], lc[5], float(CAPACITY), None, ALU.is_le))
                ch.step(v.tensor_tensor(lc[6], lc[6], lc[4], ALU.mult))
                ch.step(v.tensor_tensor(lc[7], lc[6], bc(sc[3], E), ALU.mult))
                v.sem_inc(S["bias_ready"], 1)
                v.wait_ge(S["transposed"], 1)
                v.tensor_copy(combT[0:G * E, :], bank[6][0:G * E, 0:P]).then_inc(S["pT_ready"], 1)
                for i in range(G):
                    v.wait_ge(S["pv_done"], i + 1)
                    ins = v.tensor_tensor(yw[:, i % 2], bank[4 + i % 2][:].rearrange("p (e d) -> p e d", d=D),
                                          bc(lc[7][:, i, :], D), ALU.mult).then_inc(S["prod_done"], 1)
                    v.wait_ge(S["prod_done"], i + 1)
                    ins = v.tensor_reduce(moe[:, i, :], yw[:, i % 2].rearrange("p e d -> p d e"), X, ALU.add)
                ch.step(ins)
                y = [yout[:, k].rearrange("p i d -> p (i d)") for k in range(3)]
                my = moe[:, 0:G, :].rearrange("p i d -> p (i d)")
                ch.step(v.tensor_tensor(y[0], my, bank[6][:, 256:256 + G * D], ALU.add))
                v.memset(y[1], 0.0)
                ch.step(v.tensor_tensor(maski, y[0], y[0], ALU.is_equal))
                ch.step(v.copy_predicated(y[1], maski, y[0]))
                ch.step(v.tensor_scalar(maski, y[1], HUGE, None, ALU.is_gt))
                ch.step(v.copy_predicated(y[1], maski, ten_k[:, 0, :]))
                ch.step(v.tensor_scalar(maski, y[1], -HUGE, None, ALU.is_lt))
                ch.step(v.copy_predicated(y[1], maski, ten_k[:, 1, :]))
                ch.step(v.tensor_tensor(y[2], y[1], hg.rearrange("p i d -> p (i d)"), ALU.add))
                v.sem_inc(S["last"], 1)

            @block.sync
            def _(sp):
                sp.wait_ge(S["last"], 1)
                sp.dma_start(out[:, bass.ds(g * G, G), :], yout[:, 2]).then_inc(S["x_loaded"], 16)
                sp.wait_ge(S["x_loaded"], 16)

        stage(setup)
        with nc.Fori(0, IMAGES) as b:
            stage(tokens)
            stage(project)
            stage(lambda block: windowed(block, b + 1))
            stage(lambda block: experts(block, b))
            stage(lambda block: full(block, b))
        stage(batchnorm)
        with nc.Fori(0, GROUPS) as g:
            stage(lambda block: capacity_experts(block, g))


def constants():
    f = np.float32
    c = {"ident": np.eye(P, dtype=f), "lower": np.triu(np.ones((P, P), f))}
    k, n = np.arange(FREQ)[:, None], np.arange(PATCH)[None, :]
    ang = 2 * np.pi * k * n / PATCH
    c["dft"] = (np.concatenate([np.cos(ang), -np.sin(ang)]) / np.sqrt(PATCH)).astype(f)
    freqs = (f(10000.0) ** (f(-2.0) * np.arange(D // 2, dtype=f) / f(D))).astype(f)
    theta = np.arange(SEQ, dtype=f)[None, :] * np.repeat(freqs, 2)[:, None]
    sign = np.where(np.arange(D) % 2 == 0, -1.0, 1.0)[:, None]
    c["rope_cos"] = np.tile(np.cos(theta), (2, 1)).astype(f)
    c["rope_sin"] = np.tile(np.sin(theta) * sign, (2, 1)).astype(f)
    t = np.arange(CHUNK)
    c["row_of_t"] = np.tile(np.eye(CHUNK, dtype=f), (1, NQ))
    j = np.arange(SPAN)
    m = np.zeros((CHUNK, EARLY + 1, SPAN))
    for v in range(EARLY + 1):
        ok = (j[None] >= t[:, None]) & (j[None] <= t[:, None] + WINDOW) & (j[None] >= WINDOW - CHUNK * v)
        m[:, v] = np.where(ok, 0.0, -1e30)
    c["window_mask"] = m.astype(f)
    c["by_head"] = np.repeat(np.eye(2, dtype=f), D, axis=0)
    c["copies"] = np.stack([np.tile(np.eye(P, dtype=f)[:, CHUNK * m:CHUNK * (m + 1)], (1, NQ)) for m in range(NQ)], 1)
    c["first_weight"] = np.tile(np.arange(E, 0, -1, dtype=f), (P, 1))
    return c


def layouts(i):
    def two(a):
        return np.concatenate([a, a], axis=0)

    a = {k: np.asarray(v) for k, v in i.items()}
    x = a["x"].transpose(0, 1, 3, 2)
    swap = np.arange(D) ^ 1
    wq = a["L0_attn_wq"].reshape(PAIRS, 2, D, D)
    wk = a["L0_attn_wkv"][:D]
    w1 = a["L0_ffn_w1"].reshape(E // 2, 2, D, D)
    fw1 = a["L1_ffn_w1"].reshape(E, D, 2, P)
    return {
        "x": np.concatenate([x, np.concatenate([x[..., STRIDE:], np.repeat(x[..., -1:], STRIDE, -1)], -1)],
                            axis=1)[[*range(IMAGES), 0]],
        "tok_w": a["L0_tok_W"].reshape(D, 2 * FREQ, CH).transpose(1, 0, 2),
        "wq": np.concatenate([z.transpose(3, 0, 1, 2).reshape(D, PAIRS, P) for z in (wq, wq[:, :, swap])]),
        "wk": np.concatenate([np.concatenate([z.T, z.T], axis=1) for z in (wk, wk[swap])]),
        "wv0": a["L0_attn_wkv"][D:].T,
        "wo0": a["L0_attn_wo"].reshape(D, PAIRS, P).transpose(2, 1, 0),
        "q_norm": a["L0_attn_q_norm_w"].reshape(D, 1), "k_norm": a["L0_attn_k_norm_w"].reshape(D, 1),
        "router": a["L0_ffn_router_w"].T,
        "moe_w1": two(w1.transpose(2, 0, 1, 3).reshape(D, E // 2, P)),
        "moe_b1": a["L0_ffn_b1"].reshape(E // 2, P).T,
        "moe_w2": a["L0_ffn_w2"].reshape(E // 2, P, D).transpose(1, 0, 2),
        "moe_b2": a["L0_ffn_b2"],
        "wq1": two(np.concatenate([a["L1_attn_Wq"]] * 2, axis=1)),
        "wk1": two(np.concatenate([a["L1_attn_Wk"]] * 2, axis=1)),
        "bq1": a["L1_attn_bq"].reshape(D, 1), "bk1": a["L1_attn_bk"].reshape(D, 1),
        "bv1": a["L1_attn_bv"].reshape(D, 1),
        "wvT1": a["L1_attn_Wv"].T, "wl1": a["L1_attn_Wl"],
        "bl1": a["L1_attn_bl"].reshape(1, D), "gamma": a["L1_attn_gamma"].reshape(1, D),
        "beta": a["L1_attn_beta"].reshape(1, D), "gate_b": a["L1_ffn_gate_b"].reshape(1, E),
        "gate": a["L1_ffn_gate_w"],
        "ffn_w1": fw1.transpose(2, 1, 0, 3).reshape(P, E, P),
        "ffn_b1": a["L1_ffn_b1"].reshape(FCH, P).T,
        "ffn_w2": a["L1_ffn_w2"].reshape(FCH, P, D).transpose(1, 0, 2),
        "ffn_b2": a["L1_ffn_b2"],
    }


def kernel(**inputs):
    import concourse.bacc as _bacc
    from concourse.bass_utils import run_bass_kernel_spmd as _run

    nc = _bacc.Bacc("TRN2", target_bir_lowering=False, num_devices=1)
    arrays, args = {}, {}
    for name, a in {**constants(), **layouts(inputs)}.items():
        a = np.ascontiguousarray(a)
        arrays[f"in_{name}"] = a
        args[name] = nc.dram_tensor(f"in_{name}", a.shape, mybir.dt.from_np(a.dtype), kind="ExternalInput").ap()
    out = nc.dram_tensor("out", (IMAGES * SEQ, D), F32, kind="ExternalOutput").ap()
    program(nc, args, out.rearrange("(i p) d -> p i d", p=P))
    r = _run(nc, [arrays], core_ids=[0])
    return r.results[0]["out"].reshape(IMAGES, SEQ, D)
```

```python
from contextlib import ExitStack

import numpy as np

import concourse.bass as bass
from concourse import mybir

F32 = mybir.dt.float32
BF16 = mybir.dt.bfloat16
I32 = mybir.dt.int32
ALU = mybir.AluOpType
ACT = mybir.ActivationFunctionType
X = mybir.AxisListType.X

P = 128
IMAGES, CH, T, V = 4, 64, 128, 64
D = 64
PATCH, STRIDE = 16, 8
NPATCH = T // STRIDE
SEQ = V * NPATCH
TILES = SEQ // P
ALLT = IMAGES * TILES
FREQ = PATCH // 2 + 1
HEADS = 16
PAIRS = HEADS // 2
WINDOW = 128
CHUNK = 32
CHUNKS = SEQ // CHUNK
SPAN = WINDOW + CHUNK
EARLY = WINDOW // CHUNK
NQ = 4
E = 8
F1 = 256
FCH = E * F1 // P
GROUP_TILES = 4
GROUPS = ALLT // GROUP_TILES
GT = GROUP_TILES * P
CAPACITY = -(-5 * IMAGES * SEQ // (4 * E))
LN_EPS = 1e-5
BN_EPS = 1e-5
RMS_EPS = 1.1920929e-07
HUGE = 3.4028235e38
HALF = 512
Q_COLS, K_COLS, MOE_COLS, Q1_COLS = 0, 2 * PAIRS * P, 2 * (PAIRS + 1) * P, 2 * (PAIRS + 1) * P + E * D
K1_COLS = Q1_COLS + P
PROJ = K1_COLS + P
FFN_COLS = FCH * P + E


class Chain:

    def __init__(self, engine, sem):
        self.engine, self.sem, self.n = engine, sem, 0

    def step(self, ins):
        self.n += 1
        ins.then_inc(self.sem, 1)
        self.engine.wait_ge(self.sem, self.n)


def program(nc, inp, out):
    with ExitStack() as ctx:
        def sb(name, shape, dt=F32):
            return ctx.enter_context(nc.sbuf_tensor(name, shape, dt))

        def sem(name):
            return ctx.enter_context(nc.semaphore(name))

        bank = [ctx.enter_context(nc.psum_tensor(f"bank{i}", [P, HALF], F32)) for i in range(8)]

        shapes = {k: (list(v.shape), v.dtype) for k, v in inp.items()}
        loaded = ["ident", "dft", "rope_cos", "rope_sin", "row_of_t", "window_mask", "lower", "copies", "first_weight",
                  "tok_w", "by_head", "wv0", "wo0", "router", "moe_b1", "moe_w2", "wvT1", "wl1", "proj_w"]
        big1 = sb("big1", [P, PAIRS, SEQ])
        big2 = sb("big2", [P, PAIRS, SEQ])
        aside = ("tok_w", "row_of_t", "window_mask", "moe_w2", "proj_w")
        sbuf = {k: sb("s_" + k, *shapes[k]) for k in loaded if k not in aside}
        sbuf["tok_w"] = big1[0:2 * FREQ, 0:D * CH // SEQ, :].rearrange("p a n -> p (a n)").rearrange(
            "p (o c) -> p o c", c=CH)
        sbuf["moe_w2"] = big2[:, 0, P:P + E // 2 * D].rearrange("p (k d) -> p k d", d=D)
        sbuf["proj_w"] = big1[:, 4:8, :].rearrange("p a n -> p (a n)")[:, 0:PROJ]
        w_a, w_c = sb("w_a", [P, PROJ], BF16), sb("w_c", [P, PROJ], BF16)
        moe_w2 = sb("moe_w2", [P, E // 2, P])
        sbuf["row_of_t"] = big2[0:CHUNK, 0, 0:P]
        sbuf["window_mask"] = big2[0:CHUNK, 1, 0:(EARLY + 1) * SPAN].rearrange("p (v k) -> p v k", k=SPAN)
        row_of_t = sb("row_of_t", [CHUNK, P], BF16)
        window_mask = sb("window_mask", [CHUNK, EARLY + 1, SPAN], BF16)
        ident, lower = sbuf["ident"], sbuf["lower"]
        qn, kn, wqk = sb("qn", [P, 1]), sb("kn", [P, 1]), sb("wqk", [P, 1])
        bq, bk = sb("bq", [P, 1]), sb("bk", [P, 1])
        bvcol, bvrep = sb("bvcol", [D, 1]), sb("bvrep", [D, P])
        blrow, gammarow, betarow = sb("blrow", [P, D]), sb("gammarow", [P, D]), sb("betarow", [P, D])
        vbias = sb("vbias", [P, D])
        gate_b = sb("gate_b", [P, E])
        b2sel0 = sb("b2sel0", [TILES * E, TILES, D])
        ones, ones_mean, zeros = sb("ones", [P, P]), sb("ones_mean", [P, P]), sb("zeros", [P, P])
        wvl = sb("wvl", [D, D])
        weff = sb("weff", [P, STRIDE, D])

        xb = sb("xb", [P, V, T])
        xflat = xb[:].rearrange("p v t -> p (v t)")
        taken = 0

        def from_xb(n, dt=F32):
            nonlocal taken
            taken += n
            ap = xflat[:, taken - n:taken]
            return ap if dt == F32 else ap.bitcast(dt)

        ffn_w = from_xb(FFN_COLS)
        ffn_w2 = from_xb(FCH * D).rearrange("p (f d) -> p f d", d=D)
        b2sel1 = from_xb(P // E * D).rearrange("p (i d) -> p i d", d=D)
        ffn_a, ffn_c = from_xb(FFN_COLS // 2, BF16), from_xb(FFN_COLS // 2, BF16)
        gates = from_xb(ALLT * E).rearrange("p (i e) -> p i e", e=E)
        ten_k = from_xb(2 * GROUP_TILES * D).rearrange("p (s n) -> p s n", s=2)
        ffn_b1 = from_xb(FCH)
        st_all = from_xb(8 * ALLT).rearrange("p (k i) -> p k i", k=8)
        h = sb("h", [P, TILES, D])
        st = sb("st", [P, 8, TILES])
        xT = sb("xT", [P, WINDOW + SEQ])
        parts_a2 = xflat[:, 0:3 * SEQ // 2].bitcast(BF16).rearrange("p (s n) -> p s n", s=3)
        parts = big1[:, 6:8, :].rearrange("p a n -> p (a n)")[:, 0:3 * SEQ // 2].bitcast(BF16).rearrange(
            "p (s n) -> p s n", s=3)
        qT = big1[:].rearrange("p a n -> p (a n)").rearrange("p (c a t) -> p c a t", a=PAIRS, t=CHUNK)
        sq = big2[:].rearrange("p a n -> p (a n)").rearrange("p (c a t) -> p c a t", a=PAIRS, t=CHUNK)
        oT = big2
        work = sb("work", [P, 4 * HALF])
        rest = work[:, 0:2 * HALF].rearrange("p (w n) -> p w n", w=2)
        prod = work[:].rearrange("p (a c n) -> p a c n", a=2, c=2)
        probs = work[:, 0:3 * NQ * SPAN].rearrange("p (a q k) -> p a q k", a=3, q=NQ)
        rq = sb("rq", [P, CHUNKS, 2, 2])
        rqflat = rq[:].rearrange("p c a e -> p (c a e)")
        kT = sb("kT", [P, 2, WINDOW + SEQ])
        rk = sb("rk", [P, TILES])
        vwin = sb("vwin", [P, CHUNKS + 1, D])
        xn = vwin[:, 0:2 * TILES, :].rearrange("p (i a) d -> p i a d", a=2)
        vrem = sb("vrem", [P, CHUNKS, D])
        tmp, moe = vrem[:, 0:TILES, :], vrem[:, TILES:2 * TILES, :]
        turned = sb("turned", [P, 2 * HALF])
        pT = turned[:].rearrange("p (a q r) -> p a q r", a=2, q=NQ)
        yw = turned[:].rearrange("p (a e d) -> p a e d", a=2, e=E)
        k_turned = vrem[:, 0:SEQ // D, :].rearrange("p c d -> p (c d)")
        tokensT = turned[:, 0:HALF]
        k_squares = turned[:]
        diag = turned[:]
        pTr_own = sb("pTr_own", [P, 4, P])
        pTr, own = pTr_own[:, 0:2, :], pTr_own[:, 2:4, :]
        newton = pTr_own
        small = sb("small", [P, 4, 4, NQ])
        lg = sb("lg", [P, 8, TILES, E])
        comb = sb("comb", [P, TILES, E])
        combT = sb("combT", [TILES * E, P])
        hT = big2[:].rearrange("p a b -> p (a b)")

        res = sb("res", [P, ALLT, D])
        hl = sb("hl", [P, ALLT, D])
        base = sb("base", [P, E])
        mean_row, var_row = sb("mean_row", [P, D]), sb("var_row", [P, D])
        first_sem = sem("const_loaded")
        sems = {n: sem(n) for n in [
            "set_ready", "w_loaded", "x_loaded", "high_done", "rest_done", "low_done", "tok_done", "h_ready", "dve_chain", "cos_done", "q_root", "k_root", "xn_ready", "xT_psum",
            "xT_act", "xT_dve", "proj_done", "square_done", "prod_done", "rot_done", "ssq_done", "v_psum", "v_act",
            "v_dve", "kprod", "scores_done", "bias_ready", "exp_done", "scaled", "transposed",
            "pT_ready", "pTr_ready", "pv_done", "oT_ready", "wo_done", "last"]}
        S = sems
        clear = range(first_sem.num, S["last"].num + 1)

        def stage(build):
            with nc.Block() as block:
                build(block)
            nc.all_engine_barrier(sems_to_clear=clear)

        def bc(ap, n):
            return ap.unsqueeze(2).to_broadcast([ap.shape[0], ap.shape[1], n])

        def rows(ap, n):
            return ap.unsqueeze(1).to_broadcast([ap.shape[0], n, ap.shape[1]])

        def layernorm(v, ch, src, dst, diff, work, stat, tiles):
            ch.step(v.tensor_reduce(stat[:, 0, :tiles], src, X, ALU.add))
            ch.step(v.tensor_scalar(stat[:, 1, :tiles], stat[:, 0, :tiles], 1.0 / D, None, ALU.mult))
            ch.step(v.tensor_tensor(diff, src, bc(stat[:, 1, :tiles], D), ALU.subtract))
            ch.step(v.tensor_tensor(work, diff, diff, ALU.mult))
            ch.step(v.tensor_reduce(stat[:, 2, :tiles], work, X, ALU.add))
            ch.step(v.tensor_scalar(stat[:, 3, :tiles], stat[:, 2, :tiles], 1.0 / D, LN_EPS, ALU.mult, ALU.add))
            one_over_root(v, ch, stat[:, 4, :tiles], stat[:, 3, :tiles])
            ch.step(v.tensor_tensor(dst, diff.unsqueeze(2).to_broadcast([P, tiles, 2, D]),
                                    stat[:, 4, :tiles].unsqueeze(2).unsqueeze(3).to_broadcast([P, tiles, 2, D]),
                                    ALU.mult))

        def one_over_root(v, ch, dst, x):
            n = x.shape[1]
            half, y, t = (newton[:, k, 0:n] for k in range(3))
            ch.step(v.tensor_scalar(half.bitcast(I32), x.bitcast(I32), 1, None, ALU.logical_shift_right))
            ch.step(v.tensor_scalar(y.bitcast(I32), half.bitcast(I32), -1.0, float(0x5F3759DF), ALU.mult, ALU.add))
            for k in range(3):
                ch.step(v.tensor_tensor(t, y, y, ALU.mult))
                ch.step(v.scalar_tensor_tensor(out=t, in0=t, scalar=-0.5, in1=x, op0=ALU.mult, op1=ALU.mult))
                ch.step(v.scalar_tensor_tensor(out=dst if k == 2 else y, in0=t, scalar=1.5, in1=y, op0=ALU.add,
                                               op1=ALU.mult))

        def split_weights(v, ch, w, part_a, part_c, high, low, rest):
            ch.step(v.tensor_copy(high, w))
            ch.step(v.tensor_tensor(rest, w, high, ALU.subtract))
            ch.step(v.tensor_copy(low, rest))
            v.tensor_copy(part_a[0:D], high[0:D])
            v.tensor_copy(part_a[D:P], low[D:P])
            v.tensor_copy(part_c[D:P], high[D:P])
            ch.step(v.tensor_tensor(part_c[0:D], rest[0:D], low[0:D], ALU.subtract))

        def split_product(out_ap, cols, part_a, part_c, xs, start=True):
            for k, w in ((0, part_a), (1, part_a), (2, part_c)):
                ins = nc.tensor.matmul(out_ap, w[:, cols], xs[:, k, :], start=(k == 0), stop=(k == 2))
            return ins

        def split_scalar(a, banks, xs):
            for w in range(2):
                a.wait_ge(S["xT_psum"], w + 1)
                nc.scalar.activation(xs[:, 0, w * HALF:(w + 1) * HALF], bank[banks[w]][:],
                                     ACT.Copy).then_inc(S["high_done"], 1)
            for w in range(2):
                a.wait_ge(S["rest_done"], w + 1)
                nc.scalar.activation(xs[:, 1, w * HALF:(w + 1) * HALF], rest[:, w, :], ACT.Copy).then_inc(S["low_done"], 1)
                nc.scalar.activation(xT[:, WINDOW + w * HALF:WINDOW + (w + 1) * HALF], bank[banks[w]][:], ACT.Copy)

        def split_vector(v, banks, xs):
            for w in range(2):
                cols = slice(w * HALF, (w + 1) * HALF)
                v.wait_ge(S["high_done"], w + 1)
                v.tensor_tensor(rest[:, w, :], bank[banks[w]][:], xs[:, 0, cols],
                                ALU.subtract).then_inc(S["rest_done"], 1)
                v.tensor_copy(xs[0:D, 2, cols], xs[0:D, 0, cols])
            for w in range(2):
                cols = slice(w * HALF, (w + 1) * HALF)
                v.wait_ge(S["low_done"], w + 1)
                v.tensor_tensor(xs[D:P, 2, cols], rest[D:P, w, :], xs[D:P, 1, cols], ALU.subtract)

        def transpose_tiles(pe, src, tiles, banks):
            for i in range(tiles):
                twice = src[:, i].rearrange("p a d -> p (a d)")
                ins = nc.tensor.transpose(bank[banks[i // 4]][:, (i % 4) * P:(i % 4 + 1) * P], twice, ident[:])
                if i % 4 == 3:
                    ins.then_inc(S["xT_psum"], 1)

        def setup(block):
            @block.sync
            def _(sp):
                n = 0
                sp.dma_start(sbuf["proj_w"], inp["proj_w"]).then_inc(S["w_loaded"], 16)
                for k in loaded:
                    if k == "proj_w":
                        continue
                    sp.dma_start(sbuf[k] if k in aside else sbuf[k][:], inp[k]).then_inc(first_sem, 16)
                    n += 1
                for half in range(2):
                    r = slice(D * half, D * half + D)
                    for dst, src in ((qn, "q_norm"), (kn, "k_norm"), (bq, "bq1"), (bk, "bk1")):
                        sp.dma_start(dst[r, :], inp[src]).then_inc(first_sem, 16)
                        n += 1
                sp.dma_start(bvcol[:], inp["bv1"]).then_inc(first_sem, 16)
                n += 1
                for dst, src in ((blrow, "bl1"), (gammarow, "gamma"), (betarow, "beta"), (gate_b, "gate_b")):
                    sp.dma_start(dst[:], inp[src].to_broadcast([P, inp[src].shape[1]])).then_inc(first_sem, 16)
                    n += 1
                sp.wait_ge(S["set_ready"], 1)
                for i in range(TILES):
                    sp.dma_start(b2sel0[E * i:E * i + E, i, :], inp["moe_b2"]).then_inc(first_sem, 16)
                    n += 1
                load_x(sp, 0, first_sem)
                n += 1
                sp.wait_ge(first_sem, 16 * n)
                sp.sem_inc(S["x_loaded"], 1)

            @block.vector
            def _(v):
                ch = Chain(v, S["dve_chain"])
                ch.step(v.memset(b2sel0[:], 0.0))
                v.sem_inc(S["set_ready"], 1)
                v.memset(ones[:], 1.0)
                v.memset(ones_mean[:], 1.0 / (ALLT * P))
                v.memset(zeros[:], 0.0)
                v.memset(base[:], 0.0)
                v.memset(xT[:, 0:WINDOW], 0.0)
                v.memset(kT[:], 0.0)
                ch.step(v.memset(moe_w2[:], 0.0))
                v.wait_ge(S["w_loaded"], 16)
                n = PROJ // 2
                scratch = big2[:, 2:6, :].rearrange("p a n -> p (a n)")
                for k in range(2):
                    cols = slice(k * n, k * n + n)
                    split_weights(v, ch, sbuf["proj_w"][:, cols], w_a[:, cols], w_c[:, cols],
                                  scratch[:, 0:n // 2].bitcast(BF16), scratch[:, n // 2:n].bitcast(BF16),
                                  scratch[:, n:2 * n])
                v.wait_ge(S["x_loaded"], 1)
                for r in range(2):
                    v.tensor_copy(moe_w2[D * r:D * r + D, :, D * r:D * r + D], sbuf["moe_w2"][D * r:D * r + D])
                v.tensor_copy(row_of_t[:], sbuf["row_of_t"])
                v.tensor_copy(window_mask[:], sbuf["window_mask"])
                ch.step(v.tensor_scalar(wqk[:], qn[:], kn[:, 0:1], float(np.sqrt(D)), ALU.mult, ALU.mult))
                ch.step(v.tensor_scalar(bvrep[:], zeros[0:D, :], bvcol[:, 0:1], None, ALU.add))
                v.sem_inc(S["h_ready"], 1)
                v.wait_ge(S["tok_done"], 1)
                v.tensor_copy(weff[:], bank[0][:].rearrange("p (o r) -> p r o", r=STRIDE))
                v.wait_ge(S["proj_done"], 1)
                v.tensor_tensor(vbias[:], bank[1][:, 0:D], blrow[:], ALU.add)
                ch.step(v.tensor_copy(wvl[:], bank[1][0:D, D:2 * D]))

            @block.tensor
            def _(pe):
                pe.wait_ge(S["x_loaded"], 1)
                w = sbuf["tok_w"]
                for o in range(D):
                    for j in range(2):
                        ins = nc.tensor.matmul(bank[0][D * j:D * j + D, o * STRIDE:(o + 1) * STRIDE], w[:, o, :],
                                               sbuf["dft"][:, j * STRIDE:(j + 1) * STRIDE], start=True, stop=True)
                ins.then_inc(S["tok_done"], 1)
                pe.wait_ge(S["h_ready"], 1)
                nc.tensor.matmul(bank[1][:, 0:D], bvrep[:], sbuf["wl1"][:], start=True, stop=True)
                nc.tensor.matmul(bank[1][0:D, D:2 * D], sbuf["wvT1"][:], sbuf["wl1"][:], start=True,
                                 stop=True).then_inc(S["proj_done"], 1)

        def load_x(sp, b, s):
            sp.dma_start(xb[:], inp["x"][bass.ds(b, 1)].rearrange("b p v t -> (b p) v t")).then_inc(s, 16)

        def tokens(block):
            @block.tensor
            def _(pe):
                steps = xflat.rearrange("p (s r) -> p r s", r=STRIDE)
                for r in range(STRIDE):
                    for w in range(2):
                        ins = nc.tensor.matmul(bank[0][D * w:D * w + D, :], weff[:, r, :],
                                               steps[:, r, w * HALF:(w + 1) * HALF], start=(r == 0), stop=(r == STRIDE - 1))
                ins.then_inc(S["proj_done"], 1)
                pe.wait_ge(S["v_act"], 1)
                for j in range(TILES // 2):
                    ins = nc.tensor.transpose(bank[3][:, P * j:P * j + P], tokensT[:, P * j:P * j + P], ident[:])
                ins.then_inc(S["tok_done"], 1)
                pe.wait_ge(S["xn_ready"], 1)
                transpose_tiles(pe, xn, TILES, [1, 2])

            @block.scalar
            def _(a):
                a.wait_ge(S["proj_done"], 1)
                nc.scalar.activation(tokensT, bank[0][:], ACT.Copy).then_inc(S["v_act"], 1)
                a.wait_ge(S["tok_done"], 1)
                nc.scalar.activation(h[:].rearrange("p (w j) d -> p j w d", w=2),
                                     bank[3][:].rearrange("p (j w d) -> p j w d", w=2, d=D), ACT.Copy).then_inc(S["h_ready"], 1)
                split_scalar(a, (1, 2), parts_a2)

            @block.vector
            def _(v):
                ch = Chain(v, S["dve_chain"])
                v.wait_ge(S["h_ready"], 1)
                layernorm(v, ch, h[:], xn, tmp, moe, st, TILES)
                v.sem_inc(S["xn_ready"], 1)
                split_vector(v, (1, 2), parts_a2)

        UNITS = 2 * (PAIRS + 1)

        def unit(u):
            if u < 2:
                return PAIRS, u
            group, i = divmod(u - 2, 4)
            return 4 * (group % 2) + i, group // 2

        SIDE = (2, 3, 4, 5, 6, 7, 9, 10, 11, 12, 13, 14)

        def project(block):
            @block.tensor
            def _(pe):
                def k_sums():
                    pe.wait_ge(S["square_done"], 2)
                    for i in range(TILES):
                        ins = nc.tensor.matmul(bank[7][:, i:i + 1], k_squares[:, P * i:P * i + P],
                                               sbuf["by_head"][:, 0:1], start=True, stop=True)
                    ins.then_inc(S["v_psum"], 1)

                def value_windows(n):
                    if n == 0:
                        pe.wait_ge(S["v_dve"], 1)
                    else:
                        pe.wait_ge(S["v_act"], n)
                    for m in range(8 if n < 4 else 1):
                        c = 8 * n + m
                        ins = nc.tensor.matmul(bank[7][:, D * m:D * m + D], xT[0:D, CHUNK * c:CHUNK * c + P],
                                               sbuf["wv0"][:], start=True, stop=True)
                    ins.then_inc(S["v_psum"], 1)

                def k_norms(w):
                    if w == 0:
                        pe.wait_ge(S["v_act"], 5)
                        pe.wait_ge(S["k_root"], 1)
                    else:
                        pe.wait_ge(S["v_dve"], 2)
                    nc.tensor.matmul(bank[7][:], ones[:], diag[:, w * HALF:(w + 1) * HALF], start=True,
                                     stop=True).then_inc(S["v_psum"], 1)

                def value_copies(m):
                    if m == 0:
                        pe.wait_ge(S["v_dve"], 3)
                    else:
                        pe.wait_ge(S["v_act"], 5 + m)
                    nc.tensor.matmul(bank[7][:], sbuf["copies"][:, m, :], vwin[:, NQ:CHUNKS + 1:NQ, :], start=True,
                                     stop=True).then_inc(S["v_psum"], 1)

                def q_sums(group, i):
                    w, hh = divmod(group, 2)
                    for c in range(w * CHUNKS // 2 + 4 * i, w * CHUNKS // 2 + 4 * i + 4):
                        ins = nc.tensor.matmul(bank[6][:, 4 * c + 2 * hh:4 * c + 2 * hh + 2],
                                               sq[:, c, 4 * hh:4 * hh + 4, :].rearrange("p a t -> p (a t)"),
                                               sbuf["by_head"][:], start=True, stop=True)
                    return ins

                for u in range(UNITS + 4):
                    if u < UNITS:
                        pair, w = unit(u)
                        if u >= 3:
                            pe.wait_ge(S["prod_done"], u - 2)
                            pe.wait_ge(S["square_done"], u - 2)
                        for c in range(2):
                            cols = slice((2 * pair + c) * P, (2 * pair + c) * P + P)
                            ins = split_product(bank[2 * (u % 3) + c][:], cols, w_a, w_c,
                                                parts_a2[:, :, w * HALF:(w + 1) * HALF])
                        ins.then_inc(S["proj_done"], 1)
                    if u == SIDE[0]:
                        k_sums()
                    if SIDE[1] <= u <= SIDE[5]:
                        value_windows(u - SIDE[1])
                    if SIDE[6] <= u <= SIDE[7]:
                        k_norms(u - SIDE[6])
                    if SIDE[8] <= u <= SIDE[11]:
                        value_copies(u - SIDE[8])
                    if u >= 6:
                        group, i = divmod(u - 6, 4)
                        if i == 0:
                            pe.wait_ge(S["square_done"], 6 + 4 * group)
                        ins = q_sums(group, i)
                ins.then_inc(S["ssq_done"], 1)

            @block.scalar
            def _(a):
                for u in range(UNITS):
                    pair, w = unit(u)
                    a.wait_ge(S["cos_done"], u + 1)
                    dst = (sq[:, w * CHUNKS // 2:(w + 1) * CHUNKS // 2, pair, :] if pair < PAIRS
                           else k_squares[:, w * HALF:(w + 1) * HALF])
                    src = bank[2 * (u % 3)][:]
                    if pair < PAIRS:
                        src = src.rearrange("p (c t) -> p c t", t=CHUNK)
                    nc.scalar.activation(dst, src, ACT.Square).then_inc(S["square_done"], 1)
                    if SIDE[1] <= u <= SIDE[5]:
                        n = u - SIDE[1]
                        a.wait_ge(S["v_psum"], n + 2)
                        last = min(8 * n + 8, CHUNKS + 1)
                        nc.scalar.activation(vwin[:, 8 * n:last, :].rearrange("p c d -> p (c d)"),
                                             bank[7][:, 0:D * (last - 8 * n)], ACT.Copy).then_inc(S["v_act"], 1)
                    if SIDE[8] <= u <= SIDE[11]:
                        m = u - SIDE[8]
                        a.wait_ge(S["v_psum"], m + 9)
                        nc.scalar.activation(vrem[:, m::NQ, :], bank[7][:].rearrange("p (c d) -> p c d", d=D),
                                             ACT.Copy).then_inc(S["v_act"], 1)

            @block.vector
            def _(v):
                ch = Chain(v, S["dve_chain"])
                for u in range(UNITS):
                    pair, w = unit(u)
                    cols = slice(w * HALF, (w + 1) * HALF)
                    v.wait_ge(S["proj_done"], u + 1)
                    if u >= 2:
                        v.wait_ge(S["rot_done"], u - 1)
                    v.tensor_tensor(prod[:, u % 2, 0, :], bank[2 * (u % 3)][:], sbuf["rope_cos"][:, cols],
                                    ALU.mult).then_inc(S["cos_done"], 1)
                    v.tensor_tensor(prod[:, u % 2, 1, :], bank[2 * (u % 3) + 1][:], sbuf["rope_sin"][:, cols],
                                    ALU.mult).then_inc(S["prod_done"], 1)
                    if u == SIDE[0]:
                        v.wait_ge(S["v_psum"], 1)
                        ch.step(v.tensor_scalar(rk[:], bank[7][:, 0:TILES], D * RMS_EPS, None, ALU.add))
                        v.sem_inc(S["v_dve"], 1)
                        one_over_root(v, ch, rk[:], rk[:])
                        v.tensor_tensor(diag[:].rearrange("p (i k) -> p i k", k=P), rows(ident[:], TILES), bc(rk[:], P),
                                        ALU.mult).then_inc(S["k_root"], 1)
                    if SIDE[6] <= u <= SIDE[7]:
                        w = u - SIDE[6]
                        v.wait_ge(S["v_psum"], w + 7)
                        for e in range(2):
                            r = slice(D * e, D * e + D)
                            ins = v.scalar_tensor_tensor(out=kT[r, e, WINDOW + w * HALF:WINDOW + (w + 1) * HALF],
                                                         in0=k_turned[r, w * HALF:(w + 1) * HALF], scalar=wqk[r, 0:1],
                                                         in1=bank[7][r, :], op0=ALU.mult, op1=ALU.mult)
                        ins.then_inc(S["v_dve"], 1)
                v.wait_ge(S["ssq_done"], 1)
                ch.step(v.tensor_scalar(rqflat, bank[6][:, 0:NQ * CHUNKS], D * RMS_EPS, None, ALU.add))
                one_over_root(v, ch, rqflat, rqflat)

            @block.gpsimd
            def _(g):
                for u in range(UNITS):
                    pair, w = unit(u)
                    g.wait_ge(S["prod_done"], u + 1)
                    dst, first, second = k_turned[:, w * HALF:(w + 1) * HALF], prod[:, u % 2, 0, :], prod[:, u % 2, 1, :]
                    if pair < PAIRS:
                        dst = qT[:, w * CHUNKS // 2:(w + 1) * CHUNKS // 2, pair, :]
                        first, second = (z.rearrange("p (c t) -> p c t", t=CHUNK) for z in (first, second))
                    g.tensor_tensor(dst, first, second, ALU.add).then_inc(S["rot_done"], 1)

        def windowed(block, b):
            def s_bank(c, half):
                return bank[2 * (c % 2) + half]

            @block.sync
            def _(sp):
                load_x(sp, b, S["x_loaded"])
                sp.wait_ge(S["x_loaded"], 16)

            @block.tensor
            def _(pe):
                def scores(c):
                    if c >= 2:
                        pe.wait_ge(S["exp_done"], NQ * (c - 1))
                    variant = min(c, EARLY)
                    for hh in range(2):
                        tiles = s_bank(c, hh)[:, 0:2 * SPAN].rearrange("p (e k) -> p e k", e=2)
                        if c < EARLY:
                            mask, masked = rows(window_mask[:, variant, :], 2), tiles
                        else:
                            mask = window_mask[:, variant].rearrange("p (g k) -> p g k", k=CHUNK)[:, ::SPAN // CHUNK - 1, :]
                            mask = mask.unsqueeze(1).to_broadcast([CHUNK, 2, 2, CHUNK])
                            masked = tiles.rearrange("p e (g k) -> p e g k", k=CHUNK)[:, :, ::SPAN // CHUNK - 1, :]
                        nc.tensor.matmul(masked, row_of_t[:], mask, start=True, stop=True, skip_group_check=True)
                        ins = nc.tensor.matmul(tiles, qT[:, c, 4 * hh:4 * hh + 4, :].rearrange("p a t -> p (a t)"),
                                               kT[:, :, CHUNK * c:CHUNK * c + SPAN], start=False, stop=True,
                                               skip_group_check=True)
                    ins.then_inc(S["scores_done"], 1)

                def turn(c):
                    pe.wait_ge(S["scaled"], c + 1)
                    if c >= 2:
                        pe.wait_ge(S["pT_ready"], c - 1)
                        pe.wait_ge(S["pTr_ready"], c - 1)
                    for q in range(NQ):
                        nc.tensor.transpose(bank[4 + c % 2][:, P * q:P * q + P], probs[:, c % 3, q, 0:P], ident[:])
                    nc.tensor.transpose(bank[6 + c % 2][:, 0:P], own[:, c % 2, :],
                                        ident[:]).then_inc(S["transposed"], 1)

                def values(c):
                    pe.wait_ge(S["pT_ready"], c + 1)
                    pe.wait_ge(S["pTr_ready"], c + 1)
                    if c >= 2:
                        pe.wait_ge(S["oT_ready"], c - 1)
                    pe.wait_ge(S["exp_done"], NQ * min(c + 3, CHUNKS))
                    for own_keys in range(2):
                        for hh in range(2):
                            for e in range(2):
                                q = 2 * hh + e
                                o = s_bank(c, hh)[D * e:D * e + D, 2 * SPAN:2 * SPAN + P]
                                r = slice(CHUNK * q, CHUNK * q + CHUNK)
                                if own_keys:
                                    ins = nc.tensor.matmul(o, vrem[r, c, :], pTr[r, c % 2, :], start=False, stop=True,
                                                           tile_position=(CHUNK * q, D * e), skip_group_check=True)
                                else:
                                    nc.tensor.matmul(o, vwin[:, c, :], pT[:, c % 2, q, :], start=True, stop=True,
                                                     skip_group_check=True)
                    ins.then_inc(S["pv_done"], 1)

                for n in range(CHUNKS + 4):
                    if n >= 4:
                        values(n - 4)
                    if n < CHUNKS:
                        scores(n)
                    if 2 <= n < CHUNKS + 2:
                        turn(n - 2)
                pe.wait_ge(S["oT_ready"], CHUNKS)
                for i in range(TILES):
                    for p in range(PAIRS):
                        ins = nc.tensor.matmul(bank[0][:, D * i:D * i + D], oT[:, p, P * i:P * i + P],
                                               sbuf["wo0"][:, p, :], start=(p == 0), stop=(p == PAIRS - 1))
                ins.then_inc(S["wo_done"], 1)
                pe.wait_ge(S["xn_ready"], 1)
                transpose_tiles(pe, xn, TILES, [1, 2])

            @block.vector
            def _(v):
                ch = Chain(v, S["dve_chain"])
                for n in range(CHUNKS + 2):
                    c = n
                    if c < CHUNKS:
                        v.wait_ge(S["scores_done"], c + 1)
                        for e in range(2):
                            ins = v.tensor_reduce(small[:, c % 4, 0, 2 * e:2 * e + 2],
                                                  s_bank(c, e)[:, 0:2 * SPAN].rearrange("p (a k) -> p a k", a=2),
                                                  X, ALU.max)
                        ch.step(ins)
                        v.scalar_tensor_tensor(out=small[:, c % 4, 1, :], in0=small[:, c % 4, 0, :], scalar=-1.0,
                                               in1=rq[:, c].rearrange("p a e -> p (a e)"), op0=ALU.mult, op1=ALU.mult).then_inc(S["bias_ready"], 1)
                    c = n - 1
                    if 0 <= c < CHUNKS:
                        v.wait_ge(S["exp_done"], NQ * (c + 1))
                        ch.step(v.reciprocal(small[:, c % 4, 3, :], small[:, c % 4, 2, :]))
                        if c >= 2:
                            v.wait_ge(S["transposed"], c - 1)
                        for q in range(NQ):
                            v.tensor_scalar(probs[:, c % 3, q, 0:P], probs[:, c % 3, q, 0:P], small[:, c % 4, 3, q:q + 1],
                                            None, ALU.mult)
                        v.tensor_tensor(own[:, c % 2, :].rearrange("p (q k) -> p q k", q=NQ), probs[:, c % 3, :, P:SPAN],
                                        bc(small[:, c % 4, 3, :], CHUNK), ALU.mult).then_inc(S["scaled"], 1)
                    c = n - 2
                    if c >= 0:
                        v.wait_ge(S["transposed"], c + 1)
                        if c >= 2:
                            v.wait_ge(S["pv_done"], c - 1)
                        v.tensor_copy(pT[:, c % 2, :, :].rearrange("p q r -> p (q r)"),
                                      bank[4 + c % 2][:]).then_inc(S["pT_ready"], 1)
                v.wait_ge(S["wo_done"], 1)
                ch.step(v.tensor_tensor(h[:].rearrange("p i d -> p (i d)"), h[:].rearrange("p i d -> p (i d)"),
                                        bank[0][:], ALU.add))
                layernorm(v, ch, h[:], xn, tmp, moe, st, TILES)
                v.sem_inc(S["xn_ready"], 1)
                split_vector(v, (1, 2), parts)

            @block.scalar
            def _(a):
                for n in range(CHUNKS + 4):
                    c = n
                    if c < CHUNKS:
                        a.wait_ge(S["bias_ready"], c + 1)
                        if c >= 3:
                            a.wait_ge(S["transposed"], c - 2)
                        for q in range(NQ):
                            nc.scalar.activation(probs[:, c % 3, q, :],
                                                 s_bank(c, q // 2)[:, SPAN * (q % 2):SPAN * (q % 2) + SPAN], ACT.Exp,
                                                 bias=small[:, c % 4, 1, q:q + 1], scale=rq[:, c, q // 2, q % 2:q % 2 + 1],
                                                 accum_out=small[:, c % 4, 2, q:q + 1]).then_inc(S["exp_done"], 1)
                    c = n - 2
                    if 0 <= c < CHUNKS:
                        a.wait_ge(S["transposed"], c + 1)
                        if c >= 2:
                            a.wait_ge(S["pv_done"], c - 1)
                        nc.scalar.activation(pTr[:, c % 2, :], bank[6 + c % 2][:, 0:P],
                                             ACT.Copy).then_inc(S["pTr_ready"], 1)
                    c = n - 4
                    if c >= 0:
                        a.wait_ge(S["pv_done"], c + 1)
                        for hh in range(2):
                            ins = nc.scalar.activation(
                                oT[:, 4 * hh:4 * hh + 4, CHUNK * c:CHUNK * (c + 1)],
                                s_bank(c, hh)[:, 2 * SPAN:2 * SPAN + P].rearrange("p (a t) -> p a t", t=CHUNK),
                                ACT.Copy)
                        ins.then_inc(S["oT_ready"], 1)
                split_scalar(a, (1, 2), parts)

        def first_argmax(v, ch, p, top, cand, best, hot, tiles):
            ch.step(v.tensor_reduce(top, p, X, ALU.max))
            ch.step(v.tensor_tensor(cand, p, bc(top, E), ALU.is_ge))
            ch.step(v.tensor_tensor(cand, cand, rows(sbuf["first_weight"][:], tiles), ALU.mult))
            ch.step(v.tensor_reduce(best, cand, X, ALU.max))
            ch.step(v.tensor_tensor(hot, cand, bc(best, E), ALU.is_equal))

        def experts(block, b):
            @block.tensor
            def _(pe):
                for i in range(TILES):
                    ins = nc.tensor.matmul(bank[7][:, E * i:E * i + E], xT[0:D, WINDOW + P * i:WINDOW + P * i + P],
                                           sbuf["router"][:], start=True, stop=True)
                ins.then_inc(S["tok_done"], 1)
                for u in range(8):
                    k, w = divmod(u, 2)
                    if u >= 4:
                        pe.wait_ge(S["exp_done"], u - 3 + 1)
                    split_product(bank[u % 4][:], slice(MOE_COLS + P * k, MOE_COLS + P * k + P), w_a, w_c,
                                  parts[:, :, w * HALF:(w + 1) * HALF]).then_inc(S["proj_done"], 1)
                pe.wait_ge(S["bias_ready"], 1)
                nc.tensor.transpose(bank[6][0:TILES * E, 0:P], comb[:].rearrange("p i e -> p (i e)"),
                                    ident[:]).then_inc(S["transposed"], 1)
                pe.wait_ge(S["exp_done"], 9)
                pe.wait_ge(S["pT_ready"], 1)
                for i in range(TILES):
                    if i >= 2:
                        pe.wait_ge(S["prod_done"], i - 1)
                    for k in range(E // 2):
                        nc.tensor.matmul(bank[i % 2][:, P * k:P * k + P], hT[:, SEQ * k + P * i:SEQ * k + P * i + P],
                                         moe_w2[:, k, :], start=True, stop=True)
                    nc.tensor.matmul(bank[5][:, D * i:D * i + D], combT[:], b2sel0[:, i, :], start=True,
                                     stop=True).then_inc(S["pv_done"], 1)
                pe.wait_ge(S["xn_ready"], 1)
                transpose_tiles(pe, xn, TILES, [6, 4])

            @block.scalar
            def _(a):
                a.wait_ge(S["h_ready"], 1)
                nc.scalar.activation(lg[:, 1], lg[:, 0], ACT.Exp).then_inc(S["exp_done"], 1)
                for u in range(8):
                    k, w = divmod(u, 2)
                    a.wait_ge(S["proj_done"], u + 1)
                    nc.scalar.activation(hT[:, SEQ * k + w * HALF:SEQ * k + (w + 1) * HALF], bank[u % 4][:], ACT.Gelu,
                                         bias=sbuf["moe_b1"][:, k:k + 1]).then_inc(S["exp_done"], 1)
                split_scalar(a, (6, 4), parts)

            @block.vector
            def _(v):
                ch = Chain(v, S["dve_chain"])
                v.wait_ge(S["tok_done"], 1)
                logits = bank[7][:, 0:TILES * E].rearrange("p (i e) -> p i e", e=E)
                ch.step(v.tensor_reduce(st[:, 0, :], logits, X, ALU.max))
                ch.step(v.tensor_tensor(lg[:, 0], logits, bc(st[:, 0, :], E), ALU.subtract))
                v.sem_inc(S["h_ready"], 1)
                v.wait_ge(S["exp_done"], 1)
                ch.step(v.tensor_reduce(st[:, 1, :], lg[:, 1], X, ALU.add))
                ch.step(v.reciprocal(st[:, 2, :], st[:, 1, :]))
                ch.step(v.tensor_tensor(lg[:, 2], lg[:, 1], bc(st[:, 2, :], E), ALU.mult))
                first_argmax(v, ch, lg[:, 2], st[:, 3, :], lg[:, 3], st[:, 4, :], lg[:, 4], TILES)
                ch.step(v.scalar_tensor_tensor(out=lg[:, 5], in0=lg[:, 4], scalar=-2.0, in1=lg[:, 2], op0=ALU.mult,
                                               op1=ALU.add))
                first_argmax(v, ch, lg[:, 5], st[:, 5, :], lg[:, 3], st[:, 4, :], lg[:, 6], TILES)
                ch.step(v.tensor_tensor(st[:, 6, :], st[:, 3, :], st[:, 5, :], ALU.add))
                ch.step(v.tensor_scalar(st[:, 7, :], st[:, 6, :], 1e-12, None, ALU.max))
                ch.step(v.reciprocal(st[:, 6, :], st[:, 7, :]))
                ch.step(v.tensor_tensor(lg[:, 7], lg[:, 4], lg[:, 6], ALU.add))
                ch.step(v.tensor_tensor(lg[:, 7], lg[:, 7], lg[:, 2], ALU.mult))
                ch.step(v.tensor_tensor(comb[:], lg[:, 7], bc(st[:, 6, :], E), ALU.mult))
                v.sem_inc(S["bias_ready"], 1)
                v.wait_ge(S["transposed"], 1)
                v.tensor_copy(combT[:], bank[6][0:TILES * E, 0:P]).then_inc(S["pT_ready"], 1)
                for i in range(TILES):
                    v.wait_ge(S["pv_done"], i + 1)
                    v.tensor_tensor(yw[:, i % 2], bank[i % 2][:].rearrange("p (e d) -> p e d", d=D),
                                    bc(comb[:, i, :], D), ALU.mult).then_inc(S["prod_done"], 1)
                    v.wait_ge(S["prod_done"], i + 1)
                    ins = v.tensor_reduce(moe[:, i, :], yw[:, i % 2].rearrange("p e d -> p d e"), X, ALU.add)
                ch.step(ins)
                mflat = moe.rearrange("p i d -> p (i d)")
                ch.step(v.tensor_tensor(mflat, mflat, bank[5][:], ALU.add))
                ch.step(v.tensor_tensor(moe, moe, xn[:, :, 0, :], ALU.add))
                ch.step(v.tensor_tensor(h[:], h[:], moe, ALU.add))
                layernorm(v, ch, h[:], xn, tmp, moe, st, TILES)
                v.sem_inc(S["xn_ready"], 1)
                v.tensor_tensor(res[:, bass.ds(b * TILES, TILES), :], h[:], xn[:, :, 0, :], ALU.add)
                split_vector(v, (6, 4), parts)

        qT1 = big1[:, 0, :]
        kT1 = big1[:, 1, :]
        v1 = big1[:, 2, 0:HALF].rearrange("p (i d) -> p i d", d=D)
        p1 = big2[:, 0:2, :]
        pT1 = big2[:, 2:4, :]

        def full(block, b):
            @block.tensor
            def _(pe):
                for n, first in enumerate((Q1_COLS, K1_COLS)):
                    for w in range(2):
                        ins = split_product(bank[2 * n + w][:], slice(first, first + P), w_a, w_c,
                                            parts[:, :, w * HALF:(w + 1) * HALF])
                    ins.then_inc(S["proj_done"], 1)
                for i in range(TILES):
                    ins = nc.tensor.matmul(bank[4][:, D * i:D * i + D], xT[0:D, WINDOW + P * i:WINDOW + P * i + P],
                                           wvl[:], start=True, stop=True)
                ins.then_inc(S["proj_done"], 1)

                def scores(i):
                    if i == 0:
                        pe.wait_ge(S["h_ready"], 2)
                        pe.wait_ge(S["square_done"], 2)
                    if i >= 2:
                        pe.wait_ge(S["exp_done"], i - 1)
                    for w in range(2):
                        r = slice(D * w, D * w + D)
                        ins = nc.tensor.matmul(bank[2 * (i % 2) + w][:], qT1[r, P * i:P * i + P],
                                               kT1[r, w * HALF:(w + 1) * HALF], start=True, stop=True)
                    ins.then_inc(S["scores_done"], 1)

                def turn(i):
                    pe.wait_ge(S["exp_done"], i + 1)
                    if i == 0:
                        pe.wait_ge(S["v_act"], 1)
                    else:
                        pe.wait_ge(S["pT_ready"], i)
                        pe.wait_ge(S["pTr_ready"], i)
                    for k in range(8):
                        ins = nc.tensor.transpose(bank[4 + k // 4][:, P * (k % 4):P * (k % 4) + P],
                                                  p1[:, i % 2, P * k:P * k + P], ident[:])
                        if k % 4 == 3:
                            ins.then_inc(S["transposed"], 1)

                def values(i):
                    pe.wait_ge(S["pT_ready"], i + 1)
                    pe.wait_ge(S["pTr_ready"], i + 1)
                    if i >= 2:
                        pe.wait_ge(S["last"], i - 1)
                    for k in range(8):
                        ins = nc.tensor.matmul(bank[6 + i % 2][:, 0:D], pT1[:, i % 2, P * k:P * k + P], v1[:, k, :],
                                               start=(k == 0), stop=(k == 7))
                    ins.then_inc(S["pv_done"], 1)

                for n in range(TILES + 2):
                    if n < TILES:
                        scores(n)
                    if 1 <= n < TILES + 1:
                        turn(n - 1)
                    if n >= 2:
                        values(n - 2)

            @block.scalar
            def _(a):
                a.wait_ge(S["proj_done"], 1)
                for w in range(2):
                    nc.scalar.activation(qT1[:, w * HALF:(w + 1) * HALF], bank[w][:], ACT.Identity,
                                         bias=bq[:, 0:1]).then_inc(S["h_ready"], 1)
                a.wait_ge(S["proj_done"], 3)
                nc.scalar.activation(v1.rearrange("p i d -> p (i d)"), bank[4][:], ACT.Copy).then_inc(S["v_act"], 1)
                for n in range(TILES + 1):
                    if n < TILES:
                        a.wait_ge(S["bias_ready"], n + 1)
                        if n >= 2:
                            a.wait_ge(S["transposed"], 2 * n - 2)
                        for w in range(2):
                            ins = nc.scalar.activation(p1[:, n % 2, w * HALF:(w + 1) * HALF], bank[2 * (n % 2) + w][:],
                                                       ACT.Exp, bias=st[:, 1, n:n + 1], scale=1.0 / D,
                                                       accum_out=st[:, 2 + w, n:n + 1])
                        ins.then_inc(S["exp_done"], 1)
                    i = n - 1
                    if i >= 0:
                        a.wait_ge(S["transposed"], 2 * i + 1)
                        if i >= 2:
                            a.wait_ge(S["pv_done"], i - 1)
                        nc.scalar.activation(pT1[:, i % 2, 0:HALF], bank[4][:], ACT.Copy).then_inc(S["pTr_ready"], 1)

            @block.vector
            def _(v):
                ch = Chain(v, S["dve_chain"])
                v.wait_ge(S["proj_done"], 2)
                for w in range(2):
                    v.tensor_scalar(kT1[:, w * HALF:(w + 1) * HALF], bank[2 + w][:], bk[:, 0:1], None,
                                    ALU.add).then_inc(S["square_done"], 1)
                for n in range(TILES + 2):
                    if n < TILES:
                        v.wait_ge(S["scores_done"], n + 1)
                        for w in range(2):
                            ins = v.tensor_reduce(st[:, 4 + w, n:n + 1], bank[2 * (n % 2) + w][:], X, ALU.max)
                        ch.step(ins)
                        ch.step(v.tensor_tensor(st[:, 6, n:n + 1], st[:, 4, n:n + 1], st[:, 5, n:n + 1], ALU.max))
                        v.tensor_scalar(st[:, 1, n:n + 1], st[:, 6, n:n + 1], -1.0 / D, None,
                                        ALU.mult).then_inc(S["bias_ready"], 1)
                    i = n - 1
                    if 0 <= i < TILES:
                        v.wait_ge(S["transposed"], 2 * i + 2)
                        if i >= 2:
                            v.wait_ge(S["pv_done"], i - 1)
                        v.tensor_copy(pT1[:, i % 2, HALF:], bank[5][:]).then_inc(S["pT_ready"], 1)
                        ch.step(v.tensor_tensor(st[:, 7, i:i + 1], st[:, 2, i:i + 1], st[:, 3, i:i + 1], ALU.add))
                        ch.step(v.reciprocal(st[:, 0, i:i + 1], st[:, 7, i:i + 1]))
                    i = n - 2
                    if i >= 0:
                        v.wait_ge(S["pv_done"], i + 1)
                        v.scalar_tensor_tensor(out=hl_row(b, i), in0=bank[6 + i % 2][:, 0:D], scalar=st[:, 0, i:i + 1],
                                               in1=vbias[:], op0=ALU.mult, op1=ALU.add).then_inc(S["last"], 1)

        def hl_row(b, i):
            return hl[:, bass.ds(b * TILES + i, 1), :].rearrange("p a d -> p (a d)")

        def batchnorm(block):
            @block.sync
            def _(sp):
                sp.dma_start(ffn_w, inp["ffn_w"]).then_inc(S["w_loaded"], 16)
                for dst, k in ((ffn_w2, "ffn_w2"), (ffn_b1, "ffn_b1")):
                    sp.dma_start(dst, inp[k]).then_inc(S["x_loaded"], 16)
                sp.wait_ge(S["set_ready"], 1)
                for i in range(P // E):
                    sp.dma_start(b2sel1[E * i:E * i + E, i, :], inp["ffn_b2"]).then_inc(S["x_loaded"], 16)
                sp.wait_ge(S["x_loaded"], 16 * (2 + P // E))

            q4 = [slice(TILES * g, TILES * g + TILES) for g in range(IMAGES)]

            @block.tensor
            def _(pe):
                for step in range(2):
                    if step:
                        pe.wait_ge(S["square_done"], 1)
                    src = (hl, big1_tok)[step]
                    for g in range(IMAGES):
                        ins = nc.tensor.matmul(bank[step][:], ones_mean[:], src[:, q4[g], :], start=(g == 0),
                                               stop=(g == IMAGES - 1))
                    ins.then_inc(S["proj_done"], 1)

            @block.scalar
            def _(a):
                a.wait_ge(S["h_ready"], 1)
                nc.scalar.activation(big1_tok[:], hl[:], ACT.Square).then_inc(S["square_done"], 1)

            @block.vector
            def _(v):
                ch = Chain(v, S["dve_chain"])
                v.memset(b2sel1, 0.0).then_inc(S["set_ready"], 1)
                v.memset(ten_k[:, 0, :], 1e4)
                v.memset(ten_k[:, 1, :], -1e4)
                v.wait_ge(S["w_loaded"], 16)
                scratch = big2[:].rearrange("p a n -> p (a n)")
                split_weights(v, ch, ffn_w, ffn_a, ffn_c, scratch[:, 0:FFN_COLS // 2].bitcast(BF16),
                              scratch[:, FFN_COLS // 2:FFN_COLS].bitcast(BF16), scratch[:, FFN_COLS:2 * FFN_COLS])
                v.wait_ge(S["proj_done"], 1)
                ch.step(v.tensor_reduce(mean_row[:], bank[0][:].rearrange("p (i d) -> p d i", d=D), X, ALU.add))
                ch.step(v.tensor_tensor(hl[:], hl[:], rows(mean_row[:], ALLT), ALU.subtract))
                v.sem_inc(S["h_ready"], 1)
                v.wait_ge(S["proj_done"], 2)
                ch.step(v.tensor_reduce(var_row[:], bank[1][:].rearrange("p (i d) -> p d i", d=D), X, ALU.add))
                ch.step(v.tensor_scalar(var_row[:], var_row[:], BN_EPS, None, ALU.add))
                one_over_root(v, ch, mean_row[:], var_row[:])
                ch.step(v.tensor_copy(var_row[:], mean_row[:]))
                ch.step(v.tensor_tensor(var_row[:], var_row[:], gammarow[:], ALU.mult))
                ch.step(v.tensor_tensor(hl[:], hl[:], rows(var_row[:], ALLT), ALU.mult))
                ch.step(v.tensor_tensor(hl[:], hl[:], rows(betarow[:], ALLT), ALU.add))
                ch.step(v.scalar_tensor_tensor(out=res[:], in0=hl[:], scalar=0.0, in1=res[:], op0=ALU.max, op1=ALU.add))

        big1_tok = big1[:].rearrange("p a b -> p (a b)")[:, 0:ALLT * D].rearrange("p (i d) -> p i d", d=D)

        big1_flat, big2_flat = (z[:].rearrange("p a b -> p (a b)") for z in (big1, big2))
        everything = ALLT * P
        parts_all = big1_flat[:, 0:3 * everything // 2].bitcast(BF16).rearrange("p (s n) -> p s n", s=3)
        gatesT = big1_flat[:, 3 * everything // 2:3 * everything // 2 + 2 * P].rearrange("p (k n) -> p k n", k=2)
        squares = big2_flat[:, 0:ALLT * D].rearrange("p (i d) -> p i d", d=D)
        xn_all = big2_flat[:, ALLT * D:3 * ALLT * D].rearrange("p (i a d) -> p i a d", a=2, d=D)
        la = [big2_flat[:, 3 * ALLT * D + ALLT * E * k:3 * ALLT * D + ALLT * E * (k + 1)].rearrange(
            "p (i e) -> p i e", e=E) for k in range(8)]
        sa = [st_all[:, k, :] for k in range(8)]
        rests = work[:].rearrange("p (k n) -> p k n", k=4)
        B4 = ALLT // GROUP_TILES

        def route(block):
            @block.tensor
            def _(pe):
                for j in range(B4):
                    if j == 0:
                        pe.wait_ge(S["xn_ready"], 1)
                    if j >= 4:
                        pe.wait_ge(S["rest_done"], j - 3)
                    transpose_tiles(pe, xn_all[:, GROUP_TILES * j:GROUP_TILES * (j + 1)], GROUP_TILES, [j % 4])
                for i in range(ALLT):
                    if i % GROUP_TILES == 0:
                        pe.wait_ge(S["prod_done"], i // GROUP_TILES + 1)
                    for k, w in ((0, ffn_a), (1, ffn_a), (2, ffn_c)):
                        ins = nc.tensor.matmul(bank[7][:, E * i:E * i + E], parts_all[:, k, P * i:P * i + P],
                                               w[:, FCH * P:FFN_COLS], start=(k == 0), stop=(k == 2))
                ins.then_inc(S["tok_done"], 1)
                pe.wait_ge(S["bias_ready"], 1)
                chosen = la[4].rearrange("p i e -> p (i e)")
                nc.tensor.matmul(bank[6][:, 0:ALLT * E], lower[:], chosen, start=True, stop=True)
                nc.tensor.matmul(bank[6][:, ALLT * E:2 * ALLT * E], ones[:], chosen, start=True,
                                 stop=True).then_inc(S["ssq_done"], 1)
                pe.wait_ge(S["bias_ready"], 2)
                flat = gates.rearrange("p i e -> p (i e)")
                for k in range(2):
                    ins = nc.tensor.transpose(bank[5][:, P * k:P * k + P], flat[:, P * k:P * k + P], ident[:])
                ins.then_inc(S["transposed"], 1)
                pe.wait_ge(S["pT_ready"], 1)
                for i in range(ALLT):
                    k, m = divmod(i, P // E)
                    ins = nc.tensor.matmul(bank[i // 8][:, D * (i % 8):D * (i % 8) + D], gatesT[:, k, :],
                                           b2sel1[:, m, :], start=True, stop=True)
                    if i % 8 == 7:
                        ins.then_inc(S["pv_done"], 1)

            @block.scalar
            def _(a):
                for n in range(B4 + 1):
                    if n < B4:
                        a.wait_ge(S["xT_psum"], n + 1)
                        nc.scalar.activation(parts_all[:, 0, n * HALF:(n + 1) * HALF], bank[n % 4][:],
                                             ACT.Copy).then_inc(S["high_done"], 1)
                    j = n - 1
                    if j >= 0:
                        a.wait_ge(S["rest_done"], j + 1)
                        nc.scalar.activation(parts_all[:, 1, j * HALF:(j + 1) * HALF], rests[:, j % 4, :],
                                             ACT.Copy).then_inc(S["low_done"], 1)
                a.wait_ge(S["h_ready"], 1)
                nc.scalar.activation(la[1], la[0], ACT.Exp).then_inc(S["exp_done"], 1)
                for k in range(4):
                    a.wait_ge(S["pv_done"], k + 1)
                    nc.scalar.activation(hl[:, 8 * k:8 * k + 8, :].rearrange("p i d -> p (i d)"), bank[k][:], ACT.Copy)

            @block.vector
            def _(v):
                ch = Chain(v, S["dve_chain"])
                layernorm(v, ch, res[:], xn_all, hl[:], squares, st_all, ALLT)
                v.sem_inc(S["xn_ready"], 1)
                for n in range(B4 + 1):
                    if n < B4:
                        cols = slice(n * HALF, (n + 1) * HALF)
                        v.wait_ge(S["high_done"], n + 1)
                        v.tensor_tensor(rests[:, n % 4, :], bank[n % 4][:], parts_all[:, 0, cols],
                                        ALU.subtract).then_inc(S["rest_done"], 1)
                        v.tensor_copy(parts_all[0:D, 2, cols], parts_all[0:D, 0, cols])
                    j = n - 1
                    if j >= 0:
                        cols = slice(j * HALF, (j + 1) * HALF)
                        v.wait_ge(S["low_done"], j + 1)
                        v.tensor_tensor(parts_all[D:P, 2, cols], rests[D:P, j % 4, :], parts_all[D:P, 1, cols],
                                        ALU.subtract).then_inc(S["prod_done"], 1)
                v.wait_ge(S["tok_done"], 1)
                ch.step(v.tensor_tensor(la[2], bank[7][:, 0:ALLT * E].rearrange("p (i e) -> p i e", e=E),
                                        rows(gate_b[:], ALLT), ALU.add))
                ch.step(v.tensor_reduce(sa[0], la[2], X, ALU.max))
                ch.step(v.tensor_tensor(la[0], la[2], bc(sa[0], E), ALU.subtract))
                v.sem_inc(S["h_ready"], 1)
                v.wait_ge(S["exp_done"], 1)
                ch.step(v.tensor_reduce(sa[1], la[1], X, ALU.add))
                ch.step(v.reciprocal(sa[2], sa[1]))
                ch.step(v.tensor_tensor(la[2], la[1], bc(sa[2], E), ALU.mult))
                first_argmax(v, ch, la[2], sa[3], la[3], sa[4], la[4], ALLT)
                v.sem_inc(S["bias_ready"], 1)
                v.wait_ge(S["ssq_done"], 1)
                count, total = (bank[6][:, ALLT * E * k:ALLT * E * (k + 1)].rearrange("p (i e) -> p i e", e=E)
                                for k in range(2))
                src, dst = la[5], la[6]
                ch.step(v.tensor_copy(src, total))
                step = 1
                while step < ALLT:
                    v.tensor_copy(dst[:, 0:step, :], src[:, 0:step, :])
                    ch.step(v.tensor_tensor(dst[:, step:, :], src[:, step:, :], src[:, :ALLT - step, :], ALU.add))
                    src, dst = dst, src
                    step *= 2
                ch.step(v.tensor_tensor(dst, src, total, ALU.subtract))
                ch.step(v.tensor_tensor(src, dst, count, ALU.add))
                ch.step(v.tensor_scalar(dst, src, float(CAPACITY), None, ALU.is_le))
                ch.step(v.tensor_tensor(src, dst, la[4], ALU.mult))
                ch.step(v.tensor_tensor(gates, src, bc(sa[3], E), ALU.mult))
                v.sem_inc(S["bias_ready"], 1)
                v.wait_ge(S["transposed"], 1)
                v.tensor_copy(gatesT.rearrange("p k n -> p (k n)"), bank[5][:, 0:2 * P]).then_inc(S["pT_ready"], 1)

        G = GROUP_TILES
        RING = 8
        LAG = 3
        hid = big2_flat[:, 0:RING * GT].rearrange("p (f t) -> p f t", t=GT)
        weighted = big2_flat[:, RING * GT:RING * GT + G * E * D].rearrange("p (i e d) -> p i e d", e=E, d=D)
        y_at = RING * GT + G * E * D
        ys = [big2_flat[:, y_at + G * D * k:y_at + G * D * (k + 1)] for k in range(5)]
        maski = big2_flat[:, y_at + 5 * G * D:y_at + 6 * G * D].bitcast(I32)

        def capacity_experts(block, it):
            @block.tensor
            def _(pe):
                relu_done = (S["v_act"], S["v_dve"])

                def hidden(n):
                    gg, f = divmod(n, FCH)
                    if n >= 4:
                        pe.wait_ge(relu_done[n % 2], (n - 4) // 2 + 1)
                    split_product(bank[n % 4][:], slice(P * f, P * f + P), ffn_a, ffn_c,
                                  parts_all[:, :, bass.ds(it * (2 * GT) + gg * GT, GT)]).then_inc(S["proj_done"], 1)

                def outputs(n):
                    f = n % FCH
                    e, k = divmod(f, 2)
                    pe.wait_ge(relu_done[n % 2], n // 2 + 1)
                    for i in range(G):
                        if n == FCH:
                            pe.wait_ge(S["prod_done"], i + 1)
                        ins = nc.tensor.matmul(bank[4 + i][:, D * e:D * e + D], hid[:, n % RING, P * i:P * i + P],
                                               ffn_w2[:, f, :], start=(k == 0), stop=(k == 1))
                        if f == FCH - 1:
                            ins.then_inc(S["pv_done"], 1)

                for n in range(2 * FCH + LAG):
                    if n < 2 * FCH:
                        hidden(n)
                    if n >= LAG:
                        outputs(n - LAG)

            @block.scalar
            def _(a):
                for n in range(0, 2 * FCH, 2):
                    f = n % FCH
                    a.wait_ge(S["proj_done"], n + 1)
                    nc.scalar.activation(hid[:, n % RING, :], bank[n % 4][:], ACT.Relu,
                                         bias=ffn_b1[:, f:f + 1]).then_inc(S["v_act"], 1)

            @block.vector
            def _(v):
                ch = Chain(v, S["dve_chain"])

                def hidden(n):
                    f = n % FCH
                    v.wait_ge(S["proj_done"], n + 1)
                    v.tensor_scalar(hid[:, n % RING, :], bank[n % 4][:], ffn_b1[:, f:f + 1], 0.0, ALU.add,
                                    ALU.max).then_inc(S["v_dve"], 1)

                def weigh(gg):
                    for i in range(G):
                        v.wait_ge(S["pv_done"], G * gg + i + 1)
                        tile_gates = gates[:, bass.ds(it * (2 * G) + (gg * G + i), 1), :].rearrange("p i e -> p (i e)")
                        ins = v.tensor_tensor(weighted[:, i], bank[4 + i][:].rearrange("p (e d) -> p e d", d=D),
                                              bc(tile_gates, D), ALU.mult).then_inc(S["prod_done"], 1)
                    v.wait_ge(S["prod_done"], G * gg + G)

                def sum_experts(gg):
                    y0, y1 = ys[0], ys[1]
                    at = bass.ds(it * (2 * G) + gg * G, G)
                    ch.step(v.tensor_reduce(y0.rearrange("p (i d) -> p i d", d=D), weighted.rearrange("p i e d -> p i d e"),
                                            X, ALU.add))
                    ch.step(v.tensor_tensor(y1, y0, hl[:, at, :].rearrange("p i d -> p (i d)"), ALU.add))

                def guard(gg):
                    y1 = ys[1]
                    at = bass.ds(it * (2 * G) + gg * G, G)
                    v.memset(ys[2], 0.0)
                    ch.step(v.tensor_tensor(maski, y1, y1, ALU.is_equal))
                    ch.step(v.copy_predicated(ys[2], maski, y1))
                    ch.step(v.tensor_scalar(maski, ys[2], HUGE, None, ALU.is_gt))
                    ch.step(v.copy_predicated(ys[2], maski, ten_k[:, 0, :]))
                    ch.step(v.tensor_scalar(maski, ys[2], -HUGE, None, ALU.is_lt))
                    ch.step(v.copy_predicated(ys[2], maski, ten_k[:, 1, :]))
                    ch.step(v.tensor_tensor(ys[3 + gg], ys[2], res[:, at, :].rearrange("p i d -> p (i d)"), ALU.add))
                    v.sem_inc(S["last"], 1)

                for n in range(1, FCH + LAG, 2):
                    hidden(n)
                weigh(0)
                for n in range(FCH + LAG, 2 * FCH, 2):
                    hidden(n)
                    if n == FCH + LAG:
                        sum_experts(0)
                    elif n == FCH + LAG + 2:
                        guard(0)
                weigh(1)
                sum_experts(1)
                guard(1)

            @block.sync
            def _(sp):
                for gg in range(2):
                    sp.wait_ge(S["last"], gg + 1)
                    sp.dma_start(out[:, bass.ds(it * (2 * G) + gg * G, G), :], ys[3 + gg].rearrange(
                        "p (i d) -> p i d", d=D)).then_inc(S["x_loaded"], 16)
                sp.wait_ge(S["x_loaded"], 32)

        stage(setup)
        with nc.Fori(0, IMAGES) as b:
            stage(tokens)
            stage(project)
            stage(lambda block: windowed(block, b + 1))
            stage(lambda block: experts(block, b))
            stage(lambda block: full(block, b))
        stage(batchnorm)
        stage(route)
        with nc.Fori(0, GROUPS // 2) as g:
            stage(lambda block: capacity_experts(block, g))


def constants():
    f = np.float32
    c = {"ident": np.eye(P, dtype=f), "lower": np.triu(np.ones((P, P), f))}
    k, n = np.arange(FREQ)[:, None], np.arange(PATCH)[None, :]
    ang = 2 * np.pi * k * n / PATCH
    c["dft"] = (np.concatenate([np.cos(ang), -np.sin(ang)]) / np.sqrt(PATCH)).astype(f)
    freqs = (f(10000.0) ** (f(-2.0) * np.arange(D // 2, dtype=f) / f(D))).astype(f)
    theta = np.arange(SEQ, dtype=f)[None, :] * np.repeat(freqs, 2)[:, None]
    sign = np.where(np.arange(D) % 2 == 0, -1.0, 1.0)[:, None]
    c["rope_cos"] = np.tile(np.cos(theta), (2, 1)).astype(f)
    c["rope_sin"] = np.tile(np.sin(theta) * sign, (2, 1)).astype(f)
    t = np.arange(CHUNK)
    c["row_of_t"] = np.tile(np.eye(CHUNK, dtype=f), (1, NQ))
    j = np.arange(SPAN)
    m = np.zeros((CHUNK, EARLY + 1, SPAN))
    for v in range(EARLY + 1):
        ok = (j[None] >= t[:, None]) & (j[None] <= t[:, None] + WINDOW) & (j[None] >= WINDOW - CHUNK * v)
        m[:, v] = np.where(ok, 0.0, -1e30)
    c["window_mask"] = m.astype(f)
    c["by_head"] = np.repeat(np.eye(2, dtype=f), D, axis=0)
    c["copies"] = np.stack([np.tile(np.eye(P, dtype=f)[:, CHUNK * m:CHUNK * (m + 1)], (1, NQ)) for m in range(NQ)], 1)
    c["first_weight"] = np.tile(np.arange(E, 0, -1, dtype=f), (P, 1))
    return c


def layouts(i):
    def two(a):
        return np.concatenate([a, a], axis=0)

    a = {k: np.asarray(v) for k, v in i.items()}
    x = a["x"].transpose(0, 1, 3, 2)
    swap = np.arange(D) ^ 1
    wq = a["L0_attn_wq"].reshape(PAIRS, 2, D, D)
    wk = a["L0_attn_wkv"][:D]
    q = np.stack([wq, wq[:, :, swap]], axis=1).transpose(4, 0, 1, 2, 3).reshape(D, 2 * PAIRS * P)
    k = np.stack([wk, wk, wk[swap], wk[swap]]).transpose(2, 0, 1).reshape(D, 2 * P)
    w1 = a["L0_ffn_w1"].reshape(E // 2, 2, D, D)
    fw1 = a["L1_ffn_w1"].transpose(1, 0, 2).reshape(D, FCH * P)
    return {
        "x": np.concatenate([x, np.concatenate([x[..., STRIDE:], np.repeat(x[..., -1:], STRIDE, -1)], -1)],
                            axis=1)[[*range(IMAGES), 0]],
        "tok_w": a["L0_tok_W"].reshape(D, 2 * FREQ, CH).transpose(1, 0, 2),
        "wv0": a["L0_attn_wkv"][D:].T,
        "wo0": a["L0_attn_wo"].reshape(D, PAIRS, P).transpose(2, 1, 0),
        "q_norm": a["L0_attn_q_norm_w"].reshape(D, 1), "k_norm": a["L0_attn_k_norm_w"].reshape(D, 1),
        "router": a["L0_ffn_router_w"].T,
        "proj_w": two(np.concatenate([q, k, w1.transpose(2, 0, 1, 3).reshape(D, E * D), *[a["L1_attn_Wq"]] * 2,
                                      *[a["L1_attn_Wk"]] * 2], axis=1)),
        "moe_b1": a["L0_ffn_b1"].reshape(E // 2, P).T,
        "moe_w2": a["L0_ffn_w2"].reshape(E // 2, P, D).transpose(1, 0, 2),
        "moe_b2": a["L0_ffn_b2"],
        "bq1": a["L1_attn_bq"].reshape(D, 1), "bk1": a["L1_attn_bk"].reshape(D, 1),
        "bv1": a["L1_attn_bv"].reshape(D, 1),
        "wvT1": a["L1_attn_Wv"].T, "wl1": a["L1_attn_Wl"],
        "bl1": a["L1_attn_bl"].reshape(1, D), "gamma": a["L1_attn_gamma"].reshape(1, D),
        "beta": a["L1_attn_beta"].reshape(1, D), "gate_b": a["L1_ffn_gate_b"].reshape(1, E),
        "ffn_w": two(np.concatenate([fw1, a["L1_ffn_gate_w"]], axis=1)),
        "ffn_b1": a["L1_ffn_b1"].reshape(FCH, P).T,
        "ffn_w2": a["L1_ffn_w2"].reshape(FCH, P, D).transpose(1, 0, 2),
        "ffn_b2": a["L1_ffn_b2"],
    }


def kernel(**inputs):
    import concourse.bacc as _bacc
    from concourse.bass_utils import run_bass_kernel_spmd as _run

    nc = _bacc.Bacc("TRN2", target_bir_lowering=False, num_devices=1)
    arrays, args = {}, {}
    for name, a in {**constants(), **layouts(inputs)}.items():
        a = np.ascontiguousarray(a)
        arrays[f"in_{name}"] = a
        args[name] = nc.dram_tensor(f"in_{name}", a.shape, mybir.dt.from_np(a.dtype), kind="ExternalInput").ap()
    out = nc.dram_tensor("out", (IMAGES * SEQ, D), F32, kind="ExternalOutput").ap()
    program(nc, args, out.rearrange("(i p) d -> p i d", p=P))
    r = _run(nc, [arrays], core_ids=[0])
    return r.results[0]["out"].reshape(IMAGES, SEQ, D)
```

```python
from contextlib import ExitStack

import numpy as np

import concourse.bass as bass
from concourse import mybir

F32 = mybir.dt.float32
BF16 = mybir.dt.bfloat16
I32 = mybir.dt.int32
ALU = mybir.AluOpType
ACT = mybir.ActivationFunctionType
X = mybir.AxisListType.X

P = 128
IMAGES, CH, T, V = 4, 64, 128, 64
D = 64
PATCH, STRIDE = 16, 8
NPATCH = T // STRIDE
SEQ = V * NPATCH
TILES = SEQ // P
ALLT = IMAGES * TILES
FREQ = PATCH // 2 + 1
HEADS = 16
PAIRS = HEADS // 2
WINDOW = 128
CHUNK = 32
CHUNKS = SEQ // CHUNK
SPAN = WINDOW + CHUNK
EARLY = WINDOW // CHUNK
NQ = 4
E = 8
F1 = 256
FCH = E * F1 // P
GROUP_TILES = 4
GROUPS = ALLT // GROUP_TILES
GT = GROUP_TILES * P
CAPACITY = -(-5 * IMAGES * SEQ // (4 * E))
LN_EPS = 1e-5
BN_EPS = 1e-5
RMS_EPS = 1.1920929e-07
HUGE = 3.4028235e38
HALF = 512
Q_COLS, K_COLS, MOE_COLS, Q1_COLS = 0, 2 * PAIRS * P, 2 * (PAIRS + 1) * P, 2 * (PAIRS + 1) * P + E * D
K1_COLS = Q1_COLS + P
PROJ = K1_COLS + P
FFN_COLS = FCH * P + E


class Chain:

    def __init__(self, engine, sem):
        self.engine, self.sem, self.n = engine, sem, 0

    def step(self, ins):
        self.n += 1
        ins.then_inc(self.sem, 1)
        self.engine.wait_ge(self.sem, self.n)


def program(nc, inp, out):
    with ExitStack() as ctx:
        def sb(name, shape, dt=F32):
            return ctx.enter_context(nc.sbuf_tensor(name, shape, dt))

        def sem(name):
            return ctx.enter_context(nc.semaphore(name))

        bank = [ctx.enter_context(nc.psum_tensor(f"bank{i}", [P, HALF], F32)) for i in range(8)]

        shapes = {k: (list(v.shape), v.dtype) for k, v in inp.items()}
        loaded = ["ident", "dft", "rope_cos", "rope_sin", "row_of_t", "window_mask", "lower", "first_weight",
                  "tok_w", "by_head", "wv0", "wo0", "router", "moe_b1", "moe_w2", "wvT1", "wl1", "proj_w"]
        big1 = sb("big1", [P, PAIRS, SEQ])
        big2 = sb("big2", [P, PAIRS, SEQ])
        aside = ("tok_w", "row_of_t", "window_mask", "moe_w2", "proj_w")
        sbuf = {k: sb("s_" + k, *shapes[k]) for k in loaded if k not in aside}
        sbuf["tok_w"] = big1[0:2 * FREQ, 0:D * CH // SEQ, :].rearrange("p a n -> p (a n)").rearrange(
            "p (o c) -> p o c", c=CH)
        sbuf["moe_w2"] = big2[:, 0, P:P + E // 2 * D].rearrange("p (k d) -> p k d", d=D)
        moe_b2_rows = big2[:, 0, P + E // 2 * D:P + E // 2 * D + E * D]
        sbuf["proj_w"] = big1[:, 4:8, :].rearrange("p a n -> p (a n)")[:, 0:PROJ]
        w_a, w_c = sb("w_a", [P, PROJ], BF16), sb("w_c", [P, PROJ], BF16)
        moe_w2 = sb("moe_w2", [P, E // 2, P])
        sbuf["row_of_t"] = big2[0:CHUNK, 0, 0:P]
        sbuf["window_mask"] = big2[0:CHUNK, 1, 0:(EARLY + 1) * SPAN].rearrange("p (v k) -> p v k", k=SPAN)
        row_of_t = sb("row_of_t", [CHUNK, P], BF16)
        window_mask = sb("window_mask", [CHUNK, EARLY + 1, SPAN], BF16)
        ident, lower = sbuf["ident"], sbuf["lower"]
        qn, kn, wqk = sb("qn", [P, 1]), sb("kn", [P, 1]), sb("wqk", [P, 1])
        bq, bk = sb("bq", [P, 1]), sb("bk", [P, 1])
        bvcol, bvrep = sb("bvcol", [D, 1]), sb("bvrep", [D, P])
        blrow, gammarow, betarow = sb("blrow", [P, D]), sb("gammarow", [P, D]), sb("betarow", [P, D])
        vbias = sb("vbias", [P, D])
        gate_b = sb("gate_b", [P, E])
        both_halves = sb("both_halves", [P, D])
        part_rows = sb("part_rows", [P, P], BF16)
        moe_b2 = sb("moe_b2", [P, E * D], BF16)
        ones, ones_mean, zeros = sb("ones", [P, P]), sb("ones_mean", [P, P]), sb("zeros", [P, P])
        wvl = sb("wvl", [D, D])
        weff = sb("weff", [P, STRIDE, D])

        xb = sb("xb", [P, V, T])
        xflat = xb[:].rearrange("p v t -> p (v t)")
        taken = 0

        def from_xb(n, dt=F32):
            nonlocal taken
            taken += n
            ap = xflat[:, taken - n:taken]
            return ap if dt == F32 else ap.bitcast(dt)

        ffn_w = from_xb(FFN_COLS)
        ffn_w2 = from_xb(FCH * D).rearrange("p (f d) -> p f d", d=D)
        ffn_b2 = from_xb(D)[0:E]
        b2_parts = from_xb(3 * P // 2, BF16)[0:E].rearrange("e (k d) -> e k d", k=3)
        others = from_xb(E * P // 2, BF16)[0:E].rearrange("e (x f) -> e x f", x=E)
        ffn_a, ffn_c = from_xb(FFN_COLS // 2, BF16), from_xb(FFN_COLS // 2, BF16)
        gates = from_xb(ALLT)
        ten_k = from_xb(2 * GROUP_TILES * D).rearrange("p (s n) -> p s n", s=2)
        ffn_b1 = from_xb(FCH)
        st_all = from_xb(8 * ALLT).rearrange("p (k i) -> p k i", k=8)
        h = sb("h", [P, TILES, D])
        st = sb("st", [P, 8, TILES])
        xT = sb("xT", [P, WINDOW + SEQ])
        parts_a2 = xflat[:, 0:3 * SEQ // 2].bitcast(BF16).rearrange("p (s n) -> p s n", s=3)
        parts = big1[:, 6:8, :].rearrange("p a n -> p (a n)")[:, 0:3 * SEQ // 2].bitcast(BF16).rearrange(
            "p (s n) -> p s n", s=3)
        qT = big1[:].rearrange("p a n -> p (a n)").rearrange("p (c a t) -> p c a t", a=PAIRS, t=CHUNK)
        sq = big2[:].rearrange("p a n -> p (a n)").rearrange("p (c a t) -> p c a t", a=PAIRS, t=CHUNK)
        oT = big2
        work = sb("work", [P, 4 * HALF])
        rest = work[:, 0:2 * HALF].rearrange("p (w n) -> p w n", w=2)
        prod = work[:].rearrange("p (a c n) -> p a c n", a=2, c=2)
        probs = work[:, 0:3 * NQ * SPAN].rearrange("p (a q k) -> p a q k", a=3, q=NQ)
        rq = sb("rq", [P, CHUNKS, 2, 2])
        rqflat = rq[:].rearrange("p c a e -> p (c a e)")
        kT = sb("kT", [P, 2, WINDOW + SEQ])
        rk = sb("rk", [P, TILES])
        vwin = sb("vwin", [P, CHUNKS, D])
        xn = vwin[:, 0:2 * TILES, :].rearrange("p (i a) d -> p i a d", a=2)
        vrem = sb("vrem", [P, CHUNKS, D])
        tmp, moe = vrem[:, 0:TILES, :], vrem[:, TILES:2 * TILES, :]
        turned = sb("turned", [P, 2 * HALF])
        pT = turned[:].rearrange("p (a q r) -> p a q r", a=2, q=NQ)
        yw = turned[:].rearrange("p (a e d) -> p a e d", a=2, e=E)
        values = xflat[:, 3 * SEQ // 2:2 * SEQ].rearrange("p (i d) -> p i d", d=D)
        k_turned = xflat[:, 2 * SEQ:3 * SEQ]
        tokensT = work[:, 2 * HALF:3 * HALF]
        k_squares = turned[:]
        diag = turned[:]
        pTr_own = sb("pTr_own", [P, 4, P])
        pTr, own = pTr_own[:, 0:2, :], pTr_own[:, 2:4, :]
        sums_turned = pTr_own[:].rearrange("p a n -> p (a n)")
        newton = pTr_own
        small = sb("small", [P, 4, 4, NQ])
        lg = sb("lg", [P, 8, TILES, E])
        comb = sb("comb", [P, TILES, E])
        hT = big2[:].rearrange("p a b -> p (a b)")

        res = sb("res", [P, ALLT, D])
        hl = sb("hl", [P, ALLT, D])
        base = sb("base", [P, E])
        mean_row, var_row = sb("mean_row", [P, D]), sb("var_row", [P, D])
        first_sem = sem("const_loaded")
        sems = {n: sem(n) for n in [
            "set_ready", "tok_loaded", "w_loaded", "x_loaded", "high_done", "rest_done", "low_done", "tok_done", "h_ready", "dve_chain", "cos_done", "q_root", "k_root", "xn_ready", "xT_psum",
            "xT_act", "xT_dve", "proj_done", "square_done", "prod_done", "rot_done", "ssq_done", "v_psum", "v_act",
            "v_dve", "kprod", "scores_done", "bias_ready", "exp_done", "scaled", "transposed",
            "pT_ready", "pTr_ready", "pv_done", "oT_ready", "wo_done", "last"]}
        S = sems
        clear = range(first_sem.num, S["last"].num + 1)

        def stage(build):
            with nc.Block() as block:
                build(block)
            nc.all_engine_barrier(sems_to_clear=clear)

        def bc(ap, n):
            return ap.unsqueeze(2).to_broadcast([ap.shape[0], ap.shape[1], n])

        def rows(ap, n):
            return ap.unsqueeze(1).to_broadcast([ap.shape[0], n, ap.shape[1]])

        def layernorm(v, ch, src, dst, diff, work, stat, tiles):
            ch.step(v.tensor_reduce(stat[:, 0, :tiles], src, X, ALU.add))
            ch.step(v.tensor_scalar(stat[:, 1, :tiles], stat[:, 0, :tiles], 1.0 / D, None, ALU.mult))
            ch.step(v.tensor_tensor(diff, src, bc(stat[:, 1, :tiles], D), ALU.subtract))
            ch.step(v.tensor_tensor(work, diff, diff, ALU.mult))
            ch.step(v.tensor_reduce(stat[:, 2, :tiles], work, X, ALU.add))
            ch.step(v.tensor_scalar(stat[:, 3, :tiles], stat[:, 2, :tiles], 1.0 / D, LN_EPS, ALU.mult, ALU.add))
            one_over_root(v, ch, stat[:, 4, :tiles], stat[:, 3, :tiles])
            for i in range(0, tiles, 4):
                v.tensor_tensor(dst[:, i:i + 4], diff[:, i:i + 4].unsqueeze(2).to_broadcast([P, 4, 2, D]),
                                stat[:, 4, i:i + 4].unsqueeze(2).unsqueeze(3).to_broadcast([P, 4, 2, D]),
                                ALU.mult).then_inc(S["xn_ready"], 1)

        def one_over_root(v, ch, dst, x):
            n = x.shape[1]
            half, y, t = (newton[:, k, 0:n] for k in range(3))
            ch.step(v.tensor_scalar(half.bitcast(I32), x.bitcast(I32), 1, None, ALU.logical_shift_right))
            ch.step(v.tensor_scalar(y.bitcast(I32), half.bitcast(I32), -1.0, float(0x5F3759DF), ALU.mult, ALU.add))
            for k in range(3):
                ch.step(v.tensor_tensor(t, y, y, ALU.mult))
                ch.step(v.scalar_tensor_tensor(out=t, in0=t, scalar=-0.5, in1=x, op0=ALU.mult, op1=ALU.mult))
                ch.step(v.scalar_tensor_tensor(out=dst if k == 2 else y, in0=t, scalar=1.5, in1=y, op0=ALU.add,
                                               op1=ALU.mult))

        def split_weights(v, ch, w, part_a, part_c, high, low, rest):
            ch.step(v.tensor_copy(high, w))
            ch.step(v.tensor_tensor(rest, w, high, ALU.subtract))
            ch.step(v.tensor_copy(low, rest))
            v.tensor_copy(part_a[0:D], high[0:D])
            v.tensor_copy(part_a[D:P], low[D:P])
            v.tensor_copy(part_c[D:P], high[D:P])
            ch.step(v.tensor_tensor(part_c[0:D], rest[0:D], low[0:D], ALU.subtract))

        def split_bias(v, ch, b, parts, high, low, rest):
            ch.step(v.tensor_copy(high, b))
            ch.step(v.tensor_tensor(rest, b, high, ALU.subtract))
            ch.step(v.tensor_copy(low, rest))
            v.tensor_copy(parts[0:32], high[0:32])
            v.tensor_copy(parts[32:64], low[32:64])
            ch.step(v.tensor_tensor(parts[64:P], rest[64:P], low[64:P], ALU.subtract))

        def split_product(out_ap, cols, part_a, part_c, xs, start=True):
            for k, w in ((0, part_a), (1, part_a), (2, part_c)):
                ins = nc.tensor.matmul(out_ap, w[:, cols], xs[:, k, :], start=(k == 0), stop=(k == 2))
            return ins

        def split_scalar(a, banks, xs):
            for w in range(2):
                a.wait_ge(S["xT_psum"], w + 1)
                nc.scalar.activation(xs[:, 0, w * HALF:(w + 1) * HALF], bank[banks[w]][:],
                                     ACT.Copy).then_inc(S["high_done"], 1)
            for w in range(2):
                a.wait_ge(S["rest_done"], w + 1)
                nc.scalar.activation(xs[:, 1, w * HALF:(w + 1) * HALF], rest[:, w, :], ACT.Copy).then_inc(S["low_done"], 1)
                nc.scalar.activation(xT[:, WINDOW + w * HALF:WINDOW + (w + 1) * HALF], bank[banks[w]][:], ACT.Copy)

        def split_vector(v, banks, xs):
            for w in range(2):
                cols = slice(w * HALF, (w + 1) * HALF)
                v.wait_ge(S["high_done"], w + 1)
                v.tensor_tensor(rest[:, w, :], bank[banks[w]][:], xs[:, 0, cols],
                                ALU.subtract).then_inc(S["rest_done"], 1)
                v.tensor_copy(xs[0:D, 2, cols], xs[0:D, 0, cols])
            for w in range(2):
                cols = slice(w * HALF, (w + 1) * HALF)
                v.wait_ge(S["low_done"], w + 1)
                v.tensor_tensor(xs[D:P, 2, cols], rest[D:P, w, :], xs[D:P, 1, cols], ALU.subtract)

        def transpose_tiles(pe, src, tiles, banks, ready=0):
            for i in range(tiles):
                if i % 4 == 0:
                    pe.wait_ge(S["xn_ready"], ready + i // 4 + 1)
                twice = src[:, i].rearrange("p a d -> p (a d)")
                ins = nc.tensor.transpose(bank[banks[i // 4]][:, (i % 4) * P:(i % 4 + 1) * P], twice, ident[:])
                if i % 4 == 3:
                    ins.then_inc(S["xT_psum"], 1)

        def setup(block):
            @block.sync
            def _(sp):
                n = 0
                for k in ("tok_w", "dft"):
                    sp.dma_start(sbuf[k] if k in aside else sbuf[k][:], inp[k]).then_inc(S["tok_loaded"], 16)
                sp.dma_start(sbuf["proj_w"], inp["proj_w"]).then_inc(S["w_loaded"], 16)
                for k in loaded:
                    if k in ("proj_w", "tok_w", "dft"):
                        continue
                    sp.dma_start(sbuf[k] if k in aside else sbuf[k][:], inp[k]).then_inc(first_sem, 16)
                    n += 1
                for half in range(2):
                    r = slice(D * half, D * half + D)
                    for dst, src in ((qn, "q_norm"), (kn, "k_norm"), (bq, "bq1"), (bk, "bk1")):
                        sp.dma_start(dst[r, :], inp[src]).then_inc(first_sem, 16)
                        n += 1
                sp.dma_start(bvcol[:], inp["bv1"]).then_inc(first_sem, 16)
                n += 1
                for dst, src in ((blrow, "bl1"), (gammarow, "gamma"), (betarow, "beta"), (gate_b, "gate_b"),
                                 (moe_b2_rows, "moe_b2")):
                    sp.dma_start(dst[:] if dst is not moe_b2_rows else dst, inp[src].to_broadcast([P, inp[src].shape[1]])).then_inc(first_sem, 16)
                    n += 1
                load_x(sp, 0, first_sem)
                n += 1
                sp.wait_ge(first_sem, 16 * n)
                sp.sem_inc(S["x_loaded"], 1)

            @block.vector
            def _(v):
                ch = Chain(v, S["dve_chain"])
                ch.step(v.memset(part_rows[:], 0.0))
                for row in (0, 32, 64):
                    v.memset(part_rows[row:row + 1, :], 1.0)
                v.memset(ones[:], 1.0)
                v.memset(ones_mean[:], 1.0 / (ALLT * P))
                v.memset(zeros[:], 0.0)
                v.memset(base[:], 0.0)
                v.memset(xT[:, 0:WINDOW], 0.0)
                v.memset(kT[:], 0.0)
                ch.step(v.memset(moe_w2[:], 0.0))
                v.wait_ge(S["w_loaded"], 16)
                n = PROJ // 2
                scratch = big2[:, 2:6, :].rearrange("p a n -> p (a n)")
                for k in range(2):
                    cols = slice(k * n, k * n + n)
                    split_weights(v, ch, sbuf["proj_w"][:, cols], w_a[:, cols], w_c[:, cols],
                                  scratch[:, 0:n // 2].bitcast(BF16), scratch[:, n // 2:n].bitcast(BF16),
                                  scratch[:, n:2 * n])
                v.wait_ge(S["x_loaded"], 1)
                for r in range(2):
                    v.tensor_copy(moe_w2[D * r:D * r + D, :, D * r:D * r + D], sbuf["moe_w2"][D * r:D * r + D])
                room = big2[:, 6:8, :].rearrange("p a n -> p (a n)")
                split_bias(v, ch, moe_b2_rows, moe_b2, room[:, 0:E * D // 2].bitcast(BF16),
                           room[:, E * D:E * D + E * D // 2].bitcast(BF16), room[:, 2 * E * D:3 * E * D])
                v.tensor_tensor(both_halves[:], ident[:, 0:D], ident[:, D:P], ALU.add)
                v.tensor_copy(row_of_t[:], sbuf["row_of_t"])
                v.tensor_copy(window_mask[:], sbuf["window_mask"])
                ch.step(v.tensor_scalar(wqk[:], qn[:], kn[:, 0:1], float(np.sqrt(D)), ALU.mult, ALU.mult))
                ch.step(v.tensor_scalar(bvrep[:], zeros[0:D, :], bvcol[:, 0:1], None, ALU.add))
                v.sem_inc(S["h_ready"], 1)
                v.wait_ge(S["tok_done"], 1)
                v.tensor_copy(weff[:], bank[0][:].rearrange("p (o r) -> p r o", r=STRIDE)).then_inc(S["xn_ready"], 1)
                v.wait_ge(S["proj_done"], 1)
                v.tensor_tensor(vbias[:], bank[1][:, 0:D], blrow[:], ALU.add)
                ch.step(v.tensor_copy(wvl[:], bank[1][0:D, D:2 * D]))

            @block.tensor
            def _(pe):
                pe.wait_ge(S["tok_loaded"], 32)
                w = sbuf["tok_w"]
                for o in range(D):
                    for j in range(2):
                        ins = nc.tensor.matmul(bank[0][D * j:D * j + D, o * STRIDE:(o + 1) * STRIDE], w[:, o, :],
                                               sbuf["dft"][:, j * STRIDE:(j + 1) * STRIDE], start=True, stop=True)
                ins.then_inc(S["tok_done"], 1)
                pe.wait_ge(S["h_ready"], 1)
                nc.tensor.matmul(bank[1][:, 0:D], bvrep[:], sbuf["wl1"][:], start=True, stop=True)
                nc.tensor.matmul(bank[1][0:D, D:2 * D], sbuf["wvT1"][:], sbuf["wl1"][:], start=True,
                                 stop=True).then_inc(S["proj_done"], 1)
                pe.wait_ge(S["xn_ready"], 1)
                for r in range(STRIDE):
                    ins = token_products(r)
                ins.then_inc(S["prod_done"], 1)

            @block.scalar
            def _(a):
                a.wait_ge(S["prod_done"], 1)
                nc.scalar.activation(tokensT, bank[5][:], ACT.Copy)

        def load_x(sp, b, s):
            sp.dma_start(xb[:], inp["x"][bass.ds(b, 1)].rearrange("b p v t -> (b p) v t")).then_inc(s, 16)

        def token_products(r):
            steps = xflat.rearrange("p (s r) -> p r s", r=STRIDE)
            for w in range(2):
                ins = nc.tensor.matmul(bank[5][D * w:D * w + D, :], weff[:, r, :], steps[:, r, w * HALF:(w + 1) * HALF],
                                       start=(r == 0), stop=(r == STRIDE - 1))
            return ins

        def turn_halves(done):
            for j in range(TILES // 2):
                ins = nc.tensor.transpose(bank[3][:, P * j:P * j + P], tokensT[:, P * j:P * j + P], ident[:])
            ins.then_inc(done, 1)

        def tokens(block):
            @block.tensor
            def _(pe):
                turn_halves(S["tok_done"])
                transpose_tiles(pe, xn, TILES, [1, 2])

            @block.scalar
            def _(a):
                a.wait_ge(S["tok_done"], 1)
                nc.scalar.activation(h[:].rearrange("p (w j) d -> p j w d", w=2),
                                     bank[3][:].rearrange("p (j w d) -> p j w d", w=2, d=D), ACT.Copy).then_inc(S["h_ready"], 1)
                split_scalar(a, (1, 2), parts_a2)

            @block.vector
            def _(v):
                ch = Chain(v, S["dve_chain"])
                v.wait_ge(S["h_ready"], 1)
                layernorm(v, ch, h[:], xn, tmp, moe, st, TILES)
                split_vector(v, (1, 2), parts_a2)

        UNITS = 2 * (PAIRS + 1)

        def unit(u):
            if u < 2:
                return PAIRS, u
            group, i = divmod(u - 2, 4)
            return 4 * (group % 2) + i, group // 2

        SIDE = (2, 3, 7, 8)

        def project(block):
            @block.tensor
            def _(pe):
                def k_sums():
                    pe.wait_ge(S["square_done"], 2)
                    for i in range(TILES):
                        ins = nc.tensor.matmul(bank[7][:, i:i + 1], k_squares[:, P * i:P * i + P],
                                               sbuf["by_head"][:, 0:1], start=True, stop=True)
                    ins.then_inc(S["v_psum"], 1)

                def token_values():
                    pe.wait_ge(S["v_dve"], 1)
                    for i in range(TILES):
                        ins = nc.tensor.matmul(bank[7][:, D * i:D * i + D], xT[0:D, WINDOW + P * i:WINDOW + P * i + P],
                                               sbuf["wv0"][:], start=True, stop=True)
                    ins.then_inc(S["v_psum"], 1)

                def k_norms(w):
                    if w == 0:
                        pe.wait_ge(S["v_act"], 1)
                        pe.wait_ge(S["k_root"], 1)
                    else:
                        pe.wait_ge(S["v_dve"], 2)
                    nc.tensor.matmul(bank[7][:], ones[:], diag[:, w * HALF:(w + 1) * HALF], start=True,
                                     stop=True).then_inc(S["v_psum"], 1)

                def q_sums(group):
                    w, hh = divmod(group, 2)
                    pe.wait_ge(S["square_done"], 6 + 4 * group)
                    if group:
                        pe.wait_ge(S["q_root"], group)
                    for a in range(4):
                        ins = nc.tensor.matmul(bank[6][32 * a:32 * a + 32, :], sbuf["by_head"][:],
                                               sq[:, w * CHUNKS // 2:(w + 1) * CHUNKS // 2, 4 * hh + a, :], start=True,
                                               stop=True)
                    ins.then_inc(S["ssq_done"], 1)

                for u in range(UNITS + 1):
                    if u < UNITS:
                        pair, w = unit(u)
                        if u >= 3:
                            pe.wait_ge(S["prod_done"], u - 2)
                            pe.wait_ge(S["square_done"], u - 2)
                        for c in range(2):
                            cols = slice((2 * pair + c) * P, (2 * pair + c) * P + P)
                            ins = split_product(bank[2 * (u % 3) + c][:], cols, w_a, w_c,
                                                parts_a2[:, :, w * HALF:(w + 1) * HALF])
                        ins.then_inc(S["proj_done"], 1)
                    if u == SIDE[0]:
                        k_sums()
                    if u == SIDE[1]:
                        token_values()
                    if SIDE[2] <= u <= SIDE[3]:
                        k_norms(u - SIDE[2])
                    if u >= 6 and (u - 6) % 4 == 0:
                        q_sums((u - 6) // 4)

            @block.scalar
            def _(a):
                for u in range(UNITS):
                    pair, w = unit(u)
                    a.wait_ge(S["cos_done"], u + 1)
                    dst = (sq[:, w * CHUNKS // 2:(w + 1) * CHUNKS // 2, pair, :] if pair < PAIRS
                           else k_squares[:, w * HALF:(w + 1) * HALF])
                    src = bank[2 * (u % 3)][:]
                    if pair < PAIRS:
                        src = src.rearrange("p (c t) -> p c t", t=CHUNK)
                    nc.scalar.activation(dst, src, ACT.Square).then_inc(S["square_done"], 1)
                    if u == SIDE[1]:
                        a.wait_ge(S["v_psum"], 2)
                        nc.scalar.activation(values.rearrange("p i d -> p (i d)"), bank[7][:],
                                             ACT.Copy).then_inc(S["v_act"], 1)

            @block.sync
            def _(sp):
                n = 0
                sp.wait_ge(S["v_act"], 1)
                sp.wait_ge(S["set_ready"], 1)
                for s in range(NQ):
                    low = CHUNK * s
                    sp.dma_start(vwin[0:P - low, NQ + s::NQ, :], values[low:P, 0:TILES - 1, :]).then_inc(S["x_loaded"], 16)
                    n += 1
                    if s:
                        sp.dma_start(vwin[P - low:P, s::NQ, :], values[0:low, :, :]).then_inc(S["x_loaded"], 16)
                        n += 1
                for s in range(NQ):
                    for q in range(NQ):
                        sp.dma_start(vrem[CHUNK * q:CHUNK * q + CHUNK, s::NQ, :],
                                     values[CHUNK * s:CHUNK * s + CHUNK, :, :]).then_inc(S["x_loaded"], 16)
                        n += 1
                sp.wait_ge(S["x_loaded"], 16 * n)

            @block.vector
            def _(v):
                ch = Chain(v, S["dve_chain"])

                def q_sums(group):
                    w, hh = divmod(group, 2)
                    v.wait_ge(S["ssq_done"], group + 1)
                    ch.step(v.transpose(sums_turned, bank[6][:]))
                    v.sem_inc(S["q_root"], 1)
                    ch.step(v.tensor_scalar(rq[:, w * CHUNKS // 2:(w + 1) * CHUNKS // 2, hh, :],
                                            sums_turned.rearrange("p (c e) -> p c e", e=32)[:, :, 0:2], D * RMS_EPS, None,
                                            ALU.add))

                for u in range(UNITS):
                    pair, w = unit(u)
                    cols = slice(w * HALF, (w + 1) * HALF)
                    v.wait_ge(S["proj_done"], u + 1)
                    if u >= 2:
                        v.wait_ge(S["rot_done"], u - 1)
                    v.tensor_tensor(prod[:, u % 2, 0, :], bank[2 * (u % 3)][:], sbuf["rope_cos"][:, cols],
                                    ALU.mult).then_inc(S["cos_done"], 1)
                    v.tensor_tensor(prod[:, u % 2, 1, :], bank[2 * (u % 3) + 1][:], sbuf["rope_sin"][:, cols],
                                    ALU.mult).then_inc(S["prod_done"], 1)
                    if u == SIDE[0]:
                        v.wait_ge(S["v_psum"], 1)
                        ch.step(v.tensor_scalar(rk[:], bank[7][:, 0:TILES], D * RMS_EPS, None, ALU.add))
                        v.sem_inc(S["v_dve"], 1)
                        one_over_root(v, ch, rk[:], rk[:])
                        v.tensor_tensor(diag[:].rearrange("p (i k) -> p i k", k=P), rows(ident[:], TILES), bc(rk[:], P),
                                        ALU.mult).then_inc(S["k_root"], 1)
                    if SIDE[2] <= u <= SIDE[3]:
                        w = u - SIDE[2]
                        v.wait_ge(S["v_psum"], w + 3)
                        for e in range(2):
                            r = slice(D * e, D * e + D)
                            ins = v.scalar_tensor_tensor(out=kT[r, e, WINDOW + w * HALF:WINDOW + (w + 1) * HALF],
                                                         in0=k_turned[r, w * HALF:(w + 1) * HALF], scalar=wqk[r, 0:1],
                                                         in1=bank[7][r, :], op0=ALU.mult, op1=ALU.mult)
                        ins.then_inc(S["v_dve"], 1)
                    if u >= 8 and (u - 8) % 4 == 0:
                        q_sums((u - 8) // 4)
                q_sums(3)
                one_over_root(v, ch, rqflat, rqflat)

            @block.gpsimd
            def _(g):
                g.memset(vwin[:, 0:NQ, :], 0.0).then_inc(S["set_ready"], 1)
                for u in range(UNITS):
                    pair, w = unit(u)
                    g.wait_ge(S["prod_done"], u + 1)
                    dst, first, second = k_turned[:, w * HALF:(w + 1) * HALF], prod[:, u % 2, 0, :], prod[:, u % 2, 1, :]
                    if pair < PAIRS:
                        dst = qT[:, w * CHUNKS // 2:(w + 1) * CHUNKS // 2, pair, :]
                        first, second = (z.rearrange("p (c t) -> p c t", t=CHUNK) for z in (first, second))
                    g.tensor_tensor(dst, first, second, ALU.add).then_inc(S["rot_done"], 1)

        def windowed(block, b):
            def s_bank(c, half):
                return bank[2 * (c % 2) + half]

            @block.sync
            def _(sp):
                load_x(sp, b, S["x_loaded"])
                sp.wait_ge(S["x_loaded"], 16)

            @block.tensor
            def _(pe):
                def scores(c):
                    if c >= 2:
                        pe.wait_ge(S["exp_done"], NQ * (c - 1))
                    variant = min(c, EARLY)
                    for hh in range(2):
                        tiles = s_bank(c, hh)[:, 0:2 * SPAN].rearrange("p (e k) -> p e k", e=2)
                        if c < EARLY:
                            mask, masked = rows(window_mask[:, variant, :], 2), tiles
                        else:
                            mask = window_mask[:, variant].rearrange("p (g k) -> p g k", k=CHUNK)[:, ::SPAN // CHUNK - 1, :]
                            mask = mask.unsqueeze(1).to_broadcast([CHUNK, 2, 2, CHUNK])
                            masked = tiles.rearrange("p e (g k) -> p e g k", k=CHUNK)[:, :, ::SPAN // CHUNK - 1, :]
                        nc.tensor.matmul(masked, row_of_t[:], mask, start=True, stop=True, skip_group_check=True)
                        ins = nc.tensor.matmul(tiles, qT[:, c, 4 * hh:4 * hh + 4, :].rearrange("p a t -> p (a t)"),
                                               kT[:, :, CHUNK * c:CHUNK * c + SPAN], start=False, stop=True,
                                               skip_group_check=True)
                    ins.then_inc(S["scores_done"], 1)

                def turn(c):
                    pe.wait_ge(S["scaled"], c + 1)
                    if c >= 2:
                        pe.wait_ge(S["pT_ready"], c - 1)
                        pe.wait_ge(S["pTr_ready"], c - 1)
                    for q in range(NQ):
                        nc.tensor.transpose(bank[4 + c % 2][:, P * q:P * q + P], probs[:, c % 3, q, 0:P], ident[:])
                    nc.tensor.transpose(bank[6 + c % 2][:, 0:P], own[:, c % 2, :],
                                        ident[:]).then_inc(S["transposed"], 1)

                def values(c):
                    pe.wait_ge(S["pT_ready"], c + 1)
                    pe.wait_ge(S["pTr_ready"], c + 1)
                    if c >= 2:
                        pe.wait_ge(S["oT_ready"], c - 1)
                    pe.wait_ge(S["exp_done"], NQ * min(c + 3, CHUNKS))
                    for own_keys in range(2):
                        for hh in range(2):
                            for e in range(2):
                                q = 2 * hh + e
                                o = s_bank(c, hh)[D * e:D * e + D, 2 * SPAN:2 * SPAN + P]
                                r = slice(CHUNK * q, CHUNK * q + CHUNK)
                                if own_keys:
                                    ins = nc.tensor.matmul(o, vrem[r, c, :], pTr[r, c % 2, :], start=False, stop=True,
                                                           tile_position=(CHUNK * q, D * e), skip_group_check=True)
                                else:
                                    nc.tensor.matmul(o, vwin[:, c, :], pT[:, c % 2, q, :], start=True, stop=True,
                                                     skip_group_check=True)
                    ins.then_inc(S["pv_done"], 1)

                for n in range(CHUNKS + 4):
                    if n >= 4:
                        values(n - 4)
                    if n < CHUNKS:
                        scores(n)
                    if 2 <= n < CHUNKS + 2:
                        turn(n - 2)
                pe.wait_ge(S["oT_ready"], CHUNKS)
                for p in range(PAIRS):
                    for w in range(2):
                        ins = nc.tensor.matmul(bank[0][D * w:D * w + D, :], sbuf["wo0"][:, p, :],
                                               oT[:, p, w * HALF:(w + 1) * HALF], start=(p == 0), stop=(p == PAIRS - 1))
                ins.then_inc(S["proj_done"], 1)
                pe.wait_ge(S["v_act"], 1)
                turn_halves(S["wo_done"])
                transpose_tiles(pe, xn, TILES, [1, 2])

            @block.vector
            def _(v):
                ch = Chain(v, S["dve_chain"])
                for n in range(CHUNKS + 2):
                    c = n
                    if c < CHUNKS:
                        v.wait_ge(S["scores_done"], c + 1)
                        for e in range(2):
                            ins = v.tensor_reduce(small[:, c % 4, 0, 2 * e:2 * e + 2],
                                                  s_bank(c, e)[:, 0:2 * SPAN].rearrange("p (a k) -> p a k", a=2),
                                                  X, ALU.max)
                        ch.step(ins)
                        v.scalar_tensor_tensor(out=small[:, c % 4, 1, :], in0=small[:, c % 4, 0, :], scalar=-1.0,
                                               in1=rq[:, c].rearrange("p a e -> p (a e)"), op0=ALU.mult, op1=ALU.mult).then_inc(S["bias_ready"], 1)
                    c = n - 1
                    if 0 <= c < CHUNKS:
                        v.wait_ge(S["exp_done"], NQ * (c + 1))
                        ch.step(v.reciprocal(small[:, c % 4, 3, :], small[:, c % 4, 2, :]))
                        if c >= 2:
                            v.wait_ge(S["transposed"], c - 1)
                        for q in range(NQ):
                            v.tensor_scalar(probs[:, c % 3, q, 0:P], probs[:, c % 3, q, 0:P], small[:, c % 4, 3, q:q + 1],
                                            None, ALU.mult)
                        v.tensor_tensor(own[:, c % 2, :].rearrange("p (q k) -> p q k", q=NQ), probs[:, c % 3, :, P:SPAN],
                                        bc(small[:, c % 4, 3, :], CHUNK), ALU.mult).then_inc(S["scaled"], 1)
                    c = n - 2
                    if c >= 0:
                        v.wait_ge(S["transposed"], c + 1)
                        if c >= 2:
                            v.wait_ge(S["pv_done"], c - 1)
                        v.tensor_copy(pT[:, c % 2, :, :].rearrange("p q r -> p (q r)"),
                                      bank[4 + c % 2][:]).then_inc(S["pT_ready"], 1)
                v.wait_ge(S["wo_done"], 1)
                by_half = h[:].rearrange("p (w j) d -> p j w d", w=2)
                ch.step(v.tensor_tensor(by_half, by_half, bank[3][:].rearrange("p (j w d) -> p j w d", w=2, d=D),
                                        ALU.add))
                layernorm(v, ch, h[:], xn, tmp, moe, st, TILES)
                split_vector(v, (1, 2), parts)

            @block.scalar
            def _(a):
                for n in range(CHUNKS + 4):
                    c = n
                    if c < CHUNKS:
                        a.wait_ge(S["bias_ready"], c + 1)
                        if c >= 3:
                            a.wait_ge(S["transposed"], c - 2)
                        for q in range(NQ):
                            nc.scalar.activation(probs[:, c % 3, q, :],
                                                 s_bank(c, q // 2)[:, SPAN * (q % 2):SPAN * (q % 2) + SPAN], ACT.Exp,
                                                 bias=small[:, c % 4, 1, q:q + 1], scale=rq[:, c, q // 2, q % 2:q % 2 + 1],
                                                 accum_out=small[:, c % 4, 2, q:q + 1]).then_inc(S["exp_done"], 1)
                    c = n - 2
                    if 0 <= c < CHUNKS:
                        a.wait_ge(S["transposed"], c + 1)
                        if c >= 2:
                            a.wait_ge(S["pv_done"], c - 1)
                        nc.scalar.activation(pTr[:, c % 2, :], bank[6 + c % 2][:, 0:P],
                                             ACT.Copy).then_inc(S["pTr_ready"], 1)
                    c = n - 4
                    if c >= 0:
                        a.wait_ge(S["pv_done"], c + 1)
                        for hh in range(2):
                            ins = nc.scalar.activation(
                                oT[:, 4 * hh:4 * hh + 4, CHUNK * c:CHUNK * (c + 1)],
                                s_bank(c, hh)[:, 2 * SPAN:2 * SPAN + P].rearrange("p (a t) -> p a t", t=CHUNK),
                                ACT.Copy)
                        ins.then_inc(S["oT_ready"], 1)
                a.wait_ge(S["proj_done"], 1)
                nc.scalar.activation(tokensT, bank[0][:], ACT.Copy).then_inc(S["v_act"], 1)
                split_scalar(a, (1, 2), parts)

        def first_argmax(v, ch, p, top, cand, best, hot, tiles):
            ch.step(v.tensor_reduce(top, p, X, ALU.max))
            ch.step(v.tensor_tensor(cand, p, bc(top, E), ALU.is_ge))
            ch.step(v.tensor_tensor(cand, cand, rows(sbuf["first_weight"][:], tiles), ALU.mult))
            ch.step(v.tensor_reduce(best, cand, X, ALU.max))
            ch.step(v.tensor_tensor(hot, cand, bc(best, E), ALU.is_equal))

        def experts(block, b):
            @block.tensor
            def _(pe):
                for i in range(TILES):
                    ins = nc.tensor.matmul(bank[7][:, E * i:E * i + E], xT[0:D, WINDOW + P * i:WINDOW + P * i + P],
                                           sbuf["router"][:], start=True, stop=True)
                ins.then_inc(S["tok_done"], 1)

                def hidden(u):
                    w, k = divmod(u, E // 2)
                    if u >= 4:
                        pe.wait_ge(S["exp_done"], u - 3 + 1)
                    split_product(bank[u % 4][:], slice(MOE_COLS + P * k, MOE_COLS + P * k + P), w_a, w_c,
                                  parts[:, :, w * HALF:(w + 1) * HALF]).then_inc(S["proj_done"], 1)

                def outputs(i):
                    if i == 0:
                        pe.wait_ge(S["h_ready"], 1)
                    if i % 4 == 0:
                        pe.wait_ge(S["exp_done"], 5 + i)
                    if i >= 2:
                        pe.wait_ge(S["prod_done"], i - 1)
                    nc.tensor.matmul(bank[6 + i % 2][:], part_rows[:], moe_b2[:], start=True, stop=True,
                                     skip_group_check=True)
                    for k in range(E // 2):
                        ins = nc.tensor.matmul(bank[6 + i % 2][:, P * k:P * k + P],
                                               hT[:, SEQ * k + P * i:SEQ * k + P * i + P], moe_w2[:, k, :], start=False,
                                               stop=True, skip_group_check=True)
                    ins.then_inc(S["pv_done"], 1)

                for u in range(2 * (E // 2)):
                    hidden(u)
                    if u >= 6:
                        outputs(u - 6)
                for i in range(2, TILES):
                    outputs(i)
                for r in range(STRIDE):
                    ins = token_products(r)
                ins.then_inc(S["wo_done"], 1)
                transpose_tiles(pe, xn, TILES, [1, 4])

            @block.scalar
            def _(a):
                a.wait_ge(S["h_ready"], 1)
                nc.scalar.activation(lg[:, 1], lg[:, 0], ACT.Exp).then_inc(S["exp_done"], 1)
                for u in range(2 * (E // 2)):
                    w, k = divmod(u, E // 2)
                    a.wait_ge(S["proj_done"], u + 1)
                    nc.scalar.activation(hT[:, SEQ * k + w * HALF:SEQ * k + (w + 1) * HALF], bank[u % 4][:], ACT.Gelu,
                                         bias=sbuf["moe_b1"][:, k:k + 1]).then_inc(S["exp_done"], 1)
                a.wait_ge(S["wo_done"], 1)
                nc.scalar.activation(tokensT, bank[5][:], ACT.Copy)
                split_scalar(a, (1, 4), parts)

            @block.vector
            def _(v):
                ch = Chain(v, S["dve_chain"])
                v.wait_ge(S["tok_done"], 1)
                logits = bank[7][:, 0:TILES * E].rearrange("p (i e) -> p i e", e=E)
                ch.step(v.tensor_reduce(st[:, 0, :], logits, X, ALU.max))
                ch.step(v.tensor_tensor(lg[:, 0], logits, bc(st[:, 0, :], E), ALU.subtract))
                v.sem_inc(S["h_ready"], 1)
                v.wait_ge(S["exp_done"], 1)
                ch.step(v.tensor_reduce(st[:, 1, :], lg[:, 1], X, ALU.add))
                ch.step(v.reciprocal(st[:, 2, :], st[:, 1, :]))
                ch.step(v.tensor_tensor(lg[:, 2], lg[:, 1], bc(st[:, 2, :], E), ALU.mult))
                first_argmax(v, ch, lg[:, 2], st[:, 3, :], lg[:, 3], st[:, 4, :], lg[:, 4], TILES)
                ch.step(v.scalar_tensor_tensor(out=lg[:, 5], in0=lg[:, 4], scalar=-2.0, in1=lg[:, 2], op0=ALU.mult,
                                               op1=ALU.add))
                first_argmax(v, ch, lg[:, 5], st[:, 5, :], lg[:, 3], st[:, 4, :], lg[:, 6], TILES)
                ch.step(v.tensor_tensor(st[:, 6, :], st[:, 3, :], st[:, 5, :], ALU.add))
                ch.step(v.tensor_scalar(st[:, 7, :], st[:, 6, :], 1e-12, None, ALU.max))
                ch.step(v.reciprocal(st[:, 6, :], st[:, 7, :]))
                ch.step(v.tensor_tensor(lg[:, 7], lg[:, 4], lg[:, 6], ALU.add))
                ch.step(v.tensor_tensor(lg[:, 7], lg[:, 7], lg[:, 2], ALU.mult))
                ch.step(v.tensor_tensor(comb[:], lg[:, 7], bc(st[:, 6, :], E), ALU.mult))
                for i in range(TILES):
                    v.wait_ge(S["pv_done"], i + 1)
                    v.tensor_tensor(yw[:, i % 2], bank[6 + i % 2][:].rearrange("p (e d) -> p e d", d=D),
                                    bc(comb[:, i, :], D), ALU.mult).then_inc(S["prod_done"], 1)
                    v.wait_ge(S["prod_done"], i + 1)
                    ins = v.tensor_reduce(moe[:, i, :], yw[:, i % 2].rearrange("p e d -> p d e"), X, ALU.add)
                ch.step(ins)
                v.wait_ge(S["set_ready"], 1)
                ch.step(v.tensor_tensor(h[:], h[:], moe, ALU.add))
                layernorm(v, ch, h[:], xn, tmp, moe, st, TILES)
                split_vector(v, (1, 4), parts)

            @block.gpsimd
            def _(g):
                g.tensor_tensor(h[:], h[:], xn[:, :, 0, :], ALU.add).then_inc(S["set_ready"], 1)
                g.wait_ge(S["xn_ready"], 2)
                g.tensor_tensor(res[:, bass.ds(b * TILES, TILES), :], h[:], xn[:, :, 0, :], ALU.add)

        qT1 = big1[:, 0, :]
        kT1 = big1[:, 1, :]
        v1 = big1[:, 2, 0:HALF].rearrange("p (i d) -> p i d", d=D)
        p1 = big2[:, 0:2, :]
        pT1 = big2[:, 2:4, :]

        def full(block, b):
            @block.tensor
            def _(pe):
                for n, first in enumerate((Q1_COLS, K1_COLS)):
                    for w in range(2):
                        ins = split_product(bank[2 * n + w][:], slice(first, first + P), w_a, w_c,
                                            parts[:, :, w * HALF:(w + 1) * HALF])
                    ins.then_inc(S["proj_done"], 1)
                for i in range(TILES):
                    ins = nc.tensor.matmul(bank[4][:, D * i:D * i + D], xT[0:D, WINDOW + P * i:WINDOW + P * i + P],
                                           wvl[:], start=True, stop=True)
                ins.then_inc(S["proj_done"], 1)

                def scores(i):
                    if i == 0:
                        pe.wait_ge(S["h_ready"], 2)
                        pe.wait_ge(S["square_done"], 2)
                    if i >= 2:
                        pe.wait_ge(S["exp_done"], i - 1)
                    for w in range(2):
                        ins = nc.tensor.matmul(bank[2 * (i % 2) + w][:], qT1[:, P * i:P * i + P],
                                               kT1[:, w * HALF:(w + 1) * HALF], start=True, stop=True)
                    ins.then_inc(S["scores_done"], 1)

                def turn(i):
                    pe.wait_ge(S["exp_done"], i + 1)
                    if i == 0:
                        pe.wait_ge(S["v_act"], 1)
                    else:
                        pe.wait_ge(S["pT_ready"], i)
                        pe.wait_ge(S["pTr_ready"], i)
                    for k in range(8):
                        ins = nc.tensor.transpose(bank[4 + k // 4][:, P * (k % 4):P * (k % 4) + P],
                                                  p1[:, i % 2, P * k:P * k + P], ident[:])
                        if k % 4 == 3:
                            ins.then_inc(S["transposed"], 1)

                def values(i):
                    pe.wait_ge(S["pT_ready"], i + 1)
                    pe.wait_ge(S["pTr_ready"], i + 1)
                    if i >= 2:
                        pe.wait_ge(S["last"], i - 1)
                    for k in range(8):
                        ins = nc.tensor.matmul(bank[6 + i % 2][:, 0:D], pT1[:, i % 2, P * k:P * k + P], v1[:, k, :],
                                               start=(k == 0), stop=(k == 7))
                    ins.then_inc(S["pv_done"], 1)

                for n in range(TILES + 2):
                    if n < TILES:
                        scores(n)
                    if 1 <= n < TILES + 1:
                        turn(n - 1)
                    if n >= 2:
                        values(n - 2)

            @block.scalar
            def _(a):
                a.wait_ge(S["proj_done"], 1)
                for w in range(2):
                    nc.scalar.activation(qT1[:, w * HALF:(w + 1) * HALF], bank[w][:], ACT.Identity,
                                         bias=bq[:, 0:1]).then_inc(S["h_ready"], 1)
                a.wait_ge(S["proj_done"], 3)
                nc.scalar.activation(v1.rearrange("p i d -> p (i d)"), bank[4][:], ACT.Copy).then_inc(S["v_act"], 1)
                for n in range(TILES + 1):
                    if n < TILES:
                        a.wait_ge(S["bias_ready"], n + 1)
                        if n >= 2:
                            a.wait_ge(S["transposed"], 2 * n - 2)
                        for w in range(2):
                            ins = nc.scalar.activation(p1[:, n % 2, w * HALF:(w + 1) * HALF], bank[2 * (n % 2) + w][:],
                                                       ACT.Exp, bias=st[:, 1, n:n + 1], scale=0.5 / D,
                                                       accum_out=st[:, 2 + w, n:n + 1])
                        ins.then_inc(S["exp_done"], 1)
                    i = n - 1
                    if i >= 0:
                        a.wait_ge(S["transposed"], 2 * i + 1)
                        if i >= 2:
                            a.wait_ge(S["pv_done"], i - 1)
                        nc.scalar.activation(pT1[:, i % 2, 0:HALF], bank[4][:], ACT.Copy).then_inc(S["pTr_ready"], 1)

            @block.vector
            def _(v):
                ch = Chain(v, S["dve_chain"])
                v.wait_ge(S["proj_done"], 2)
                for w in range(2):
                    v.tensor_scalar(kT1[:, w * HALF:(w + 1) * HALF], bank[2 + w][:], bk[:, 0:1], None,
                                    ALU.add).then_inc(S["square_done"], 1)
                for n in range(TILES + 2):
                    if n < TILES:
                        v.wait_ge(S["scores_done"], n + 1)
                        for w in range(2):
                            ins = v.tensor_reduce(st[:, 4 + w, n:n + 1], bank[2 * (n % 2) + w][:], X, ALU.max)
                        ch.step(ins)
                        ch.step(v.tensor_tensor(st[:, 6, n:n + 1], st[:, 4, n:n + 1], st[:, 5, n:n + 1], ALU.max))
                        v.tensor_scalar(st[:, 1, n:n + 1], st[:, 6, n:n + 1], -0.5 / D, None,
                                        ALU.mult).then_inc(S["bias_ready"], 1)
                    i = n - 1
                    if 0 <= i < TILES:
                        v.wait_ge(S["transposed"], 2 * i + 2)
                        if i >= 2:
                            v.wait_ge(S["pv_done"], i - 1)
                        v.tensor_copy(pT1[:, i % 2, HALF:], bank[5][:]).then_inc(S["pT_ready"], 1)
                        ch.step(v.tensor_tensor(st[:, 7, i:i + 1], st[:, 2, i:i + 1], st[:, 3, i:i + 1], ALU.add))
                        ch.step(v.reciprocal(st[:, 0, i:i + 1], st[:, 7, i:i + 1]))
                    i = n - 2
                    if i >= 0:
                        v.wait_ge(S["pv_done"], i + 1)
                        v.scalar_tensor_tensor(out=hl_row(b, i), in0=bank[6 + i % 2][:, 0:D], scalar=st[:, 0, i:i + 1],
                                               in1=vbias[:], op0=ALU.mult, op1=ALU.add).then_inc(S["last"], 1)

        def hl_row(b, i):
            return hl[:, bass.ds(b * TILES + i, 1), :].rearrange("p a d -> p (a d)")

        def batchnorm(block):
            @block.sync
            def _(sp):
                sp.dma_start(ffn_w, inp["ffn_w"]).then_inc(S["w_loaded"], 16)
                for dst, k in ((ffn_w2, "ffn_w2"), (ffn_b1, "ffn_b1")):
                    sp.dma_start(dst, inp[k]).then_inc(S["x_loaded"], 16)
                sp.dma_start(ffn_b2, inp["ffn_b2"]).then_inc(S["x_loaded"], 16)
                sp.wait_ge(S["x_loaded"], 48)

            q4 = [slice(TILES * g, TILES * g + TILES) for g in range(IMAGES)]

            @block.tensor
            def _(pe):
                for step in range(2):
                    if step:
                        pe.wait_ge(S["square_done"], 1)
                    src = (hl, big1_tok)[step]
                    for g in range(IMAGES):
                        ins = nc.tensor.matmul(bank[step][:], ones_mean[:], src[:, q4[g], :], start=(g == 0),
                                               stop=(g == IMAGES - 1))
                    ins.then_inc(S["proj_done"], 1)

            @block.scalar
            def _(a):
                a.wait_ge(S["h_ready"], 1)
                nc.scalar.activation(big1_tok[:], hl[:], ACT.Square).then_inc(S["square_done"], 1)

            @block.vector
            def _(v):
                ch = Chain(v, S["dve_chain"])
                v.wait_ge(S["proj_done"], 1)
                ch.step(v.tensor_reduce(mean_row[:], bank[0][:].rearrange("p (i d) -> p d i", d=D), X, ALU.add))
                ch.step(v.tensor_tensor(hl[:], hl[:], rows(mean_row[:], ALLT), ALU.subtract))
                v.sem_inc(S["h_ready"], 1)
                v.memset(ten_k[:, 0, :], 1e4)
                v.memset(ten_k[:, 1, :], -1e4)
                v.wait_ge(S["w_loaded"], 16)
                scratch = big2[:].rearrange("p a n -> p (a n)")
                split_weights(v, ch, ffn_w, ffn_a, ffn_c, scratch[:, 0:FFN_COLS // 2].bitcast(BF16),
                              scratch[:, FFN_COLS // 2:FFN_COLS].bitcast(BF16), scratch[:, FFN_COLS:2 * FFN_COLS])
                v.wait_ge(S["x_loaded"], 48)
                room = scratch[0:E, 3 * FFN_COLS:3 * FFN_COLS + D]
                ch.step(v.memset(b2_parts, 0.0))
                high, low, least = (b2_parts[:, k, 0:D] for k in range(3))
                ch.step(v.tensor_copy(high, ffn_b2))
                ch.step(v.tensor_tensor(room, ffn_b2, high, ALU.subtract))
                ch.step(v.tensor_copy(low, room))
                v.tensor_tensor(least, room, low, ALU.subtract)
                v.tensor_scalar(others, bc(ident[0:E, 0:E], P), -1.0, 1e30, ALU.add, ALU.mult)
                v.wait_ge(S["proj_done"], 2)
                ch.step(v.tensor_reduce(var_row[:], bank[1][:].rearrange("p (i d) -> p d i", d=D), X, ALU.add))
                ch.step(v.tensor_scalar(var_row[:], var_row[:], BN_EPS, None, ALU.add))
                one_over_root(v, ch, mean_row[:], var_row[:])
                ch.step(v.tensor_copy(var_row[:], mean_row[:]))
                ch.step(v.tensor_tensor(var_row[:], var_row[:], gammarow[:], ALU.mult))
                ch.step(v.tensor_tensor(hl[:], hl[:], rows(var_row[:], ALLT), ALU.mult))
                ch.step(v.tensor_tensor(hl[:], hl[:], rows(betarow[:], ALLT), ALU.add))
                ch.step(v.scalar_tensor_tensor(out=res[:], in0=hl[:], scalar=0.0, in1=res[:], op0=ALU.max, op1=ALU.add))

        big1_tok = big1[:].rearrange("p a b -> p (a b)")[:, 0:ALLT * D].rearrange("p (i d) -> p i d", d=D)

        big1_flat, big2_flat = (z[:].rearrange("p a b -> p (a b)") for z in (big1, big2))
        everything = ALLT * P
        parts_all = big1_flat[:, 0:3 * everything // 2].bitcast(BF16).rearrange("p (s n) -> p s n", s=3)
        squares = big2_flat[:, 0:ALLT * D].rearrange("p (i d) -> p i d", d=D)
        xn_all = big2_flat[:, ALLT * D:3 * ALLT * D].rearrange("p (i a d) -> p i a d", a=2, d=D)
        la = [big2_flat[:, 3 * ALLT * D + ALLT * E * k:3 * ALLT * D + ALLT * E * (k + 1)].rearrange(
            "p (i e) -> p i e", e=E) for k in range(8)]
        sa = [st_all[:, k, :] for k in range(8)]
        hot_rows = big1_flat[0:E, 3 * everything // 2:2 * everything].bitcast(BF16)
        rests = work[:].rearrange("p (k n) -> p k n", k=4)
        B4 = ALLT // GROUP_TILES

        def route(block):
            @block.tensor
            def _(pe):
                for j in range(B4):
                    if j >= 4:
                        pe.wait_ge(S["rest_done"], j - 3)
                    transpose_tiles(pe, xn_all[:, GROUP_TILES * j:GROUP_TILES * (j + 1)], GROUP_TILES, [j % 4], j)
                for i in range(ALLT):
                    if i % GROUP_TILES == 0:
                        pe.wait_ge(S["prod_done"], i // GROUP_TILES + 1)
                    for k, w in ((0, ffn_a), (1, ffn_a), (2, ffn_c)):
                        ins = nc.tensor.matmul(bank[7][:, E * i:E * i + E], parts_all[:, k, P * i:P * i + P],
                                               w[:, FCH * P:FFN_COLS], start=(k == 0), stop=(k == 2))
                ins.then_inc(S["tok_done"], 1)
                pe.wait_ge(S["bias_ready"], 1)
                chosen = la[4].rearrange("p i e -> p (i e)")
                nc.tensor.matmul(bank[6][:, 0:ALLT * E], lower[:], chosen, start=True, stop=True)
                nc.tensor.matmul(bank[6][:, ALLT * E:2 * ALLT * E], ones[:], chosen, start=True,
                                 stop=True).then_inc(S["ssq_done"], 1)
                for i in range(ALLT):
                    j, m = divmod(i, 4)
                    if j >= 4 and m == 0:
                        pe.wait_ge(S["v_act"], j - 3)
                    ins = nc.tensor.transpose(bank[j % 4][0:E, P * m:P * m + P], la[4][:, i, :], ident[:])
                    if m == 3:
                        ins.then_inc(S["transposed"], 1)

            @block.scalar
            def _(a):
                for n in range(B4 + 1):
                    if n < B4:
                        a.wait_ge(S["xT_psum"], n + 1)
                        nc.scalar.activation(parts_all[:, 0, n * HALF:(n + 1) * HALF], bank[n % 4][:],
                                             ACT.Copy).then_inc(S["high_done"], 1)
                    j = n - 1
                    if j >= 0:
                        a.wait_ge(S["rest_done"], j + 1)
                        nc.scalar.activation(parts_all[:, 1, j * HALF:(j + 1) * HALF], rests[:, j % 4, :],
                                             ACT.Copy).then_inc(S["low_done"], 1)
                a.wait_ge(S["h_ready"], 1)
                nc.scalar.activation(la[1], la[0], ACT.Exp).then_inc(S["exp_done"], 1)
                for j in range(B4):
                    a.wait_ge(S["transposed"], j + 1)
                    nc.scalar.activation(hot_rows[:, j * HALF:(j + 1) * HALF], bank[j % 4][0:E, :],
                                         ACT.Copy).then_inc(S["v_act"], 1)

            @block.vector
            def _(v):
                ch = Chain(v, S["dve_chain"])
                layernorm(v, ch, res[:], xn_all, hl[:], squares, st_all, ALLT)
                for n in range(B4 + 1):
                    if n < B4:
                        cols = slice(n * HALF, (n + 1) * HALF)
                        v.wait_ge(S["high_done"], n + 1)
                        v.tensor_tensor(rests[:, n % 4, :], bank[n % 4][:], parts_all[:, 0, cols],
                                        ALU.subtract).then_inc(S["rest_done"], 1)
                        v.tensor_copy(parts_all[0:D, 2, cols], parts_all[0:D, 0, cols])
                    j = n - 1
                    if j >= 0:
                        cols = slice(j * HALF, (j + 1) * HALF)
                        v.wait_ge(S["low_done"], j + 1)
                        v.tensor_tensor(parts_all[D:P, 2, cols], rests[D:P, j % 4, :], parts_all[D:P, 1, cols],
                                        ALU.subtract).then_inc(S["prod_done"], 1)
                v.wait_ge(S["tok_done"], 1)
                ch.step(v.tensor_tensor(la[2], bank[7][:, 0:ALLT * E].rearrange("p (i e) -> p i e", e=E),
                                        rows(gate_b[:], ALLT), ALU.add))
                ch.step(v.tensor_reduce(sa[0], la[2], X, ALU.max))
                ch.step(v.tensor_tensor(la[0], la[2], bc(sa[0], E), ALU.subtract))
                v.sem_inc(S["h_ready"], 1)
                v.wait_ge(S["exp_done"], 1)
                ch.step(v.tensor_reduce(sa[1], la[1], X, ALU.add))
                ch.step(v.reciprocal(sa[2], sa[1]))
                ch.step(v.tensor_tensor(la[2], la[1], bc(sa[2], E), ALU.mult))
                first_argmax(v, ch, la[2], sa[3], la[3], sa[4], la[4], ALLT)
                v.sem_inc(S["bias_ready"], 1)
                v.wait_ge(S["ssq_done"], 1)
                count, total = (bank[6][:, ALLT * E * k:ALLT * E * (k + 1)].rearrange("p (i e) -> p i e", e=E)
                                for k in range(2))
                src, dst = la[5], la[6]
                ch.step(v.tensor_copy(src, total))
                step = 1
                while step < ALLT:
                    v.tensor_copy(dst[:, 0:step, :], src[:, 0:step, :])
                    ch.step(v.tensor_tensor(dst[:, step:, :], src[:, step:, :], src[:, :ALLT - step, :], ALU.add))
                    src, dst = dst, src
                    step *= 2
                ch.step(v.tensor_tensor(dst, src, total, ALU.subtract))
                ch.step(v.tensor_tensor(src, dst, count, ALU.add))
                ch.step(v.tensor_scalar(dst, src, float(CAPACITY), None, ALU.is_le))
                ch.step(v.tensor_tensor(src, dst, la[4], ALU.mult))
                ch.step(v.tensor_reduce(sa[5], src, X, ALU.max))
                v.tensor_tensor(gates, sa[5], sa[3], ALU.mult)

        G = GROUP_TILES
        PER_BLOCK = 4
        UNITS_C = PER_BLOCK * FCH
        RING = 8
        hid = big2_flat[:, 0:RING * GT].rearrange("p (f t) -> p f t", t=GT)
        yT = turned[:].rearrange("p (a n) -> p a n", a=2)
        y_at = RING * GT
        y_gated, y_finite, *y_out = [big2_flat[:, y_at + G * D * k:y_at + G * D * (k + 1)] for k in range(2 + PER_BLOCK)]
        maski = big2_flat[:, y_at + (2 + PER_BLOCK) * G * D:y_at + (3 + PER_BLOCK) * G * D].bitcast(I32)

        def capacity_experts(block, it):
            @block.tensor
            def _(pe):
                relu_done = (S["v_act"], S["v_dve"])

                def hidden(n):
                    gg, f = divmod(n, FCH)
                    tokens_of = bass.ds(it * (PER_BLOCK * GT) + gg * GT, GT)
                    if n >= 4:
                        pe.wait_ge(relu_done[n % 2], (n - 4) // 2 + 1)
                    nc.tensor.matmul(bank[n % 4][:], others[:, f // 2, :], hot_rows[:, tokens_of], start=True, stop=False)
                    for k, w in ((0, ffn_a), (1, ffn_a), (2, ffn_c)):
                        ins = nc.tensor.matmul(bank[n % 4][:], w[:, P * f:P * f + P], parts_all[:, k, tokens_of],
                                               start=False, stop=(k == 2))
                    ins.then_inc(S["proj_done"], 1)

                def bias(gg):
                    if gg >= 2:
                        pe.wait_ge(S["pT_ready"], gg - 1)
                    for k in range(3):
                        nc.tensor.matmul(bank[4 + gg % 2][:], b2_parts[:, k, :],
                                         hot_rows[:, bass.ds(it * (PER_BLOCK * GT) + gg * GT, GT)], start=(k == 0),
                                         stop=True, skip_group_check=True)

                def outputs(n):
                    for m in (n, n + 1):
                        gg, f = divmod(m, FCH)
                        pe.wait_ge(relu_done[m % 2], m // 2 + 1)
                    for m in (n, n + 1):
                        gg, f = divmod(m, FCH)
                        half = slice(D * (m % 2), D * (m % 2) + D)
                        ins = nc.tensor.matmul(bank[4 + gg % 2][half, :], ffn_w2[:, f, :], hid[:, m % RING, :],
                                               start=False, stop=True, skip_group_check=True)
                    if f == FCH - 1:
                        ins.then_inc(S["pv_done"], 1)

                def turn(gg):
                    pe.wait_ge(S["pT_ready"], gg + 1)
                    if gg >= 2:
                        pe.wait_ge(S["prod_done"], gg - 1)
                    for i in range(G):
                        ins = nc.tensor.matmul(bank[6 + gg % 2][:, D * i:D * i + D], yT[:, gg % 2, P * i:P * i + P],
                                               both_halves[:], start=True, stop=True)
                    ins.then_inc(S["transposed"], 1)

                for n in range(UNITS_C + 2):
                    gg, f = divmod(n, FCH)
                    if n < UNITS_C:
                        hidden(n)
                        if f == 2:
                            bias(gg)
                    if n % 2 and n >= 3:
                        outputs(n - 3)
                    if gg and f == 5:
                        turn(gg - 1)
                turn(PER_BLOCK - 1)

            @block.scalar
            def _(a):
                def copy_outputs(gg):
                    a.wait_ge(S["pv_done"], gg + 1)
                    if gg >= 2:
                        a.wait_ge(S["transposed"], gg - 1)
                    nc.scalar.activation(yT[:, gg % 2, :], bank[4 + gg % 2][:], ACT.Copy).then_inc(S["pT_ready"], 1)

                for n in range(0, UNITS_C, 2):
                    gg, f = divmod(n, FCH)
                    a.wait_ge(S["proj_done"], n + 1)
                    nc.scalar.activation(hid[:, n % RING, :], bank[n % 4][:], ACT.Relu,
                                         bias=ffn_b1[:, f:f + 1]).then_inc(S["v_act"], 1)
                    if gg and f == 2:
                        copy_outputs(gg - 1)
                copy_outputs(PER_BLOCK - 1)

            @block.vector
            def _(v):
                ch = Chain(v, S["dve_chain"])

                def finish(gg):
                    v.wait_ge(S["transposed"], gg + 1)
                    at = bass.ds(it * (PER_BLOCK * G) + gg * G, G)
                    ch.step(v.tensor_tensor(y_gated.rearrange("p (i d) -> p i d", d=D),
                                            bank[6 + gg % 2][:, 0:G * D].rearrange("p (i d) -> p i d", d=D),
                                            bc(gates[:, at], D), ALU.mult))
                    v.sem_inc(S["prod_done"], 1)
                    v.memset(y_finite, 0.0)
                    ch.step(v.tensor_tensor(maski, y_gated, y_gated, ALU.is_equal))
                    ch.step(v.copy_predicated(y_finite, maski, y_gated))
                    ch.step(v.tensor_scalar(maski, y_finite, HUGE, None, ALU.is_gt))
                    ch.step(v.copy_predicated(y_finite, maski, ten_k[:, 0, :]))
                    ch.step(v.tensor_scalar(maski, y_finite, -HUGE, None, ALU.is_lt))
                    ch.step(v.copy_predicated(y_finite, maski, ten_k[:, 1, :]))
                    v.tensor_tensor(y_out[gg], y_finite, res[:, at, :].rearrange("p i d -> p (i d)"),
                                    ALU.add).then_inc(S["last"], 1)

                for n in range(1, UNITS_C, 2):
                    gg, f = divmod(n, FCH)
                    v.wait_ge(S["proj_done"], n + 1)
                    v.tensor_scalar(hid[:, n % RING, :], bank[n % 4][:], ffn_b1[:, f:f + 1], 0.0, ALU.add,
                                    ALU.max).then_inc(S["v_dve"], 1)
                    if gg and f == 7:
                        finish(gg - 1)
                finish(PER_BLOCK - 1)

            @block.sync
            def _(sp):
                for gg in range(PER_BLOCK):
                    sp.wait_ge(S["last"], gg + 1)
                    sp.dma_start(out[:, bass.ds(it * (PER_BLOCK * G) + gg * G, G), :], y_out[gg].rearrange(
                        "p (i d) -> p i d", d=D)).then_inc(S["x_loaded"], 16)
                sp.wait_ge(S["x_loaded"], 16 * PER_BLOCK)

        stage(setup)
        with nc.Fori(0, IMAGES) as b:
            stage(tokens)
            stage(project)
            stage(lambda block: windowed(block, b + 1))
            stage(lambda block: experts(block, b))
            stage(lambda block: full(block, b))
        stage(batchnorm)
        stage(route)
        with nc.Fori(0, GROUPS // PER_BLOCK) as g:
            stage(lambda block: capacity_experts(block, g))


def constants():
    f = np.float32
    c = {"ident": np.eye(P, dtype=f), "lower": np.triu(np.ones((P, P), f))}
    k, n = np.arange(FREQ)[:, None], np.arange(PATCH)[None, :]
    ang = 2 * np.pi * k * n / PATCH
    c["dft"] = (np.concatenate([np.cos(ang), -np.sin(ang)]) / np.sqrt(PATCH)).astype(f)
    freqs = (f(10000.0) ** (f(-2.0) * np.arange(D // 2, dtype=f) / f(D))).astype(f)
    theta = np.arange(SEQ, dtype=f)[None, :] * np.repeat(freqs, 2)[:, None]
    sign = np.where(np.arange(D) % 2 == 0, -1.0, 1.0)[:, None]
    c["rope_cos"] = np.tile(np.cos(theta), (2, 1)).astype(f)
    c["rope_sin"] = np.tile(np.sin(theta) * sign, (2, 1)).astype(f)
    t = np.arange(CHUNK)
    c["row_of_t"] = np.tile(np.eye(CHUNK, dtype=f), (1, NQ))
    j = np.arange(SPAN)
    m = np.zeros((CHUNK, EARLY + 1, SPAN))
    for v in range(EARLY + 1):
        ok = (j[None] >= t[:, None]) & (j[None] <= t[:, None] + WINDOW) & (j[None] >= WINDOW - CHUNK * v)
        m[:, v] = np.where(ok, 0.0, -1e30)
    c["window_mask"] = m.astype(f)
    c["by_head"] = np.repeat(np.eye(2, 32, dtype=f), D, axis=0)
    c["first_weight"] = np.tile(np.arange(E, 0, -1, dtype=f), (P, 1))
    return c


def layouts(i):
    def two(a):
        return np.concatenate([a, a], axis=0)

    a = {k: np.asarray(v) for k, v in i.items()}
    x = a["x"].transpose(0, 1, 3, 2)
    swap = np.arange(D) ^ 1
    wq = a["L0_attn_wq"].reshape(PAIRS, 2, D, D)
    wk = a["L0_attn_wkv"][:D]
    q = np.stack([wq, wq[:, :, swap]], axis=1).transpose(4, 0, 1, 2, 3).reshape(D, 2 * PAIRS * P)
    k = np.stack([wk, wk, wk[swap], wk[swap]]).transpose(2, 0, 1).reshape(D, 2 * P)
    w1 = a["L0_ffn_w1"].reshape(E // 2, 2, D, D)
    fw1 = a["L1_ffn_w1"].transpose(1, 0, 2).reshape(D, FCH * P)
    return {
        "x": np.concatenate([x, np.concatenate([x[..., STRIDE:], np.repeat(x[..., -1:], STRIDE, -1)], -1)],
                            axis=1)[[*range(IMAGES), 0]],
        "tok_w": a["L0_tok_W"].reshape(D, 2 * FREQ, CH).transpose(1, 0, 2),
        "wv0": a["L0_attn_wkv"][D:].T,
        "wo0": a["L0_attn_wo"].reshape(D, PAIRS, P).transpose(2, 1, 0),
        "q_norm": a["L0_attn_q_norm_w"].reshape(D, 1), "k_norm": a["L0_attn_k_norm_w"].reshape(D, 1),
        "router": a["L0_ffn_router_w"].T,
        "proj_w": two(np.concatenate([q, k, w1.transpose(2, 0, 1, 3).reshape(D, E * D), *[a["L1_attn_Wq"]] * 2,
                                      *[a["L1_attn_Wk"]] * 2], axis=1)),
        "moe_b1": a["L0_ffn_b1"].reshape(E // 2, P).T,
        "moe_w2": a["L0_ffn_w2"].reshape(E // 2, P, D).transpose(1, 0, 2),
        "moe_b2": a["L0_ffn_b2"].reshape(1, E * D),
        "bq1": a["L1_attn_bq"].reshape(D, 1), "bk1": a["L1_attn_bk"].reshape(D, 1),
        "bv1": a["L1_attn_bv"].reshape(D, 1),
        "wvT1": a["L1_attn_Wv"].T, "wl1": a["L1_attn_Wl"],
        "bl1": a["L1_attn_bl"].reshape(1, D), "gamma": a["L1_attn_gamma"].reshape(1, D),
        "beta": a["L1_attn_beta"].reshape(1, D), "gate_b": a["L1_ffn_gate_b"].reshape(1, E),
        "ffn_w": two(np.concatenate([fw1, a["L1_ffn_gate_w"]], axis=1)),
        "ffn_b1": a["L1_ffn_b1"].reshape(FCH, P).T,
        "ffn_w2": a["L1_ffn_w2"].reshape(FCH, P, D).transpose(1, 0, 2),
        "ffn_b2": a["L1_ffn_b2"],
    }


def kernel(**inputs):
    import concourse.bacc as _bacc
    from concourse.bass_utils import run_bass_kernel_spmd as _run

    nc = _bacc.Bacc("TRN2", target_bir_lowering=False, num_devices=1)
    arrays, args = {}, {}
    for name, a in {**constants(), **layouts(inputs)}.items():
        a = np.ascontiguousarray(a)
        arrays[f"in_{name}"] = a
        args[name] = nc.dram_tensor(f"in_{name}", a.shape, mybir.dt.from_np(a.dtype), kind="ExternalInput").ap()
    out = nc.dram_tensor("out", (IMAGES * SEQ, D), F32, kind="ExternalOutput").ap()
    program(nc, args, out.rearrange("(i p) d -> p i d", p=P))
    r = _run(nc, [arrays], core_ids=[0])
    return r.results[0]["out"].reshape(IMAGES, SEQ, D)
```
